# Optimizing a Trainium2 kernel written in Bass

```python
import numpy as np
import jax
import jax.numpy as jnp

def _softmax(x, axis=-1):
    return jax.nn.softmax(x, axis=axis)

def _gelu(x):
    return jax.nn.gelu(x, approximate=True)

def _silu(x):
    return jax.nn.silu(x)

def _sigmoid(x):
    return jax.nn.sigmoid(x)

def _layernorm(x, axis=-1, eps=1e-05):
    m = jnp.mean(x, axis=axis, keepdims=True)
    v = jnp.var(x, axis=axis, keepdims=True)
    return (x - m) / jnp.sqrt(v + eps)

def _scatter_add(tgt, idx, src, axis=0):
    return tgt.at[idx].add(src)

def _segment_sum(src, seg, n):
    return jax.ops.segment_sum(src, seg, n)
kernel_name = 'mk_early_fusion_d2_tok_img512_r4_70df95'

def setup_inputs(seed: int=0):
    np.random.seed(seed)
    _w = jnp.asarray

    def _rec_inputs():
        import jax
        import jax.numpy as jnp
        _rk = jax.random.key(seed)
        x = -7.10856e-05 + 0.999911 * jax.random.normal(jax.random.fold_in(_rk, 1), (16, 128, 64, 64), jnp.float32)
        txt = -0.0012195 + 0.0603952 * jax.random.normal(jax.random.fold_in(_rk, 2), (16, 77, 128), jnp.float32)
        return (x, txt)
    x, txt = _rec_inputs()

    def _L0_tok_setup():
        import jax, jax.numpy as jnp
        import numpy as np
        CH = 128
        K = 4
        STRIDE = 3
        VC = 100
        RES = 64
        BATCH = 32

        def _unfold(x, k, stride):
            n, c, h, w = x.shape
            oh = (h - k) // stride + 1
            ow = (w - k) // stride + 1
            i = (jnp.arange(oh) * stride)[:, None] + jnp.arange(k)[None, :]
            j = (jnp.arange(ow) * stride)[:, None] + jnp.arange(k)[None, :]
            p = x[:, :, i[:, None, :, None], j[None, :, None, :]]
            return p.transpose(0, 2, 3, 1, 4, 5).reshape(n, oh * ow, c, k, k)
        key = jax.random.key(seed)
        ks = jax.random.split(key, 4)
        c, k, v = (CH, K, VC)
        return {'x': jax.random.normal(ks[0], (BATCH, c, RES, RES), jnp.float32), 'vc_dict': jax.random.normal(ks[1], (v, c), jnp.float32) * 0.05, 'W1': jax.random.normal(ks[2], (c + k * k, 3 * c), jnp.float32) * 0.02, 'b1': jnp.zeros((3 * c,), jnp.float32), 'W2': jax.random.normal(ks[3], (3 * c, c), jnp.float32) * 0.02, 'b2': jnp.zeros((c,), jnp.float32)}
    _L0_tok_all = _L0_tok_setup()
    _L0_tok_in = {k: v for k, v in _L0_tok_all.items() if k in ('vc_dict', 'W1', 'b1', 'W2', 'b2')}
    del _L0_tok_all

    def _L0_attn_setup():
        import jax, jax.numpy as jnp
        import numpy as np
        HEADS = 8
        DIM_HEAD = 64
        SCALE = DIM_HEAD ** (-0.5)

        def entmax15(z, axis=-1):
            z = z / 2.0
            z = z - jnp.max(z, axis=axis, keepdims=True)
            zs = -jnp.sort(-z, axis=axis)
            n = z.shape[axis]
            k = jnp.arange(1, n + 1, dtype=z.dtype)
            mean = jnp.cumsum(zs, axis=axis) / k
            mean_sq = jnp.cumsum(zs * zs, axis=axis) / k
            ss = k * (mean_sq - mean * mean)
            delta = (1.0 - ss) / k
            tau = mean - jnp.sqrt(jnp.maximum(delta, 0.0))
            support = (tau <= zs).astype(jnp.int32)
            k_star = jnp.sum(support, axis=axis, keepdims=True)
            tau_star = jnp.take_along_axis(tau, k_star - 1, axis=axis)
            return jnp.square(jnp.maximum(z - tau_star, 0.0))
        key = jax.random.key(seed)
        k1, k2, k3 = jax.random.split(key, 3)
        b, n, dim = (4, 256, 128)
        inner = HEADS * DIM_HEAD
        x = jax.random.normal(k1, (b, n, dim), dtype=jnp.float32)
        w_qkv = jax.random.normal(k2, (dim, inner * 3), dtype=jnp.float32) * 0.02
        w_out = jax.random.normal(k3, (inner, dim), dtype=jnp.float32) * 0.02
        return {'x': x, 'w_qkv': w_qkv, 'w_out': w_out}
    _L0_attn_all = _L0_attn_setup()
    _L0_attn_in = {k: v for k, v in _L0_attn_all.items() if k in ('w_qkv', 'w_out')}
    del _L0_attn_all

    def _L0_ffn_setup():
        import jax, jax.numpy as jnp
        import numpy as np
        B, T, D, F, E, K = (8, 256, 128, 512, 8, 2)

        def _moe_forward(x, Wr, br, W1, b1, W2, b2):
            Bx, Tx, Dx = x.shape
            xf = x.reshape(-1, Dx)
            logits = xf @ Wr + br
            probs = jax.nn.softmax(logits, axis=-1)
            vals, idx = jax.lax.top_k(probs, K)
            cw = (jax.nn.one_hot(idx, E, dtype=x.dtype) * vals[..., None]).sum(axis=1)

            def body(acc, params):
                W1e, b1e, W2e, b2e, cwe = params
                h = jax.nn.relu(xf @ W1e + b1e)
                y = h @ W2e + b2e
                return (acc + cwe[:, None] * y, None)
            out, _ = jax.lax.scan(body, jnp.zeros_like(xf), (W1, b1, W2, b2, cw.T))
            return out.reshape(Bx, Tx, Dx)
        key = jax.random.key(seed)
        k0, k1, k2, k3 = jax.random.split(key, 4)
        s_d = 1.0 / np.sqrt(D)
        s_f = 1.0 / np.sqrt(F)
        return {'x': jax.random.normal(k0, (B, T, D), jnp.float32), 'Wr': jax.random.uniform(k1, (D, E), jnp.float32, -s_d, s_d), 'br': jnp.zeros((E,), jnp.float32), 'W1': jax.random.uniform(k2, (E, D, F), jnp.float32, -s_d, s_d), 'b1': jnp.zeros((E, F), jnp.float32), 'W2': jax.random.uniform(k3, (E, F, D), jnp.float32, -s_f, s_f), 'b2': jnp.zeros((E, D), jnp.float32)}
    _L0_ffn_all = _L0_ffn_setup()
    _L0_ffn_in = {k: v for k, v in _L0_ffn_all.items() if k in ('Wr', 'br', 'W1', 'b1', 'W2', 'b2')}
    del _L0_ffn_all

    def _L1_attn_setup():
        import jax, jax.numpy as jnp
        import numpy as np
        EPS = 1e-07
        key = jax.random.key(seed)
        ks = jax.random.split(key, 4)
        B, L, D, U = (4, 256, 128, 64)
        scale_w = (2.0 / (D + U)) ** 0.5
        x = jax.random.normal(ks[0], (B, L, D), dtype=jnp.float32)
        Wx = jax.random.normal(ks[1], (D, U), dtype=jnp.float32) * scale_w
        Wt = jax.random.normal(ks[2], (D, U), dtype=jnp.float32) * scale_w
        bt = jnp.zeros((U,), dtype=jnp.float32)
        Wa = jax.random.normal(ks[3], (U, 1), dtype=jnp.float32) * (2.0 / (U + 1)) ** 0.5
        ba = jnp.zeros((1,), dtype=jnp.float32)
        return {'x': x, 'Wx': Wx, 'Wt': Wt, 'bt': bt, 'Wa': Wa, 'ba': ba}
    _L1_attn_all = _L1_attn_setup()
    _L1_attn_in = {k: v for k, v in _L1_attn_all.items() if k in ('Wx', 'Wt', 'bt', 'Wa', 'ba')}
    del _L1_attn_all

    def _L1_ffn_setup():
        import jax, jax.numpy as jnp
        import numpy as np
        B, S, D = (8, 512, 128)
        FF = 512
        E = 8
        key = jax.random.key(seed)
        ks = jax.random.split(key, 7)
        s = 1.0 / np.sqrt(D)
        sf = 1.0 / np.sqrt(FF)
        return {'x': jax.random.normal(ks[0], (B, S, D), dtype=jnp.float32), 'Wg': jax.random.uniform(ks[1], (D, E), jnp.float32, -s, s), 'bg': jax.random.uniform(ks[2], (E,), jnp.float32, -s, s), 'W1': jax.random.uniform(ks[3], (E, D, FF), jnp.float32, -s, s), 'b1': jax.random.uniform(ks[4], (E, FF), jnp.float32, -s, s), 'W2': jax.random.uniform(ks[5], (E, FF, D), jnp.float32, -sf, sf), 'b2': jax.random.uniform(ks[6], (E, D), jnp.float32, -sf, sf)}
    _L1_ffn_all = _L1_ffn_setup()
    _L1_ffn_in = {k: v for k, v in _L1_ffn_all.items() if k in ('Wg', 'bg', 'W1', 'b1', 'W2', 'b2')}
    del _L1_ffn_all
    return {'x': x, 'txt': txt, 'L0_tok_vc_dict': _L0_tok_in['vc_dict'], 'L0_tok_W1': _L0_tok_in['W1'], 'L0_tok_b1': _L0_tok_in['b1'], 'L0_tok_W2': _L0_tok_in['W2'], 'L0_tok_b2': _L0_tok_in['b2'], 'L0_attn_w_qkv': _L0_attn_in['w_qkv'], 'L0_attn_w_out': _L0_attn_in['w_out'], 'L0_ffn_Wr': _L0_ffn_in['Wr'], 'L0_ffn_br': _L0_ffn_in['br'], 'L0_ffn_W1': _L0_ffn_in['W1'], 'L0_ffn_b1': _L0_ffn_in['b1'], 'L0_ffn_W2': _L0_ffn_in['W2'], 'L0_ffn_b2': _L0_ffn_in['b2'], 'L1_attn_Wx': _L1_attn_in['Wx'], 'L1_attn_Wt': _L1_attn_in['Wt'], 'L1_attn_bt': _L1_attn_in['bt'], 'L1_attn_Wa': _L1_attn_in['Wa'], 'L1_attn_ba': _L1_attn_in['ba'], 'L1_ffn_Wg': _L1_ffn_in['Wg'], 'L1_ffn_bg': _L1_ffn_in['bg'], 'L1_ffn_W1': _L1_ffn_in['W1'], 'L1_ffn_b1': _L1_ffn_in['b1'], 'L1_ffn_W2': _L1_ffn_in['W2'], 'L1_ffn_b2': _L1_ffn_in['b2']}

def reference(x, txt, L0_tok_vc_dict, L0_tok_W1, L0_tok_b1, L0_tok_W2, L0_tok_b2, L0_attn_w_qkv, L0_attn_w_out, L0_ffn_Wr, L0_ffn_br, L0_ffn_W1, L0_ffn_b1, L0_ffn_W2, L0_ffn_b2, L1_attn_Wx, L1_attn_Wt, L1_attn_bt, L1_attn_Wa, L1_attn_ba, L1_ffn_Wg, L1_ffn_bg, L1_ffn_W1, L1_ffn_b1, L1_ffn_W2, L1_ffn_b2):
    import jax
    import jax.numpy as jnp

    def _L0_tok_ref(x, vc_dict, W1, b1, W2, b2):
        import jax, jax.numpy as jnp
        import numpy as np
        CH = 128
        K = 4
        STRIDE = 3
        VC = 100
        RES = 64
        BATCH = 32

        def _unfold(x, k, stride):
            n, c, h, w = x.shape
            oh = (h - k) // stride + 1
            ow = (w - k) // stride + 1
            i = (jnp.arange(oh) * stride)[:, None] + jnp.arange(k)[None, :]
            j = (jnp.arange(ow) * stride)[:, None] + jnp.arange(k)[None, :]
            p = x[:, :, i[:, None, :, None], j[None, :, None, :]]
            return p.transpose(0, 2, 3, 1, 4, 5).reshape(n, oh * ow, c, k, k)
        k = K
        n, c, h, w = x.shape
        patches = _unfold(x, k, STRIDE)
        L = patches.shape[1]
        xp = patches.reshape(n * L, c, k * k)
        sim = jnp.einsum('vc,ncp->nvp', vc_dict, xp)
        score = sim.sum(axis=2)
        idx = jnp.argmax(score, axis=1)
        vc = jnp.take(vc_dict, idx, axis=0)
        sim_max = jnp.take_along_axis(sim, idx[:, None, None], axis=1)[:, 0, :]
        feat = jnp.concatenate([vc, sim_max], axis=1)
        h1 = jax.nn.leaky_relu(feat @ W1 + b1, negative_slope=0.2)
        out = jnp.tanh(h1 @ W2 + b2)
        return out.reshape(n, L, c)

    def _L0_attn_ref(x, w_qkv, w_out):
        import jax, jax.numpy as jnp
        import numpy as np
        HEADS = 8
        DIM_HEAD = 64
        SCALE = DIM_HEAD ** (-0.5)

        def entmax15(z, axis=-1):
            z = z / 2.0
            z = z - jnp.max(z, axis=axis, keepdims=True)
            zs = -jnp.sort(-z, axis=axis)
            n = z.shape[axis]
            k = jnp.arange(1, n + 1, dtype=z.dtype)
            mean = jnp.cumsum(zs, axis=axis) / k
            mean_sq = jnp.cumsum(zs * zs, axis=axis) / k
            ss = k * (mean_sq - mean * mean)
            delta = (1.0 - ss) / k
            tau = mean - jnp.sqrt(jnp.maximum(delta, 0.0))
            support = (tau <= zs).astype(jnp.int32)
            k_star = jnp.sum(support, axis=axis, keepdims=True)
            tau_star = jnp.take_along_axis(tau, k_star - 1, axis=axis)
            return jnp.square(jnp.maximum(z - tau_star, 0.0))
        b, n, dim = x.shape
        h, d = (HEADS, DIM_HEAD)
        qkv = x @ w_qkv
        q, k, v = jnp.split(qkv, 3, axis=-1)

        def to_heads(t):
            return t.reshape(b, n, h, d).transpose(0, 2, 1, 3)
        q, k, v = (to_heads(q) * SCALE, to_heads(k), to_heads(v))
        sim = jnp.einsum('bhid,bhjd->bhij', q, k)
        attn = entmax15(sim, axis=-1)
        out = jnp.einsum('bhij,bhjd->bhid', attn, v)
        out = out.transpose(0, 2, 1, 3).reshape(b, n, h * d)
        return out @ w_out

    def _L0_ffn_ref(x, Wr, br, W1, b1, W2, b2):
        import jax, jax.numpy as jnp
        import numpy as np
        B, T, D, F, E, K = (8, 256, 128, 512, 8, 2)

        def _moe_forward(x, Wr, br, W1, b1, W2, b2):
            Bx, Tx, Dx = x.shape
            xf = x.reshape(-1, Dx)
            logits = xf @ Wr + br
            probs = jax.nn.softmax(logits, axis=-1)
            vals, idx = jax.lax.top_k(probs, K)
            cw = (jax.nn.one_hot(idx, E, dtype=x.dtype) * vals[..., None]).sum(axis=1)

            def body(acc, params):
                W1e, b1e, W2e, b2e, cwe = params
                h = jax.nn.relu(xf @ W1e + b1e)
                y = h @ W2e + b2e
                return (acc + cwe[:, None] * y, None)
            out, _ = jax.lax.scan(body, jnp.zeros_like(xf), (W1, b1, W2, b2, cw.T))
            return out.reshape(Bx, Tx, Dx)
        return _moe_forward(x, Wr, br, W1, b1, W2, b2)

    def _L1_attn_ref(x, Wx, Wt, bt, Wa, ba):
        import jax, jax.numpy as jnp
        import numpy as np
        EPS = 1e-07
        k = x @ Wx
        q = x @ Wt
        h = jnp.tanh(q[:, :, None, :] + k[:, None, :, :] + bt)
        e = jnp.exp(jnp.einsum('bijq,qo->bij', h, Wa) + ba[0])
        s = jnp.sum(e, axis=-1, keepdims=True)
        a = e / (s + EPS)
        v = jnp.einsum('bij,bjd->bid', a, x)
        return v

    def _L1_ffn_ref(x, Wg, bg, W1, b1, W2, b2):
        import jax, jax.numpy as jnp
        import numpy as np
        B, S, D = (8, 512, 128)
        FF = 512
        E = 8
        b, s, d = x.shape
        xf = x.reshape(-1, d)
        logits = xf @ Wg + bg
        probs = jax.nn.softmax(logits, axis=-1)
        pmax = jnp.max(probs, axis=-1)
        routes = jnp.argmax(probs, axis=-1)
        xs = xf * pmax[:, None]
        out_tok = jnp.zeros_like(xf)
        for e in range(E):
            h = jax.nn.relu(xs @ W1[e] + b1[e])
            y = h @ W2[e] + b2[e]
            out_tok = jnp.where((routes == e)[:, None], y, out_tok)
        order = jnp.argsort(routes)
        return out_tok[order].reshape(b, s, d)
    h = _L0_tok_ref(x, L0_tok_vc_dict, L0_tok_W1, L0_tok_b1, L0_tok_W2, L0_tok_b2)
    h = jnp.concatenate([h, txt], axis=1)
    h = h + _L0_attn_ref(_layernorm(h, axis=-1), L0_attn_w_qkv, L0_attn_w_out)
    h = h + _L0_ffn_ref(_layernorm(h, axis=-1), L0_ffn_Wr, L0_ffn_br, L0_ffn_W1, L0_ffn_b1, L0_ffn_W2, L0_ffn_b2)
    h = h + _L1_attn_ref(_layernorm(h, axis=-1), L1_attn_Wx, L1_attn_Wt, L1_attn_bt, L1_attn_Wa, L1_attn_ba)
    h = h + _L1_ffn_ref(_layernorm(h, axis=-1), L1_ffn_Wg, L1_ffn_bg, L1_ffn_W1, L1_ffn_b1, L1_ffn_W2, L1_ffn_b2)
    return h

_drawn_inputs = setup_inputs


def setup_inputs(seed=0):
    import zlib

    import numpy as np

    out = dict(_drawn_inputs(seed))
    spreads = {'L0_tok_b1': (0.0, 0.1),
     'L0_tok_b2': (0.0, 0.1),
     'L0_ffn_br': (0.0, 0.1),
     'L0_ffn_b1': (0.0, 0.1),
     'L0_ffn_b2': (0.0, 0.1),
     'L1_attn_bt': (0.0, 0.778)}
    factors = {'x': 3.208, 'L0_tok_vc_dict': 3.046, 'L1_ffn_bg': 3.807, 'L1_ffn_b1': 3.165}
    for name, (base, spread) in spreads.items():
        noise = np.random.default_rng([zlib.crc32(name.encode()), seed]).standard_normal(out[name].shape)
        drawn = base * np.exp(spread * noise) if base else spread * noise
        out[name] = jnp.asarray(drawn.astype(out[name].dtype))
    for name, factor in factors.items():
        out[name] = (out[name] * factor).astype(out[name].dtype)
    return out
```

```python
from contextlib import ExitStack
from math import sqrt

import numpy as np

import concourse.bass as bass
from concourse import mybir

F32 = mybir.dt.float32
U32 = mybir.dt.uint32
ALU = mybir.AluOpType
ACT = mybir.ActivationFunctionType
AX_X = mybir.AxisListType.X

D = 128
RES, K, STRIDE = 64, 4, 3
SIDE = (RES - K) // STRIDE + 1
IMG = SIDE * SIDE
TXT = 77
N = IMG + TXT
HALF = N // 2
NT, TW = 5, 104
T = NT * TW
TH = T // 2
IMG_LAST = IMG - 4 * TW
LAST = N - 4 * TW
VC = 100
SW = 111
HEADS, DH = 8, 64
PAIRS = HEADS // 2
STEPS = 8
E, FC = 8, 4
HC = 3
U = 64
GROUPS, M = 5, 13
QUADS = GROUPS * M
RING = 3
TH_RING = 3
EPS = 1e-5


def psum_plan():
    keys = ["score", "ohT", "vsel", "simmax"] + [("h1", c) for c in range(HC)] + ["tok"]
    keys += [("xnT", 0)]
    for p in range(PAIRS):
        keys += [("q", p), ("k", p)]
    keys += [("s", h, t) for h in range(HEADS) for t in range(NT)]
    keys += ["ntT"] + [("v", t) for t in range(NT)]
    keys += [("st", 2 * p + hh, jt) for p in range(PAIRS) for jt in range(NT) for hh in range(2)]
    keys += ["o", ("xnT", 1)]

    def experts(f):
        out = [("hid", f, 0, c) for c in range(FC)]
        for e in range(E):
            if e + 1 < E:
                out += [("hid", f, e + 1, c) for c in range(FC)]
            out += [("y", f, e)]
        return out

    keys += [("lg", 0), ("cwT", 0), ("b2", 0)] + experts(0)
    keys += [("xnT", 2), "k2", "q2"] + [("et", g) for g in range(GROUPS)] + ["v1", ("xnT", 3)]
    keys += [("lg", 1), ("cwT", 1), ("b2", 1), "xsT"] + experts(1)
    slot = {k: i % RING for i, k in enumerate(keys)}
    nth = {k: i // RING for i, k in enumerate(keys)}
    assert len(slot) == len(keys)
    return slot, nth


def fusion_kernel(nc, x, txt, vc, tW1, tb1, tW2, tb2, w_qkv, w_out, Wr, br, W1, b1, W2, b2,
                  Wx, Wt, bt, Wa, ba, Wg, bg, V1, c1, V2, c2, out, y_dram, B=16):
    ctx = ExitStack()
    slot, nth = psum_plan()

    def sb(name, shape, dt=F32):
        return ctx.enter_context(nc.sbuf_tensor(name, shape, dt))

    def sem(name):
        return ctx.enter_context(nc.semaphore(name))

    with ctx:
        vc_v = sb("vc_v", [VC, D])
        vcT = sb("vcT", [D, VC])
        w1a = sb("w1a", [D, HC * 128])
        w1b = sb("w1b", [128, HC * 128])
        tb1_s = sb("tb1_s", [128, HC])
        tw2_s = sb("tw2_s", [128, HC, D])
        tb2_s = sb("tb2_s", [1, D])
        wqkv = sb("wqkv", [D, 3 * HEADS * DH])
        wout = sb("wout", [128, PAIRS, D])
        wr = [sb(f"wr{f}", [D, E]) for f in range(2)]
        br_s = [sb(f"br{f}", [1, E]) for f in range(2)]
        w1 = [sb(f"w1_{f}", [D, E, FC * 128]) for f in range(2)]
        b1_s = [sb(f"b1_{f}", [128, E, FC]) for f in range(2)]
        w2 = [sb(f"w2_{f}", [128, E, FC, D]) for f in range(2)]
        b2_s = [sb(f"b2_{f}", [E, D]) for f in range(2)]
        wxx = sb("wxx", [D, 2 * U])
        wt = sb("wt", [D, U])
        bt2 = sb("bt2", [128, 1])
        wa2 = sb("wa2", [128, 1])
        ba_s = sb("ba_s", [128, 1])
        ident = sb("ident", [128, 128])
        ones = sb("ones", [128, 128])
        before = sb("before", [TW, TW])
        valid = sb("valid", [TW, NT])
        sel = sb("sel", [128, K, 32])
        wasel = sb("wasel", [128, M, 32])
        iota_v = sb("iota_v", [SW, VC])
        iota_e = sb("iota_e", [TW, E])
        neg_half = sb("neg_half", [TW, NT])
        xb = sb("xb", [D, RES * RES])
        h = sb("h", [TW, NT, D])
        xn = sb("xn", [TW, NT, D + 1])
        xnT = sb("xnT", [D, T])
        stats = sb("stats", [TW, NT, 6])
        mv = sb("mv", [TW, NT, 2])
        vare = sb("vare", [TW, NT])
        rstd = sb("rstd", [TW, NT])
        ntau = sb("ntau", [TW, HEADS, NT])
        ntT = sb("ntT", [HEADS * NT, TW])
        sumz = sb("sumz", [TW, HEADS, NT])
        zmax = sb("zmax", [TW, HEADS, NT])
        s1 = sb("s1", [TW, 2, NT])
        s2 = sb("s2", [TW, 2, NT])
        sa = sb("sa", [TW, NT])
        sc = sb("sc", [TW, NT])
        lg = sb("lg", [TW, NT, E])
        mx8 = sb("mx8", [TW, NT, 8])
        idx8 = sb("idx8", [TW, NT, 8], U32)
        idxf = sb("idxf", [TW, NT, 2])
        pr = sb("pr", [TW, NT, E])
        den = sb("den", [TW, NT])
        oh2 = sb("oh2", [TW, NT, E])
        cw = sb("cw", [TW, NT, E])
        cwT = sb("cwT", [E, T])
        ybuf = sb("ybuf", [TW, NT, D])
        K2 = sb("K2", [128, T])
        Q2 = sb("Q2", [128, TH])
        ex = sb("ex", [128, 2, T])
        OH = sb("OH", [TW, B * NT, E])
        pos = sb("pos", [TW, B * NT])
        pos_u = sb("pos_u", [TW, B * NT], U32)
        tidx8 = sb("tidx8", [SW, 4, 8], U32)
        tidxf = sb("tidxf", [SW, 4])
        tmx8 = sb("tmx8", [SW, 4, 8])
        QK = 7770
        arena = sb("arena", [128, QK + 2 * HEADS * T])

        def cut(at, parts, *dims):
            n = int(np.prod(dims))
            assert at + n <= QK + 2 * HEADS * T
            ap = arena[0:parts, at:at + n]
            if len(dims) == 2:
                return ap.rearrange("p (a c) -> p a c", a=dims[0])
            if len(dims) == 3:
                return ap.rearrange("p (a c d) -> p a c d", a=dims[0], c=dims[1])
            return ap

        rs_a, rs_b = cut(QK, 128, RES, SIDE), cut(QK + 1344, 128, RES, SIDE)
        box = cut(QK + 2688, 128, 4 * SW)
        prod = cut(0, 128, 2, K * IMG)
        vT, simT = cut(3528, 128, IMG), cut(3969, 128, IMG)
        ohT, oh = cut(4410, VC, 4 * SW), cut(4854, SW, 4, VC)
        h1T = cut(5254, 128, HC, IMG)
        qa = cut(QK, DH + 1, HEADS, T)
        ka = cut(QK + HEADS * T, DH + 1, HEADS, T)
        Z, R = cut(0, TW, 2 * NT, N), cut(5180, TW, NT, N)
        oT, v = cut(0, 128, PAIRS, T), cut(2100, TW, NT, HEADS * DH)
        hid = cut(0, 128, 2, FC * T)
        th, ET = cut(QK, 128, TH_RING, 4 * N), cut(0, TW, NT, T)
        yall, inc = cut(0, TW, B, NT * D), cut(B * NT * D, TW, 2, B * NT * E)

        ps = [ctx.enter_context(nc.psum_tensor(f"ps{i}", [128, 2, 512], F32)) for i in range(RING)]
        acc = ctx.enter_context(nc.psum_tensor("acc", [128, 2, 512], F32))
        full = [sem(f"psum_full{s}") for s in range(RING)]
        read = [sem(f"psum_read{s}") for s in range(RING)]
        x_in, txt_in, thr_in, out_written = sem("x_in"), sem("txt_in"), sem("thr_in"), sem("out_written")
        pad_zero, boxed, box_step, ones_row = sem("pad_zero"), sem("boxed"), sem("box_step"), sem("ones_row")
        oh_ready, h1_ready = sem("oh_ready"), sem("h1_ready")
        prod_ready, prod_used = sem("prod_ready"), sem("prod_used")
        var_ready, rstd_ready, xn_ready = sem("var_ready"), sem("rstd_ready"), sem("xn_ready")
        ntau_ready, relu_ready, square_ready = sem("ntau_ready"), sem("relu_ready"), sem("square_ready")
        pt_ready, pt_used, acc_read = sem("pt_ready"), sem("pt_used"), sem("acc_read")
        lg_ready, exp_ready, cw_ready = sem("lg_ready"), sem("exp_ready"), sem("cw_ready")
        th_ready, th_used = sem("th_ready"), sem("th_used")
        h_ready, y_ready = sem("h_ready"), sem("y_ready")
        dve_link = sem("dve_link")
        batch_sems = range(full[0].num, dve_link.num + 1)
        loaded, setup_done, zeroed, x0_in = sem("loaded"), sem("setup_done"), sem("zeroed"), sem("x0_in")
        vcT_full, tables_ready = sem("vcT_full"), sem("tables_ready")
        place_full, place_step, pos_ready = sem("place_full"), sem("place_step"), sem("pos_ready")
        y_in, scattered = sem("y_in"), sem("scattered")

        def P(key):
            return ps[slot[key]]

        def FULL(key):
            return full[slot[key]]

        def READ(key):
            return read[slot[key]]

        def wait_full(eng, key):
            eng.wait_ge(full[slot[key]], nth[key] + 1)

        def wait_free(eng, key):
            if nth[key] > 0:
                eng.wait_ge(read[slot[key]], nth[key])

        def wait_read(eng, key):
            eng.wait_ge(read[slot[key]], nth[key] + 1)

        N_LOADS, SETUP = [0], [0]
        with nc.Block() as setup:
            @setup.sync
            def _(sp):
                loads = [
                    (vc_v[:], vc), (w1a[:], tW1[0:D, :]),
                    (tb1_s[:], tb1.rearrange("(c p) -> p c", p=128)),
                    (tw2_s[:], tW2.rearrange("(c p) d -> p c d", p=128)),
                    (tb2_s[:], tb2.rearrange("(o d) -> o d", o=1)),
                    (wqkv[:], w_qkv), (wout[:], w_out.rearrange("(c p) d -> p c d", p=128)),
                    (wxx[:, 0:U], Wx), (wxx[:, U:2 * U], Wx), (wt[:], Wt),
                    (bt2[0:U, :], bt.rearrange("(u o) -> u o", o=1)), (bt2[U:2 * U, :], bt.rearrange("(u o) -> u o", o=1)),
                    (wa2[0:U, :], Wa), (wa2[U:2 * U, :], Wa),
                    (ba_s[:], ba.rearrange("(o p) -> o p", o=1).broadcast_to([128, 1])),
                ]
                for f, (g_w, g_b, e_w1, e_b1, e_w2, e_b2) in enumerate(((Wr, br, W1, b1, W2, b2), (Wg, bg, V1, c1, V2, c2))):
                    loads += [
                        (wr[f][:], g_w), (br_s[f][:], g_b.rearrange("(o e) -> o e", o=1)),
                        (w1[f][:], e_w1.rearrange("e d f -> d e f")),
                        (b1_s[f][:].rearrange("p e c -> p (e c)"), e_b1.rearrange("e (c p) -> p (e c)", p=128)),
                        (b2_s[f][:], e_b2),
                    ]
                    loads += [(w2[f][:, e], e_w2[e].rearrange("(c p) d -> p c d", p=128)) for e in range(E)]
                sp.dma_start(xb[:], x[0].rearrange("c i j -> c (i j)")).then_inc(x0_in, 16)
                for dst, src in loads:
                    sp.dma_start(dst, src, allow_slow_non_contiguous=True).then_inc(loaded, 16)
                sp.wait_ge(zeroed, 1)
                for dj in range(K):
                    sp.dma_start(w1b[32 * dj:32 * dj + K, :], tW1[D + dj:D + K * K:K, :]).then_inc(loaded, 16)
                N_LOADS[0] = 16 * (len(loads) + K)
                sp.wait_ge(loaded, N_LOADS[0])
                sp.wait_ge(x0_in, 16)

            @setup.gpsimd
            def _(pool):
                g = nc.gpsimd
                n = [0]

                def done(ins):
                    ins.then_inc(setup_done, 1)
                    n[0] += 1
                    return n[0]

                g.memset(w1b[:], 0.0).then_inc(zeroed, 1)
                done(g.memset(ident[:], 0.0))
                done(g.memset(sel[:], 0.0))
                done(g.memset(before[:], 1.0))
                done(g.memset(valid[:], 1.0))
                done(g.memset(ones[:], 1.0))
                done(g.memset(neg_half[:], -0.5))
                done(g.memset(xn[:, :, D:D + 1], 1.0))
                done(g.memset(ex[:], 0.0))
                done(g.memset(wasel[:], 0.0))
                done(g.iota(iota_v[:], [[1, VC]], base=0, channel_multiplier=0, allow_small_or_imprecise_dtypes=True))
                k = done(g.iota(iota_e[:], [[1, E]], base=0, channel_multiplier=0, allow_small_or_imprecise_dtypes=True))
                pool.wait_ge(setup_done, k)
                done(g.affine_select(out=ident[:], in_=ident[:], compare_op=ALU.not_equal, fill=1.0, base=0,
                                     pattern=[[-1, 128]], channel_multiplier=1))
                done(g.affine_select(out=sel[:], in_=sel[:], compare_op=ALU.not_equal, fill=1.0, base=0,
                                     pattern=[[1, K], [-1, 32]], channel_multiplier=0))
                done(g.affine_select(out=before[:], in_=before[:], compare_op=ALU.is_gt, fill=0.0, base=0,
                                     pattern=[[1, TW]], channel_multiplier=-1))
                done(g.affine_select(out=valid[:], in_=valid[:], compare_op=ALU.is_gt, fill=0.0, base=N,
                                     pattern=[[-TW, NT]], channel_multiplier=-1))
                SETUP[0] = n[0]
                pool.wait_ge(setup_done, SETUP[0])

            @setup.tensor
            def _(pe):
                mm, tr = nc.tensor.matmul, nc.tensor.transpose
                pe.wait_ge(loaded, N_LOADS[0])
                pe.wait_ge(setup_done, SETUP[0])
                tr(ps[0][0:D, 0, 0:VC], vc_v[:], ident[0:VC, 0:VC]).then_inc(vcT_full, 1)
                pe.wait_ge(tables_ready, 3)

            @setup.scalar
            def _(act):
                act.wait_ge(loaded, N_LOADS[0])
                act.wait_ge(setup_done, SETUP[0])

            @setup.vector
            def _(dve):
                V = nc.vector
                dve.wait_ge(loaded, N_LOADS[0])
                dve.wait_ge(setup_done, SETUP[0])
                dve.wait_ge(vcT_full, 1)
                V.tensor_copy(vcT[:], ps[0][0:D, 0, 0:VC]).then_inc(tables_ready, 1)
                for s in range(2):
                    flat = wasel[U * s:U * s + U].rearrange("p m j -> p (m j)")
                    V.tensor_copy(flat[:, M * s:M * s + 33 * (M - 1) + 1:33],
                                  wa2[U * s:U * s + U, :].broadcast_to([U, M])).then_inc(tables_ready, 1)

        with nc.Fori(0, B) as b:
            with nc.Block() as block:
                @block.sync
                def _(sp):
                    sp.wait_ge(pad_zero, 1)
                    sp.dma_start(h[IMG_LAST:LAST, NT - 1, :],
                                 txt[bass.ds(b, 1)].rearrange("o t d -> (o t) d")).then_inc(txt_in, 16)
                    sp.wait_ge(boxed, 1)
                    sp.wait_ge(prod_ready, K)
                    sp.dma_start(xb[:], x[bass.ds((b + 1) % B, 1)].rearrange("o c i j -> (o c) (i j)")).then_inc(x_in, 16)
                    wait_read(sp, "ntT")
                    sp.dma_start(qa[DH:DH + 1, :, :].rearrange("o h (t i) -> o (h t) i", t=NT),
                                 ntT[:]).then_inc(thr_in, 16)
                    sp.wait_ge(h_ready, 1)
                    ob = out[bass.ds(b, 1)].rearrange("o t d -> (o t) d")
                    sp.dma_start(ob[0:4 * TW, :].rearrange("(t p) d -> p t d", p=TW), h[:, 0:4, :]).then_inc(out_written, 16)
                    sp.dma_start(ob[4 * TW:N, :], h[0:LAST, 4, :]).then_inc(out_written, 16)
                    sp.wait_ge(y_ready, 1)
                    sp.dma_start(y_dram[bass.ds(b, 1)].rearrange("o p n -> (o p) n"),
                                 ybuf[:].rearrange("p t d -> p (t d)")).then_inc(out_written, 16)
                    sp.wait_ge(out_written, 48)
                    sp.wait_ge(x_in, 16)

                @block.gpsimd
                def _(pool):
                    g = nc.gpsimd
                    g.memset(h[96:TW, NT - 1, :], 0.0).then_inc(pad_zero, 1)
                    pool.wait_ge(pad_zero, 1)
                    xv = xb[:].rearrange("p (i j) -> p i j", i=RES)
                    c = [xv[:, :, dj:dj + STRIDE * (SIDE - 1) + 1:STRIDE] for dj in range(K)]
                    g.tensor_tensor(rs_a, c[0], c[1], ALU.add).then_inc(box_step, 1)
                    g.tensor_tensor(rs_b, c[2], c[3], ALU.add).then_inc(box_step, 1)
                    pool.wait_ge(box_step, 2)
                    g.tensor_tensor(rs_a, rs_a, rs_b, ALU.add).then_inc(box_step, 1)
                    pool.wait_ge(box_step, 3)
                    r = [rs_a[:, di:di + STRIDE * (SIDE - 1) + 1:STRIDE, :] for di in range(K)]
                    bx = box[:, 0:IMG].rearrange("p (i j) -> p i j", i=SIDE)
                    rb = rs_b[:, 0:SIDE, :]
                    g.memset(box[:, IMG:4 * SW], 0.0).then_inc(box_step, 1)
                    g.tensor_tensor(bx, r[0], r[1], ALU.add).then_inc(box_step, 1)
                    g.tensor_tensor(rb, r[2], r[3], ALU.add).then_inc(box_step, 1)
                    pool.wait_ge(box_step, 6)
                    g.tensor_tensor(bx, bx, rb, ALU.add).then_inc(boxed, 1)
                    wait_full(pool, "score")
                    g.memset(ka[DH:DH + 1, :, :], 1.0).then_inc(ones_row, 1)
                    pool.wait_ge(ones_row, 1)
                    for i in range(4):
                        pool.wait_ge(var_ready, i + 1)
                        g.tensor_tensor(rstd[:], vare[:], neg_half[:], ALU.pow).then_inc(rstd_ready, 1)

                @block.tensor
                def _(pe):
                    mm, tr = nc.tensor.matmul, nc.tensor.transpose
                    pe.wait_ge(boxed, 1)
                    wait_free(pe, "score")
                    for t in range(4):
                        last = mm(P("score")[0:SW, 0, VC * t:VC * t + VC], box[:, SW * t:SW * t + SW], vcT[:], start=True, stop=True)
                    last.then_inc(FULL("score"), 1)
                    pe.wait_ge(oh_ready, 1)
                    wait_free(pe, "ohT")
                    for t in range(4):
                        last = tr(P("ohT")[0:VC, 0, SW * t:SW * t + SW], oh[:, t, :], ident[0:SW, 0:SW])
                    last.then_inc(FULL("ohT"), 1)
                    wait_read(pe, "ohT")
                    wait_free(pe, "vsel")
                    mm(P("vsel")[:, 0, 0:IMG], vc_v[:], ohT[:, 0:IMG], start=True, stop=True).then_inc(FULL("vsel"), 1)
                    wait_free(pe, "simmax")
                    for di in range(K):
                        pe.wait_ge(prod_ready, di + 1)
                        for dj in range(K):
                            last = mm(P("simmax")[32 * dj:32 * dj + 32, 0, 0:IMG], sel[:, di, :],
                                      prod[:, di % 2, dj * IMG:(dj + 1) * IMG], start=di == 0, stop=di == K - 1,
                                      skip_group_check=True)
                        last.then_inc(prod_used if di < K - 1 else FULL("simmax"), 1)
                    wait_read(pe, "simmax")
                    for c in range(HC):
                        wait_free(pe, ("h1", c))
                        mm(P(("h1", c))[:, 0, 0:IMG], w1a[:, 128 * c:128 * c + 128], vT, start=True, stop=False)
                        mm(P(("h1", c))[:, 0, 0:IMG], w1b[:, 128 * c:128 * c + 128], simT, start=False, stop=True).then_inc(FULL(("h1", c)), 1)
                    pe.wait_ge(h1_ready, 1)
                    wait_free(pe, "tok")
                    for t in range(NT):
                        w = TW if t < 4 else IMG_LAST
                        o = P("tok")[0:w, t // 4, 128 * (t % 4):128 * (t % 4) + 128]
                        for c in range(HC):
                            mm(o, h1T[:, c, TW * t:TW * t + w], tw2_s[:, c, :], start=c == 0, stop=False)
                        last = mm(o, ones[0:1, 0:w], tb2_s[:], start=False, stop=True)
                    last.then_inc(FULL("tok"), 1)

                    def transposed(key, ready, src):
                        wait_free(pe, key)
                        for t in range(NT):
                            pe.wait_ge(xn_ready, ready + t + 1)
                            last = tr(P(key)[:, t // 4, TW * (t % 4):TW * (t % 4) + TW], src(t), ident[0:TW, 0:TW])
                        last.then_inc(FULL(key), 1)

                    def xn_tile(t):
                        return xn[:, t, 0:D]

                    def project(o, w):
                        for c in range(2):
                            last = mm(o[:, c, 0:TH], w, xnT[:, TH * c:TH * c + TH], start=True, stop=True)
                        return last

                    transposed(("xnT", 0), 0, xn_tile)
                    wait_read(pe, ("xnT", 0))
                    for p in range(PAIRS):
                        wait_free(pe, ("q", p))
                        project(P(("q", p)), wqkv[:, 128 * p:128 * p + 128]).then_inc(FULL(("q", p)), 1)
                        wait_free(pe, ("k", p))
                        project(P(("k", p)), wqkv[:, 512 + 128 * p:512 + 128 * p + 128]).then_inc(FULL(("k", p)), 1)
                    for hd in range(HEADS):
                        if hd % 2 == 0:
                            wait_read(pe, ("q", hd // 2))
                            wait_read(pe, ("k", hd // 2))
                        for t in range(NT):
                            key = ("s", hd, t)
                            wait_free(pe, key)
                            for c in range(2):
                                last = mm(P(key)[0:TW, c, 0:HALF], qa[0:DH, hd, TW * t:TW * t + TW],
                                          ka[0:DH, hd, HALF * c:HALF * c + HALF], start=True, stop=True)
                            last.then_inc(FULL(key), 1)
                    pe.wait_ge(ntau_ready, HEADS * (STEPS + 1))
                    wait_free(pe, "ntT")
                    tr(P("ntT")[0:HEADS * NT, 0, 0:TW], ntau[:].rearrange("p h t -> p (h t)"), ident[0:TW, 0:TW]).then_inc(FULL("ntT"), 1)
                    for t in range(NT):
                        wait_free(pe, ("v", t))
                        mm(P(("v", t))[0:TW, 0, :], xnT[:, TW * t:TW * t + TW], wqkv[:, 1024:1536], start=True, stop=True).then_inc(FULL(("v", t)), 1)
                    pe.wait_ge(thr_in, 16)
                    pe.wait_ge(ones_row, 1)
                    for t in range(NT):
                        wait_read(pe, ("v", t))
                    units = [(p, jt, hh) for p in range(PAIRS) for jt in range(NT) for hh in range(2)]
                    for n in range(len(units) + 2):
                        if n < len(units):
                            p, jt, hh = units[n]
                            hd, key = 2 * p + hh, ("st", 2 * p + hh, jt)
                            wait_free(pe, key)
                            for c in range(2):
                                last = mm(P(key)[0:TW, c, 0:HALF], ka[:, hd, TW * jt:TW * jt + TW],
                                          qa[:, hd, HALF * c:HALF * c + HALF], start=True, stop=True)
                            last.then_inc(FULL(key), 1)
                        if n >= 2:
                            p, jt, hh = units[n - 2]
                            if jt == 0 and hh == 0 and p > 0:
                                pe.wait_ge(acc_read, p)
                            pe.wait_ge(pt_ready, n - 1)
                            hd = 2 * p + hh
                            for c in range(2):
                                last = mm(acc[64 * hh:64 * hh + 64, c, 0:HALF], v[:, jt, DH * hd:DH * hd + DH],
                                          R[:, (n - 2) % NT, HALF * c:HALF * c + HALF], start=jt == 0, stop=jt == NT - 1,
                                          skip_group_check=True)
                            last.then_inc(pt_used, 1)
                    wait_free(pe, "o")
                    pe.wait_ge(acc_read, PAIRS)
                    for t in range(NT):
                        for p in range(PAIRS):
                            last = mm(P("o")[0:TW, t // 4, 128 * (t % 4):128 * (t % 4) + 128], oT[:, p, TW * t:TW * t + TW],
                                      wout[:, p, :], start=p == 0, stop=p == PAIRS - 1)
                    last.then_inc(FULL("o"), 1)

                    def gate(f):
                        wait_free(pe, ("lg", f))
                        for t in range(NT):
                            o = P(("lg", f))[0:TW, 0, E * t:E * t + E]
                            mm(o, xnT[:, TW * t:TW * t + TW], wr[f][:], start=True, stop=False)
                            last = mm(o, ones[0:1, 0:TW], br_s[f][:], start=False, stop=True)
                        last.then_inc(FULL(("lg", f)), 1)
                        pe.wait_ge(cw_ready, f + 1)
                        wait_free(pe, ("cwT", f))
                        for t in range(NT):
                            last = tr(P(("cwT", f))[0:E, t // 4, TW * (t % 4):TW * (t % 4) + TW], cw[:, t, :], ident[0:TW, 0:TW])
                        last.then_inc(FULL(("cwT", f)), 1)
                        wait_read(pe, ("cwT", f))
                        wait_free(pe, ("b2", f))
                        for t in range(NT):
                            last = mm(P(("b2", f))[0:TW, t // 4, 128 * (t % 4):128 * (t % 4) + 128],
                                      cwT[:, TW * t:TW * t + TW], b2_s[f][:], start=True, stop=True)
                        last.then_inc(FULL(("b2", f)), 1)

                    def experts(f):
                        def up(e):
                            for c in range(FC):
                                key = ("hid", f, e, c)
                                wait_free(pe, key)
                                project(P(key), w1[f][:, e, 128 * c:128 * c + 128]).then_inc(FULL(key), 1)

                        up(0)
                        for e in range(E):
                            if e + 1 < E:
                                up(e + 1)
                            key = ("y", f, e)
                            wait_free(pe, key)
                            for c in range(FC):
                                wait_read(pe, ("hid", f, e, c))
                            for t in range(NT):
                                for c in range(FC):
                                    last = mm(P(key)[0:TW, t // 4, 128 * (t % 4):128 * (t % 4) + 128],
                                              hid[:, e % 2, T * c + TW * t:T * c + TW * t + TW], w2[f][:, e, c, :],
                                              start=c == 0, stop=c == FC - 1)
                            last.then_inc(FULL(key), 1)

                    transposed(("xnT", 1), NT, xn_tile)
                    wait_read(pe, ("xnT", 1))
                    gate(0)
                    experts(0)
                    transposed(("xnT", 2), 2 * NT, xn_tile)
                    wait_read(pe, ("xnT", 2))
                    wait_free(pe, "k2")
                    project(P("k2"), wxx[:]).then_inc(FULL("k2"), 1)
                    wait_free(pe, "q2")
                    for c in range(2):
                        last = mm(P("q2")[U * c:U * c + U, 0, 0:TH], wt[:], xnT[:, TH * c:TH * c + TH], start=True, stop=True,
                                  skip_group_check=True)
                    last.then_inc(FULL("q2"), 1)

                    def turn(G):
                        key = ("et", G)
                        pe.wait_ge(acc_read, PAIRS + G + 1)
                        wait_free(pe, key)
                        for jt in range(NT):
                            last = tr(P(key)[0:TW, jt // 4, 128 * (jt % 4):128 * (jt % 4) + 128], ex[:, G % 2, TW * jt:TW * jt + TW], ident[:])
                        last.then_inc(FULL(key), 1)

                    for G in range(GROUPS):
                        for m in range(M):
                            if m == 0:
                                wait_read(pe, "k2")
                                pe.wait_ge(acc_read, PAIRS + G)
                            n = G * M + m
                            pe.wait_ge(th_ready, n + 1)
                            for c in range(2):
                                for g4 in range(4):
                                    last = mm(acc[32 * g4:32 * g4 + 32, c, 0:HALF], wasel[:, m, :],
                                              th[:, n % TH_RING, N * g4 + HALF * c:N * g4 + HALF * c + HALF],
                                              start=m == 0, stop=m == M - 1, skip_group_check=True)
                            last.then_inc(th_used, 1)
                            if m == 2 and G > 0:
                                turn(G - 1)
                    turn(GROUPS - 1)
                    for G in range(GROUPS):
                        wait_read(pe, ("et", G))
                    wait_free(pe, "v1")
                    for t in range(NT):
                        for jt in range(NT):
                            last = mm(P("v1")[0:TW, t // 3, (D + 1) * (t % 3):(D + 1) * (t % 3) + D + 1],
                                      ET[:, jt, TW * t:TW * t + TW], xn[:, jt, :], start=jt == 0, stop=jt == NT - 1)
                    last.then_inc(FULL("v1"), 1)
                    transposed(("xnT", 3), 3 * NT, xn_tile)
                    wait_read(pe, ("xnT", 3))
                    gate(1)
                    transposed("xsT", 4 * NT, xn_tile)
                    wait_read(pe, "xsT")
                    experts(1)

                @block.scalar
                def _(act):
                    A = nc.scalar.activation

                    def two(dst, key, parts, w):
                        return dst.rearrange("p (c n) -> p c n", c=2), P(key)[parts, :, 0:w]

                    wait_full(act, "vsel")
                    A(vT, P("vsel")[:, 0, 0:IMG], ACT.Copy).then_inc(READ("vsel"), 1)
                    wait_full(act, "simmax")
                    A(simT, P("simmax")[:, 0, 0:IMG], ACT.Copy).then_inc(READ("simmax"), 1)
                    for c in range(HC):
                        wait_full(act, ("h1", c))
                        A(h1T[:, c, :], P(("h1", c))[:, 0, 0:IMG], ACT.Identity, bias=tb1_s[:, c:c + 1]).then_inc(READ(("h1", c)), 1)
                    wait_full(act, "tok")
                    act.wait_ge(pad_zero, 1)
                    A(h[:, 0:4, :].rearrange("p t d -> p (t d)"), P("tok")[0:TW, 0, :], ACT.Tanh)
                    A(h[0:IMG_LAST, 4, :], P("tok")[0:IMG_LAST, 1, 0:D], ACT.Tanh).then_inc(READ("tok"), 1)

                    def xnT_copy(key):
                        wait_full(act, key)
                        A(xnT[:, 0:4 * TW], P(key)[:, 0, 0:4 * TW], ACT.Copy)
                        A(xnT[:, 4 * TW:T], P(key)[:, 1, 0:TW], ACT.Copy).then_inc(READ(key), 1)

                    xnT_copy(("xnT", 0))
                    for p in range(PAIRS):
                        key = ("q", p)
                        wait_full(act, key)
                        for hh in range(2):
                            dst, src = two(qa[0:DH, 2 * p + hh, :], key, slice(DH * hh, DH * hh + DH), TH)
                            last = A(dst, src, ACT.Copy, scale=DH ** -0.5 / 2)
                        last.then_inc(READ(key), 1)
                    for hp in range(PAIRS):
                        for hh in range(2):
                            hd = 2 * hp + hh
                            for t in range(NT):
                                key = ("s", hd, t)
                                wait_full(act, key)
                                if hp > 0:
                                    act.wait_ge(relu_ready, hp * 2 * NT * STEPS)
                                dst, src = two(Z[:, NT * hh + t, :], key, slice(0, TW), HALF)
                                A(dst, src, ACT.Identity, accum_out=sumz[:, hd, t:t + 1]).then_inc(READ(key), 1)
                        for k in range(STEPS):
                            for hh in range(2):
                                hd = 2 * hp + hh
                                act.wait_ge(ntau_ready, hp * 2 * (STEPS + 1) + 2 * k + hh + 1)
                                for t in range(NT):
                                    n = ((hp * STEPS + k) * 2 + hh) * NT + t
                                    if n >= NT:
                                        act.wait_ge(square_ready, n - NT + 1)
                                    A(R[:, t, :], Z[:, NT * hh + t, :], ACT.Relu, bias=ntau[:, hd, t:t + 1],
                                      accum_out=s1[:, hh, t:t + 1]).then_inc(relu_ready, 1)
                    wait_full(act, "ntT")
                    A(ntT[:], P("ntT")[0:HEADS * NT, 0, 0:TW], ACT.Copy).then_inc(READ("ntT"), 1)
                    for p in range(PAIRS):
                        for jt in range(NT):
                            for hh in range(2):
                                n = (p * NT + jt) * 2 + hh
                                key = ("st", 2 * p + hh, jt)
                                wait_full(act, key)
                                if n >= NT:
                                    act.wait_ge(pt_used, n - NT + 1)
                                dst, src = two(R[:, n % NT, :], key, slice(0, TW), HALF)
                                A(dst, src, ACT.Relu).then_inc(READ(key), 1)
                        act.wait_ge(pt_used, 2 * NT * (p + 1))
                        A(oT[:, p, 0:N].rearrange("p (c n) -> p c n", c=2), acc[:, :, 0:HALF], ACT.Copy).then_inc(acc_read, 1)

                    def gate(f):
                        act.wait_ge(lg_ready, f + 1)
                        A(pr[:], lg[:], ACT.Exp).then_inc(exp_ready, 1)
                        wait_full(act, ("cwT", f))
                        A(cwT[:, 0:4 * TW], P(("cwT", f))[0:E, 0, 0:4 * TW], ACT.Copy)
                        A(cwT[:, 4 * TW:T], P(("cwT", f))[0:E, 1, 0:TW], ACT.Copy).then_inc(READ(("cwT", f)), 1)

                    def experts(f):
                        for e in range(E):
                            for c in range(0, FC, 2):
                                key = ("hid", f, e, c)
                                wait_full(act, key)
                                dst, src = two(hid[:, e % 2, T * c:T * c + T], key, slice(0, 128), TH)
                                A(dst, src, ACT.Relu, bias=b1_s[f][:, e, c:c + 1]).then_inc(READ(key), 1)

                    xnT_copy(("xnT", 1))
                    gate(0)
                    experts(0)
                    xnT_copy(("xnT", 2))
                    wait_full(act, "k2")
                    dst, src = two(K2[:], "k2", slice(0, 128), TH)
                    A(dst, src, ACT.Copy).then_inc(READ("k2"), 1)
                    wait_read(act, "k2")
                    wait_read(act, "q2")
                    for G in range(GROUPS):
                        for m in range(M):
                            n = G * M + m
                            if n >= TH_RING:
                                act.wait_ge(th_used, n - TH_RING + 1)
                            for g4 in range(4):
                                q = 4 * M * G + M * g4 + m
                                last = A(th[:, n % TH_RING, N * g4:N * g4 + N], K2[:, 0:N], ACT.Tanh, bias=Q2[:, q:q + 1])
                            last.then_inc(th_ready, 1)
                        act.wait_ge(th_used, M * (G + 1))
                        A(ex[:, G % 2, 0:N].rearrange("p (c n) -> p c n", c=2), acc[:, :, 0:HALF], ACT.Exp,
                          bias=ba_s[:]).then_inc(acc_read, 1)
                    xnT_copy(("xnT", 3))
                    gate(1)
                    xnT_copy("xsT")
                    experts(1)

                @block.vector
                def _(dve):
                    V = nc.vector
                    links = [0]

                    def link(ins):
                        links[0] += 1
                        ins.then_inc(dve_link, 1)
                        dve.wait_ge(dve_link, links[0])

                    def wide(ap):
                        return ap.unsqueeze(2).broadcast_to([TW, NT, E])

                    wait_full(dve, "score")
                    for t in range(4):
                        last = V.max(tmx8[:, t, :], P("score")[0:SW, 0, VC * t:VC * t + VC])
                    link(last)
                    for t in range(4):
                        last = V.max_index(tidx8[:, t, :], tmx8[:, t, :], P("score")[0:SW, 0, VC * t:VC * t + VC])
                    last.then_inc(READ("score"), 1)
                    wait_read(dve, "score")
                    link(V.tensor_copy(tidxf[:], tidx8[:, :, 0]))
                    for t in range(4):
                        last = V.tensor_scalar(oh[:, t, :], iota_v[:], tidxf[:, t:t + 1], None, ALU.is_equal)
                    last.then_inc(oh_ready, 1)
                    wait_full(dve, "ohT")
                    V.tensor_copy(ohT[:], P("ohT")[0:VC, 0, 0:4 * SW]).then_inc(READ("ohT"), 1)
                    wait_read(dve, "vsel")
                    for di in range(K):
                        if di >= 2:
                            dve.wait_ge(prod_used, di - 1)
                        whole = xb[:]
                        patch = bass.AP(whole.tensor, whole.offset + RES * di,
                                        [list(whole.ap[0]), [1, K], [STRIDE * RES, SIDE], [STRIDE, SIDE]])
                        word = bass.AP(vT.tensor, vT.offset, [list(vT.ap[0]), [0, K], [SIDE, SIDE], [1, SIDE]])
                        V.tensor_tensor(prod[:, di % 2, :].rearrange("p (k i j) -> p k i j", k=K, i=SIDE), word, patch,
                                        ALU.mult).then_inc(prod_ready, 1)

                    for c in range(HC):
                        wait_read(dve, ("h1", c))
                    V.scalar_tensor_tensor(h1T[:], h1T[:], 0.2, h1T[:], ALU.mult, ALU.max).then_inc(h1_ready, 1)

                    def norm(i):
                        for t in range(NT):
                            last = V.bn_stats(stats[:, t, :], h[:, t, :])
                        link(last)
                        for t in range(NT):
                            last = V.bn_aggr(mv[:, t, :], stats[:, t, :])
                        link(last)
                        V.tensor_scalar(vare[:], mv[:, :, 1], EPS, None, ALU.add).then_inc(var_ready, 1)
                        dve.wait_ge(rstd_ready, i + 1)
                        for t in range(NT):
                            V.tensor_scalar(xn[:, t, 0:D], h[:, t, :], mv[:, t, 0:1], rstd[:, t:t + 1], ALU.subtract,
                                            ALU.mult).then_inc(xn_ready, 1)

                    wait_read(dve, "tok")
                    dve.wait_ge(txt_in, 16)
                    norm(0)
                    for p in range(PAIRS):
                        key = ("k", p)
                        wait_full(dve, key)
                        for hh in range(2):
                            last = V.tensor_copy(ka[0:DH, 2 * p + hh, :].rearrange("p (c n) -> p c n", c=2),
                                                 P(key)[DH * hh:DH * hh + DH, :, 0:TH])
                        last.then_inc(READ(key), 1)
                    for hp in range(PAIRS):
                        for hh in range(2):
                            hd = 2 * hp + hh
                            wait_read(dve, ("s", hd, NT - 1))
                            V.tensor_reduce(zmax[:, hd, :], Z[:, NT * hh:NT * hh + NT, :], AX_X, ALU.max).then_inc(dve_link, 1)
                            links[0] += 1
                            V.tensor_scalar(ntau[:, hd, :], sumz[:, hd, :], -1.0 / N, 1.0 / sqrt(N), ALU.mult, ALU.add).then_inc(dve_link, 1)
                            links[0] += 1
                            dve.wait_ge(dve_link, links[0])
                            link(V.tensor_scalar(sa[:], zmax[:, hd, :], -1.0, 1.0, ALU.mult, ALU.add))
                            V.tensor_tensor(ntau[:, hd, :], ntau[:, hd, :], sa[:], ALU.min).then_inc(ntau_ready, 1)
                        for k in range(STEPS):
                            for hh in range(2):
                                hd = 2 * hp + hh
                                for t in range(NT):
                                    n = ((hp * STEPS + k) * 2 + hh) * NT + t
                                    dve.wait_ge(relu_ready, n + 1)
                                    V.scalar_tensor_tensor(R[:, t, :], R[:, t, :], 1.0, R[:, t, :], ALU.mult, ALU.mult,
                                                           accum_out=s2[:, hh, t:t + 1]).then_inc(square_ready, 1)
                                dve.wait_ge(square_ready, n + 1)
                                link(V.tensor_scalar(sa[:], s2[:, hh, :], 3.0, 1.0, ALU.mult, ALU.add))
                                link(V.tensor_tensor(sa[:], sa[:], s1[:, hh, :], ALU.mult))
                                link(V.reciprocal(sa[:], sa[:]))
                                link(V.scalar_tensor_tensor(sc[:], s2[:, hh, :], -1.0, s2[:, hh, :], ALU.add, ALU.mult))
                                link(V.scalar_tensor_tensor(sc[:], sc[:], -2.0, sa[:], ALU.mult, ALU.mult))
                                V.tensor_tensor(ntau[:, hd, :], ntau[:, hd, :], sc[:], ALU.add).then_inc(ntau_ready, 1)
                    for t in range(NT):
                        key = ("v", t)
                        wait_full(dve, key)
                        V.tensor_copy(v[:, t, :], P(key)[0:TW, 0, :]).then_inc(READ(key), 1)
                    for n in range(HEADS * NT):
                        p, jt, hh = n // (2 * NT), n // 2 % NT, n % 2
                        wait_read(dve, ("st", 2 * p + hh, jt))
                        V.tensor_tensor(R[:, n % NT, :], R[:, n % NT, :], R[:, n % NT, :], ALU.mult).then_inc(pt_ready, 1)

                    def add_rows(dst, key, how):
                        wait_full(dve, key)
                        for c, t0, t1 in ((0, 0, 4), (1, 4, 5)):
                            d = dst[:, t0:t1, :].rearrange("p t d -> p (t d)")
                            s = P(key)[0:TW, c, 0:D * (t1 - t0)]
                            last = V.tensor_tensor(d, d, s, ALU.add) if how == "add" else V.tensor_copy(d, s)
                        last.then_inc(READ(key), 1)
                        wait_read(dve, key)

                    add_rows(h, "o", "add")
                    norm(1)

                    def gate(f):
                        key = ("lg", f)
                        wait_full(dve, key)
                        V.tensor_copy(lg[:].rearrange("p t e -> p (t e)"), P(key)[0:TW, 0, 0:NT * E]).then_inc(READ(key), 1)
                        wait_read(dve, key)
                        for t in range(NT):
                            last = V.max(mx8[:, t, :], lg[:, t, :])
                        link(last)
                        V.tensor_tensor(lg[:], lg[:], wide(mx8[:, :, 0]), ALU.subtract).then_inc(lg_ready, 1)
                        dve.wait_ge(exp_ready, f + 1)
                        link(V.tensor_reduce(den[:], pr[:], AX_X, ALU.add))
                        link(V.reciprocal(den[:], den[:]))
                        link(V.tensor_tensor(pr[:], pr[:], wide(den[:]), ALU.mult))
                        for t in range(NT):
                            last = V.max(mx8[:, t, :], pr[:, t, :])
                        link(last)
                        for t in range(NT):
                            last = V.max_index(idx8[:, t, :], mx8[:, t, :], pr[:, t, :])
                        link(last)
                        link(V.tensor_copy(idxf[:], idx8[:, :, 0:2]))
                        experts_iota = iota_e[:].unsqueeze(1).broadcast_to([TW, NT, E])
                        if f == 0:
                            link(V.tensor_tensor(cw[:], experts_iota, wide(idxf[:, :, 0]), ALU.is_equal))
                            link(V.tensor_tensor(oh2[:], experts_iota, wide(idxf[:, :, 1]), ALU.is_equal))
                            link(V.tensor_tensor(cw[:], cw[:], oh2[:], ALU.add))
                            V.tensor_tensor(cw[:], cw[:], pr[:], ALU.mult).then_inc(cw_ready, 1)
                            dve.wait_ge(cw_ready, 1)
                            add_rows(h, ("b2", 0), "add")
                        else:
                            V.tensor_tensor(cw[:], experts_iota, wide(idxf[:, :, 0]), ALU.is_equal).then_inc(cw_ready, 1)
                            dve.wait_ge(cw_ready, 2)
                            for t in range(NT):
                                V.tensor_scalar(xn[:, t, 0:D], xn[:, t, 0:D], mx8[:, t, 0:1], None, ALU.mult).then_inc(xn_ready, 1)
                            V.tensor_tensor(OH[:, bass.ds(b * NT, NT), :], cw[:], wide(valid[:]), ALU.mult).then_inc(h_ready, 1)
                            add_rows(ybuf, ("b2", 1), "copy")

                    def experts(f, dst):
                        for e in range(E + 1):
                            if e < E:
                                for c in range(1, FC, 2):
                                    key = ("hid", f, e, c)
                                    wait_full(dve, key)
                                    V.tensor_scalar(hid[:, e % 2, T * c:T * c + T].rearrange("p (c n) -> p c n", c=2),
                                                    P(key)[:, :, 0:TH], b1_s[f][:, e, c:c + 1], 0.0, ALU.add,
                                                    ALU.max).then_inc(READ(key), 1)
                            if e > 0:
                                key = ("y", f, e - 1)
                                wait_full(dve, key)
                                if e > 1:
                                    wait_read(dve, ("y", f, e - 2))
                                for t in range(NT):
                                    last = V.scalar_tensor_tensor(dst[:, t, :], P(key)[0:TW, t // 4, 128 * (t % 4):128 * (t % 4) + 128],
                                                                  cw[:, t, e - 1:e], dst[:, t, :], ALU.mult, ALU.add)
                                last.then_inc(READ(key), 1)

                    gate(0)
                    experts(0, h)
                    wait_read(dve, ("y", 0, E - 1))
                    norm(2)
                    wait_full(dve, "q2")
                    V.tensor_scalar(Q2[:], P("q2")[:, 0, 0:TH], bt2[:], None, ALU.add).then_inc(READ("q2"), 1)
                    for G in range(GROUPS):
                        key = ("et", G)
                        wait_full(dve, key)
                        at = 4 * M * G
                        for s in range(2):
                            V.tensor_copy(ET[:, 0:4, TH * s + at:TH * s + at + 4 * M].rearrange("p j (g m) -> p j g m", g=4),
                                          P(key)[0:TW, 0, :].rearrange("p (j g m) -> p j g m", j=4, g=4)[:, :, :, M * s:M * s + M])
                        last = None
                        for s in range(2):
                            last = V.tensor_copy(ET[:, 4, TH * s + at:TH * s + at + 4 * M].rearrange("p (g m) -> p g m", g=4),
                                                 P(key)[0:TW, 1, 0:128].rearrange("p (g m) -> p g m", g=4)[:, :, M * s:M * s + M])
                        last.then_inc(READ(key), 1)
                    wait_full(dve, "v1")
                    v1 = P("v1")[0:TW, :, 0:3 * (D + 1)].rearrange("p c (t d) -> p c t d", d=D + 1)
                    V.tensor_scalar(den[:, 0:3], v1[:, 0, 0:3, D], 1e-7, None, ALU.add)
                    link(V.tensor_scalar(den[:, 3:5], v1[:, 1, 0:2, D], 1e-7, None, ALU.add))
                    link(V.reciprocal(den[:], den[:]))
                    for t in range(NT):
                        last = V.scalar_tensor_tensor(h[:, t, :], v1[:, t // 3, t % 3, 0:D], den[:, t:t + 1], h[:, t, :], ALU.mult, ALU.add)
                    last.then_inc(READ("v1"), 1)
                    wait_read(dve, "v1")
                    norm(3)
                    gate(1)
                    experts(1, ybuf)
                    wait_read(dve, ("y", 1, E - 1))
                    V.tensor_copy(sa[:], sa[:]).then_inc(y_ready, 1)

            nc.all_engine_barrier(sems_to_clear=batch_sems)
        with nc.Block() as last:
            @last.sync
            def _(sp):
                sp.dma_start(yall, y_dram.rearrange("b p n -> p b n")).then_inc(y_in, 16)

            @last.gpsimd
            def _(pool):
                g = nc.gpsimd
                pool.wait_ge(y_in, 16)
                pool.wait_ge(pos_ready, 1)
                rows = out.rearrange("b t d -> (b t) d")
                for n in range(B * NT):
                    w = TW if n % NT < NT - 1 else LAST
                    g.indirect_dma_start(out=rows, out_offset=bass.IndirectOffsetOnAxis(ap=pos_u[0:w, n:n + 1], axis=0),
                                         in_=yall[0:w, n // NT, D * (n % NT):D * (n % NT) + D], in_offset=None,
                                         compute_op=ALU.add).then_inc(scattered, 16)
                pool.wait_ge(scattered, 16 * B * NT)

            @last.tensor
            def _(pe):
                mm = nc.tensor.matmul
                W = B * NT * E // 2
                for n, w in enumerate((before, ones)):
                    for c in range(2):
                        last = mm(ps[n][0:TW, c, 0:W], w[0:TW, 0:TW], OH[:].rearrange("p t e -> p (t e)")[:, W * c:W * c + W],
                                  start=True, stop=True)
                last.then_inc(place_full, 1)

            @last.vector
            def _(dve):
                V = nc.vector
                step = [0]

                def then(ins):
                    step[0] += 1
                    ins.then_inc(place_step, 1)
                    dve.wait_ge(place_step, step[0])

                tiles = B * NT
                dve.wait_ge(place_full, 1)
                W = tiles * E // 2

                def banks(s):
                    return ps[s][0:TW, :, 0:W]

                def run(ap):
                    return ap.rearrange("p (c n) -> p c n", c=2)

                then(V.tensor_copy(run(inc[:, 0, :]), banks(1)))
                cur, d = 0, 1
                while d < tiles:
                    V.tensor_copy(inc[:, 1 - cur, 0:d * E], inc[:, cur, 0:d * E])
                    then(V.tensor_tensor(inc[:, 1 - cur, d * E:], inc[:, cur, d * E:], inc[:, cur, 0:(tiles - d) * E], ALU.add))
                    cur, d = 1 - cur, 2 * d
                base = lg[:, 0, :]
                then(V.memset(base[:, 0:1], 0.0))
                for e in range(1, E):
                    then(V.tensor_tensor(base[:, e:e + 1], base[:, e - 1:e], inc[:, cur, (tiles - 1) * E + e - 1:(tiles - 1) * E + e], ALU.add))
                s = inc[:, cur, :]
                then(V.tensor_tensor(run(s), run(s), banks(1), ALU.subtract))
                then(V.tensor_tensor(run(s), run(s), banks(0), ALU.add))
                s3 = s.rearrange("p (t e) -> p t e", e=E)
                then(V.tensor_tensor(s3, s3, base.unsqueeze(1).broadcast_to([TW, tiles, E]), ALU.add))
                then(V.tensor_tensor(s3, s3, OH[:], ALU.mult))
                then(V.tensor_reduce(pos[:], s3, AX_X, ALU.add))
                V.tensor_copy(pos_u[:], pos[:]).then_inc(pos_ready, 1)


_INS = ["x", "txt", "L0_tok_vc_dict", "L0_tok_W1", "L0_tok_b1", "L0_tok_W2", "L0_tok_b2", "L0_attn_w_qkv",
        "L0_attn_w_out", "L0_ffn_Wr", "L0_ffn_br", "L0_ffn_W1", "L0_ffn_b1", "L0_ffn_W2", "L0_ffn_b2", "L1_attn_Wx",
        "L1_attn_Wt", "L1_attn_bt", "L1_attn_Wa", "L1_attn_ba", "L1_ffn_Wg", "L1_ffn_bg", "L1_ffn_W1", "L1_ffn_b1",
        "L1_ffn_W2", "L1_ffn_b2"]


def kernel(**inputs):
    import concourse.bacc as bacc
    from concourse.bass_utils import run_bass_kernel_spmd

    nc = bacc.Bacc("TRN2", target_bir_lowering=False, num_devices=1)
    arrays, args = {}, []
    for name in _INS:
        a = np.ascontiguousarray(inputs[name])
        arrays[f"in_{name}"] = a
        args.append(nc.dram_tensor(f"in_{name}", a.shape, mybir.dt.from_np(a.dtype), kind="ExternalInput").ap())
    batches = inputs["x"].shape[0]
    out = nc.dram_tensor("out", (batches, N, D), F32, kind="ExternalOutput").ap()
    y_dram = nc.dram_tensor("y_rows", (batches, TW, NT * D), F32, kind="Internal").ap()
    fusion_kernel(nc, *args, out, y_dram, B=batches)
    r = run_bass_kernel_spmd(nc, [arrays], core_ids=[0])
    return r.results[0]["out"]
```

```python
from contextlib import ExitStack
from math import sqrt

import numpy as np

import concourse.bass as bass
from concourse import mybir

F32 = mybir.dt.float32
U32 = mybir.dt.uint32
I32 = mybir.dt.int32
ALU = mybir.AluOpType
ACT = mybir.ActivationFunctionType
AX_X = mybir.AxisListType.X

D = 128
RES, K, STRIDE = 64, 4, 3
SIDE = (RES - K) // STRIDE + 1
IMG = SIDE * SIDE
TXT = 77
N = IMG + TXT
HALF = N // 2
NT, TW = 5, 104
T = NT * TW
TH = T // 2
IMG_LAST = IMG - 4 * TW
LAST = N - 4 * TW
VC = 100
SW = 111
HEADS, DH = 8, 64
PAIRS = HEADS // 2
STEPS = 3
MORE_STEPS = 12
SETTLED = 1e-3
E, FC = 8, 4
HC = 3
U = 64
GROUPS, M = 5, 13
QUADS = GROUPS * M
ROWS = 128
XT_RING = 3
RING, AV, LOGITS = (0, 1), 2, 3
TH_RING = 3
EPS = 1e-5


def front_stages():
    out = [(("score",), 4), (("pick",), 4), (("sims",), 4), (("mlp",), 4), (("norm", 0), 4)]
    out += [(("qk", p), 1) for p in range(PAIRS)]
    out += [(("means",), 0)]
    for hp in range(PAIRS):
        out += [(("scores", hp), 2)] + [(("step", hp, k), 1) for k in range(1, STEPS)]
    out += [(("check",), 2), (("more",), 0), (("rows",), 2)]
    out += [(("weigh", n), int(n % 2 == 0)) for n in range(HEADS * NT + 2)]
    out += [(("o",), 2), (("norm", 1), 2), (("box",), 0), (("gate", 0), 3), (("up", 0), 1)]
    for e in range(E):
        out += [(("up", e + 1), 1)] if e + 1 < E else []
        out += [(("y", e), 1)]
    return out


def back_stages():
    out = [("take",), ("norm", 2), ("k2q2",)]
    for n in range(QUADS + 1):
        out += [("tanh", n)] if n < QUADS else []
        out += [("quad", n - 1)] if n > 0 else []
        if n > 0 and n % M == 0:
            out += [("exp", n // M - 1)]
        if n % M == 2 and n > M:
            out += [("turn", n // M - 1)]
    return out + [("turn", GROUPS - 1), ("v1",), ("norm", 3), ("gate", 1)]


def schedule(front, back):
    if not back:
        return [stage for stage, _ in front_stages()]
    if not front:
        return back_stages()
    rest = back_stages()
    out = [rest.pop(0) for _ in range(3)]
    for stage, quads in front_stages():
        out.append(stage)
        while rest and quads >= 0:
            if rest[0][0] == "tanh":
                if quads == 0:
                    break
                quads -= 1
            elif quads == 0 and rest[0][0] in ("v1", "norm", "gate"):
                break
            out.append(rest.pop(0))
            if out[-1][0] in ("v1", "norm", "gate"):
                break
    return out + rest


def psum_plan(stages):
    pair, nth, count, signalled, turn = {}, {}, [0] * 4, [0] * 4, 0
    for stage in stages:
        kind, arg = stage[0], stage[1:]
        keys = {
            "score": ["score"], "pick": ["ohT", "vsel"], "sims": ["simmax"],
            "mlp": [("h1", c) for c in range(HC)] + ["tok"], "norm": [("xnT",) + arg], "qk": [("q",) + arg, ("k",) + arg],
            "scores": [("s", 2 * arg[0] + hh, t) for hh in range(2) for t in range(NT)] if arg else [],
            "means": ["means"], "check": ["residue"], "rows": ["ntT"] + [("v", t) for t in range(NT)],
            "weigh": ([("av", arg[0] // (2 * NT))] if arg and arg[0] % (2 * NT) == 0 and arg[0] < HEADS * NT else [])
            + ([("st",) + arg] if arg and arg[0] < HEADS * NT else []),
            "o": ["o"], "gate": [("lg",) + arg] + (["cwT", "b2"] if arg == (0,) else []),
            "up": [("hid",) + arg + (c,) for c in range(FC)], "y": [("y",) + arg],
            "k2q2": ["k2", "q2"], "quad": [("logits", arg[0] // M)] if arg and arg[0] % M == 0 else [],
            "turn": [("turned",) + arg], "v1": ["v1"],
        }.get(kind, [])
        for key in keys:
            name = key[0] if isinstance(key, tuple) else key
            if name in ("av", "y", "tok", "simmax"):
                p = AV
            elif name == "logits":
                p = LOGITS
            else:
                p, turn = RING[turn], (turn + 1) % len(RING)
            pair[key], nth[key] = p, (count[p], signalled[p])
            count[p] += 1
            signalled[p] += name not in ("av", "logits")
    return pair, nth



def fusion_kernel(nc, x, txt, vc, tW1, tb1, tW2, tb2, w_qkv, w_out, Wr, br, W1, b1, W2, b2,
                  Wx, Wt, bt, Wa, ba, Wg, bg, V1, c1, V2, c2, out, x_rows, x_sorted, B=16):
    ctx = ExitStack()
    SORTED = (B * N + ROWS - 1) // ROWS
    PAIRED = SORTED + E - 1
    PER_PASS = -(-PAIRED // 4)
    PASSES = -(-PAIRED // PER_PASS)
    PP = PASSES * PER_PASS

    def sb(name, shape, dt=F32):
        return ctx.enter_context(nc.sbuf_tensor(name, shape, dt))

    def sem(name):
        return ctx.enter_context(nc.semaphore(name))

    with ctx:
        vc_v = sb("vc_v", [VC, D])
        vcT = sb("vcT", [D, VC])
        w1a = sb("w1a", [D, HC * 128])
        w1b = sb("w1b", [128, HC * 128])
        tb1_s = sb("tb1_s", [128, HC])
        tw2_s = sb("tw2_s", [128, HC, D])
        tb2_s = sb("tb2_s", [1, D])
        wqkv = sb("wqkv", [D, 3 * HEADS * DH])
        wout = sb("wout", [128, PAIRS, D])
        wr = [sb(f"wr{f}", [D, E]) for f in range(2)]
        br_s = [sb(f"br{f}", [1, E]) for f in range(2)]
        w1 = sb("w1", [D, E, FC * 128])
        b1_s = sb("b1_s", [128, E, FC])
        w2 = sb("w2", [128, E, FC, D])
        b2_s = sb("b2_s", [E, D])
        wxx = sb("wxx", [D, 2 * U])
        wt = sb("wt", [D, U])
        bt2 = sb("bt2", [128, 1])
        wa2 = sb("wa2", [128, 1])
        ba_s = sb("ba_s", [128, 1])
        ident = sb("ident", [128, 128])
        ones = sb("ones", [128, 128])
        before = sb("before", [TW, TW])
        valid = sb("valid", [TW, NT])
        sel = sb("sel", [128, K, 32])
        wasel = sb("wasel", [128, M, 32])
        iota_v = sb("iota_v", [SW, VC])
        iota_e = sb("iota_e", [TW, E])
        neg_half = sb("neg_half", [TW, NT])
        xb = sb("xb", [D, RES * RES])
        h = [sb(f"h{i}", [TW, NT, D]) for i in range(2)]
        xn = [sb(f"xn{i}", [TW, NT, D + 1]) for i in range(2)]
        xnT = [sb(f"xnT{i}", [D, T]) for i in range(2)]
        stats = [sb(f"stats{i}", [TW, NT, 6]) for i in range(2)]
        mv = [sb(f"mv{i}", [TW, NT, 2]) for i in range(2)]
        vare = [sb(f"vare{i}", [TW, NT]) for i in range(2)]
        rstd = [sb(f"rstd{i}", [TW, NT]) for i in range(2)]
        lg = [sb(f"lg{i}", [TW, NT, E]) for i in range(2)]
        mx8 = [sb(f"mx8{i}", [TW, NT, 8]) for i in range(2)]
        idx8 = [sb(f"idx8{i}", [TW, NT, 8], U32) for i in range(2)]
        idxf = [sb(f"idxf{i}", [TW, NT, 2]) for i in range(2)]
        pr = [sb(f"pr{i}", [TW, NT, E]) for i in range(2)]
        den = [sb(f"den{i}", [TW, NT]) for i in range(2)]
        ntau = sb("ntau", [TW, HEADS, NT])
        ntT = sb("ntT", [HEADS * NT, TW])
        rise = sb("rise", [TW, HEADS, NT])
        ksum = sb("ksum", [DH, HEADS])
        zmax = sb("zmax", [TW, NT])
        s1 = sb("s1", [TW, HEADS, NT])
        s2 = sb("s2", [TW, HEADS, NT])
        sa = sb("sa", [TW, NT])
        sc = sb("sc", [TW, NT])
        res = sb("res", [TW, HEADS * NT])
        worst = sb("worst", [TW, 1])
        flag_f = sb("flag_f", [1, 1])
        unsettled = sb("unsettled", [1, 1], I32)
        oh2 = sb("oh2", [TW, NT, E])
        cw = sb("cw", [TW, NT, E])
        cwT = sb("cwT", [E, T])
        K2 = sb("K2", [128, T])
        Q2 = sb("Q2", [128, TH])
        ex = sb("ex", [128, 2, T])
        OH = sb("OH", [TW, B * NT, E])
        tidx8 = sb("tidx8", [SW, 4, 8], U32)
        tidxf = sb("tidxf", [SW, 4])
        tmx8 = sb("tmx8", [SW, 4, 8])
        QK = 7770
        BACK = QK + 2 * HEADS * T
        WORDS = BACK + 4 * N * TH_RING + NT * T
        arena = sb("arena", [128, WORDS])

        def cut(at, parts, *dims):
            n = int(np.prod(dims))
            assert at + n <= WORDS
            ap = arena[0:parts, at:at + n]
            if len(dims) == 2:
                return ap.rearrange("p (a c) -> p a c", a=dims[0])
            if len(dims) == 3:
                return ap.rearrange("p (a c d) -> p a c d", a=dims[0], c=dims[1])
            return ap

        rs_a, rs_b = cut(QK, 128, RES, SIDE), cut(QK + 1344, 128, RES, SIDE)
        box = cut(QK + 2688, 128, 4 * SW)
        prod = cut(0, 128, 2, K * IMG)
        vT, simT = cut(3528, 128, IMG), cut(3969, 128, IMG)
        ohT, oh = cut(4410, VC, 4 * SW), cut(4854, SW, 4, VC)
        h1T = cut(5254, 128, HC, IMG)
        qa = cut(QK, DH + 1, HEADS, T)
        ka = cut(QK + HEADS * T, DH + 1, HEADS, T)
        Z, R = cut(0, TW, 2 * NT, N), cut(5180, TW, NT, N)
        oT, v = cut(0, 128, PAIRS, T), cut(2100, TW, NT, HEADS * DH)
        hid = cut(0, 128, 2, FC * T)
        th, ET = cut(BACK, 128, TH_RING, 4 * N), cut(BACK + 4 * N * TH_RING, TW, NT, T)
        c1_s, c2_s = cut(0, ROWS, E, FC * 128), cut(E * FC * 128, ROWS, E, D)
        at = E * (FC + 1) * 128
        y_sum = cut(at, ROWS, SORTED, D)
        xall = cut(at + SORTED * D, TW, B, NT * D)
        inc = xb[:, 0:2 * B * NT * E].rearrange("p (a c) -> p a c", a=2)
        xt = xb[:, 0:XT_RING * D].rearrange("p (a c) -> p a c", a=XT_RING)
        xtT, y_row = [xb[:, (XT_RING + i) * D:(XT_RING + i + 2) * D].rearrange("p (a c) -> p a c", a=2) for i in (0, 2)]
        up_b, upT = [xb[:, (XT_RING + 4 + i) * D:(XT_RING + 4 + i + 2 * FC) * D].rearrange("p (a c) -> p a c", a=2)
                     for i in (0, 2 * FC)]
        pos = sb("pos", [TW, B * NT])
        pos_u = sb("pos_u", [TW, B * NT], U32)
        total = sb("total", [128, E])
        first_row = sb("first_row", [128, E])
        end_row = sb("end_row", [128, E])
        first_tile = sb("first_tile", [128, E])
        end_tile = sb("end_tile", [128, E])
        pair_end = sb("pair_end", [128, E])
        shift = sb("shift", [128, E])
        tile_no = sb("tile_no", [128, SORTED])
        over = sb("over", [128, E, SORTED])
        pair_no = sb("pair_no", [128, PP])
        row_no = sb("row_no", [128, 1])
        gt = sb("gt", [128, E, PP])
        own = sb("own", [128, E, PP])
        part = sb("part", [128, E, PP])
        pair_e = sb("pair_e", [128, PP])
        pair_t = sb("pair_t", [128, PP])
        pair_lo = sb("pair_lo", [128, PP])
        pair_hi = sb("pair_hi", [128, PP])
        mask = sb("mask", [128, PP])
        e_tab = sb("e_tab", [128, PP], I32)
        t_tab = sb("t_tab", [128, PP], I32)
        e_now = sb("e_now", [1, PER_PASS], I32)
        t_now = sb("t_now", [1, PER_PASS], I32)
        mask_now = sb("mask_now", [128, PER_PASS])

        ps = [ctx.enter_context(nc.psum_tensor(f"ps{i}", [128, 2, 512], F32)) for i in range(4)]
        full = [sem(f"psum_full{s}") for s in range(4)]
        read = [sem(f"psum_read{s}") for s in range(4)]
        x_in, txt_in, thr_in, out_written = sem("x_in"), sem("txt_in"), sem("thr_in"), sem("out_written")
        pad_zero, box_step, ones_row = sem("pad_zero"), sem("box_step"), sem("ones_row")
        oh_ready, h1_ready = sem("oh_ready"), sem("h1_ready")
        prod_ready, prod_used = sem("prod_ready"), sem("prod_used")
        var_ready = [sem(f"var_ready{i}") for i in range(4)]
        rstd_ready = [sem(f"rstd_ready{i}") for i in range(4)]
        xn_ready = [sem(f"xn_ready{i}") for i in range(4)]
        rise_ready, relu_ready, square_ready = sem("rise_ready"), sem("relu_ready"), sem("square_ready")
        ntau_ready = sem("ntau_ready")
        worst_ready, flag_ready = sem("worst_ready"), sem("flag_ready")
        more_full, more_z, more_ntau = sem("more_full"), sem("more_z"), sem("more_ntau")
        more_relu, more_square, more_link = sem("more_relu"), sem("more_square"), sem("more_link")
        pt_ready, pt_used = sem("pt_ready"), sem("pt_used")
        lg_ready = [sem(f"lg_ready{f}") for f in range(2)]
        exp_ready = [sem(f"exp_ready{f}") for f in range(2)]
        cw_ready, h_taken, xs_ready = sem("cw_ready"), sem("h_taken"), sem("xs_ready")
        th_ready, th_used = sem("th_ready"), sem("th_used")
        dve_link = sem("dve_link")
        batch_sems = range(full[0].num, dve_link.num + 1)
        now_ready = sem("now_ready")
        xt_in = [sem(f"xt_in{i}") for i in range(XT_RING)]
        xt_full, xtT_ready = sem("xt_full"), sem("xtT_ready")
        up_full, up_ready, upT_full, upT_ready = sem("up_full"), sem("up_ready"), sem("upT_full"), sem("upT_ready")
        y_full, y_read, y_added = sem("y_full"), sem("y_read"), sem("y_added")
        pass_sems = range(now_ready.num, y_added.num + 1)
        loaded, setup_done, zeroed, x0_in = sem("loaded"), sem("setup_done"), sem("zeroed"), sem("x0_in")
        vcT_full, tables_ready, box0_step = sem("vcT_full"), sem("tables_ready"), sem("box0_step")
        place_full, place_step, pos_ready = sem("place_full"), sem("place_step"), sem("pos_ready")
        xall_in, last_loaded, pads_zero, iotas = sem("xall_in"), sem("last_loaded"), sem("pads_zero"), sem("iotas")
        scattered, tables_made, out_stored = sem("scattered"), sem("tables_made"), sem("out_stored")

        def box_sums(pool, step):
            g = nc.gpsimd
            xv = xb[:].rearrange("p (i j) -> p i j", i=RES)
            c = [xv[:, :, dj:dj + STRIDE * (SIDE - 1) + 1:STRIDE] for dj in range(K)]
            g.tensor_tensor(rs_a, c[0], c[1], ALU.add).then_inc(step, 1)
            g.tensor_tensor(rs_b, c[2], c[3], ALU.add).then_inc(step, 1)
            pool.wait_ge(step, 2)
            g.tensor_tensor(rs_a, rs_a, rs_b, ALU.add).then_inc(step, 1)
            pool.wait_ge(step, 3)
            r = [rs_a[:, di:di + STRIDE * (SIDE - 1) + 1:STRIDE, :] for di in range(K)]
            sums, rb = box[:, 0:IMG].rearrange("p (i j) -> p i j", i=SIDE), rs_b[:, 0:SIDE, :]
            g.memset(box[:, IMG:4 * SW], 0.0).then_inc(step, 1)
            g.tensor_tensor(sums, r[0], r[1], ALU.add).then_inc(step, 1)
            g.tensor_tensor(rb, r[2], r[3], ALU.add).then_inc(step, 1)
            pool.wait_ge(step, 6)
            g.tensor_tensor(sums, sums, rb, ALU.add).then_inc(step, 1)
            pool.wait_ge(step, 7)

        N_LOADS, SETUP = [0], [0]
        with nc.Block() as setup:
            @setup.sync
            def _(sp):
                loads = [
                    (vc_v[:], vc), (w1a[:], tW1[0:D, :]),
                    (tb1_s[:], tb1.rearrange("(c p) -> p c", p=128)),
                    (tw2_s[:], tW2.rearrange("(c p) d -> p c d", p=128)),
                    (tb2_s[:], tb2.rearrange("(o d) -> o d", o=1)),
                    (wqkv[:], w_qkv), (wout[:], w_out.rearrange("(c p) d -> p c d", p=128)),
                    (wxx[:, 0:U], Wx), (wxx[:, U:2 * U], Wx), (wt[:], Wt),
                    (bt2[0:U, :], bt.rearrange("(u o) -> u o", o=1)), (bt2[U:2 * U, :], bt.rearrange("(u o) -> u o", o=1)),
                    (wa2[0:U, :], Wa), (wa2[U:2 * U, :], Wa),
                    (ba_s[:], ba.rearrange("(o p) -> o p", o=1).broadcast_to([128, 1])),
                    (wr[0][:], Wr), (br_s[0][:], br.rearrange("(o e) -> o e", o=1)),
                    (wr[1][:], Wg), (br_s[1][:], bg.rearrange("(o e) -> o e", o=1)),
                    (w1[:], W1.rearrange("e d f -> d e f")),
                    (b1_s[:].rearrange("p e c -> p (e c)"), b1.rearrange("e (c p) -> p (e c)", p=128)),
                    (b2_s[:], b2),
                ]
                loads += [(w2[:, e], W2[e].rearrange("(c p) d -> p c d", p=128)) for e in range(E)]
                sp.dma_start(xb[:], x[0].rearrange("c i j -> c (i j)")).then_inc(x0_in, 16)
                for dst, src in loads:
                    sp.dma_start(dst, src, allow_slow_non_contiguous=True).then_inc(loaded, 16)
                sp.wait_ge(zeroed, 1)
                for dj in range(K):
                    sp.dma_start(w1b[32 * dj:32 * dj + K, :], tW1[D + dj:D + K * K:K, :]).then_inc(loaded, 16)
                N_LOADS[0] = 16 * (len(loads) + K)
                sp.wait_ge(loaded, N_LOADS[0])
                sp.wait_ge(x0_in, 16)

            @setup.gpsimd
            def _(pool):
                g = nc.gpsimd
                n = [0]

                def done(ins):
                    ins.then_inc(setup_done, 1)
                    n[0] += 1
                    return n[0]

                g.memset(w1b[:], 0.0).then_inc(zeroed, 1)
                done(g.memset(ident[:], 0.0))
                done(g.memset(sel[:], 0.0))
                done(g.memset(before[:], 1.0))
                done(g.memset(valid[:], 1.0))
                done(g.memset(ones[:], 1.0))
                done(g.memset(neg_half[:], -0.5))
                for i in range(2):
                    done(g.memset(xn[i][:, :, D:D + 1], 1.0))
                done(g.memset(ex[:], 0.0))
                done(g.memset(wasel[:], 0.0))
                done(g.iota(iota_v[:], [[1, VC]], base=0, channel_multiplier=0, allow_small_or_imprecise_dtypes=True))
                k = done(g.iota(iota_e[:], [[1, E]], base=0, channel_multiplier=0, allow_small_or_imprecise_dtypes=True))
                pool.wait_ge(setup_done, k)
                done(g.affine_select(out=ident[:], in_=ident[:], compare_op=ALU.not_equal, fill=1.0, base=0,
                                     pattern=[[-1, 128]], channel_multiplier=1))
                done(g.affine_select(out=sel[:], in_=sel[:], compare_op=ALU.not_equal, fill=1.0, base=0,
                                     pattern=[[1, K], [-1, 32]], channel_multiplier=0))
                done(g.affine_select(out=before[:], in_=before[:], compare_op=ALU.is_gt, fill=0.0, base=0,
                                     pattern=[[1, TW]], channel_multiplier=-1))
                done(g.affine_select(out=valid[:], in_=valid[:], compare_op=ALU.is_gt, fill=0.0, base=N,
                                     pattern=[[-TW, NT]], channel_multiplier=-1))
                SETUP[0] = n[0]
                pool.wait_ge(setup_done, SETUP[0])
                pool.wait_ge(x0_in, 16)
                box_sums(pool, box0_step)

            @setup.tensor
            def _(pe):
                pe.wait_ge(loaded, N_LOADS[0])
                pe.wait_ge(setup_done, SETUP[0])
                nc.tensor.transpose(ps[0][0:D, 0, 0:VC], vc_v[:], ident[0:VC, 0:VC]).then_inc(vcT_full, 1)

            @setup.vector
            def _(dve):
                V = nc.vector
                dve.wait_ge(loaded, N_LOADS[0])
                dve.wait_ge(setup_done, SETUP[0])
                for s in range(2):
                    flat = wasel[U * s:U * s + U].rearrange("p m j -> p (m j)")
                    V.tensor_copy(flat[:, M * s:M * s + 33 * (M - 1) + 1:33],
                                  wa2[U * s:U * s + U, :].broadcast_to([U, M])).then_inc(tables_ready, 1)
                dve.wait_ge(vcT_full, 1)
                V.tensor_copy(vcT[:], ps[0][0:D, 0, 0:VC]).then_inc(tables_ready, 1)
                dve.wait_ge(tables_ready, 3)

        def batch(stages, bx, by, x_next):
            pair, nth = psum_plan(stages)
            front, back = ("score",) in stages, ("take",) in stages

            def P(key):
                return ps[pair[key]]

            def FULL(key):
                return full[pair[key]]

            def READ(key):
                return read[pair[key]]

            def wait_full(eng, key):
                eng.wait_ge(full[pair[key]], nth[key][1] + 1)

            def wait_free(eng, key):
                if nth[key][0] > 0:
                    eng.wait_ge(read[pair[key]], nth[key][0])

            def wait_read(eng, key):
                eng.wait_ge(read[pair[key]], nth[key][0] + 1)

            def run(per_stage):
                for stage in stages:
                    if stage[0] in per_stage:
                        per_stage[stage[0]](*stage[1:])

            def unit(n):
                return n // (2 * NT), n // 2 % NT, n % 2

            def halves(dst):
                return dst.rearrange("p (c n) -> p c n", c=2)

            with nc.Block() as block:
                @block.sync
                def _(sp):
                    if front:
                        sp.wait_ge(pad_zero, 1)
                        sp.dma_start(h[0][IMG_LAST:LAST, NT - 1, :],
                                     txt[bass.ds(bx, 1)].rearrange("o t d -> (o t) d")).then_inc(txt_in, 16)
                        sp.wait_ge(prod_ready, K)
                        sp.dma_start(xb[:], x[bass.ds(x_next, 1)].rearrange("o c i j -> (o c) (i j)")).then_inc(x_in, 16)
                        wait_read(sp, "ntT")
                        sp.dma_start(qa[DH:DH + 1, :, :].rearrange("o h (t i) -> o (h t) i", t=NT), ntT[:]).then_inc(thr_in, 16)
                    if back:
                        wait_read(sp, "v1")
                        ob = out[bass.ds(by, 1)].rearrange("o t d -> (o t) d")
                        sp.dma_start(ob[0:4 * TW, :].rearrange("(t p) d -> p t d", p=TW), h[1][:, 0:4, :]).then_inc(out_written, 16)
                        sp.dma_start(ob[4 * TW:N, :], h[1][0:LAST, 4, :]).then_inc(out_written, 16)
                        sp.wait_ge(xs_ready, NT)
                        sp.dma_start(x_rows[bass.ds(by, 1)].rearrange("o p (t d) -> (o p) t d", t=NT), xn[1][:, :, 0:D]).then_inc(out_written, 16)
                        sp.wait_ge(out_written, 48)
                    if front:
                        sp.wait_ge(x_in, 16)

                @block.gpsimd
                def _(pool):
                    g = nc.gpsimd

                    def take():
                        g.tensor_copy(h[1][:], h[0][:]).then_inc(h_taken, 1)
                        pool.wait_ge(h_taken, 1)

                    def box_next():
                        pool.wait_ge(x_in, 16)
                        wait_full(pool, ("st", HEADS * NT - 1))
                        box_sums(pool, box_step)

                    def score():
                        g.memset(h[0][96:TW, NT - 1, :], 0.0).then_inc(pad_zero, 1)
                        pool.wait_ge(pad_zero, 1)

                    def pick():
                        wait_full(pool, "score")
                        g.memset(ka[DH:DH + 1, :, :], 1.0).then_inc(ones_row, 1)
                        pool.wait_ge(ones_row, 1)

                    def norm(i):
                        s = i // 2
                        pool.wait_ge(var_ready[i], 1)
                        g.tensor_tensor(rstd[s][:], vare[s][:], neg_half[:], ALU.pow).then_inc(rstd_ready[i], 1)
                        pool.wait_ge(rstd_ready[i], 1)

                    run(dict(take=take, score=score, pick=pick, norm=norm, box=box_next))

                @block.tensor
                def _(pe):
                    mm, tr = nc.tensor.matmul, nc.tensor.transpose

                    def score():
                        wait_free(pe, "score")
                        for t in range(4):
                            last = mm(P("score")[0:SW, 0, VC * t:VC * t + VC], box[:, SW * t:SW * t + SW], vcT[:], start=True, stop=True)
                        last.then_inc(FULL("score"), 1)

                    def pick():
                        pe.wait_ge(oh_ready, 1)
                        wait_free(pe, "ohT")
                        for t in range(4):
                            last = tr(P("ohT")[0:VC, 0, SW * t:SW * t + SW], oh[:, t, :], ident[0:SW, 0:SW])
                        last.then_inc(FULL("ohT"), 1)
                        wait_read(pe, "ohT")
                        wait_free(pe, "vsel")
                        mm(P("vsel")[:, 0, 0:IMG], vc_v[:], ohT[:, 0:IMG], start=True, stop=True).then_inc(FULL("vsel"), 1)

                    def sims():
                        wait_free(pe, "simmax")
                        for di in range(K):
                            pe.wait_ge(prod_ready, di + 1)
                            for dj in range(K):
                                last = mm(P("simmax")[32 * dj:32 * dj + 32, 0, 0:IMG], sel[:, di, :],
                                          prod[:, di % 2, dj * IMG:(dj + 1) * IMG], start=di == 0, stop=di == K - 1,
                                          skip_group_check=True)
                            last.then_inc(prod_used if di < K - 1 else FULL("simmax"), 1)

                    def mlp():
                        wait_read(pe, "simmax")
                        for c in range(HC):
                            key = ("h1", c)
                            wait_free(pe, key)
                            mm(P(key)[:, 0, 0:IMG], w1a[:, 128 * c:128 * c + 128], vT, start=True, stop=False)
                            mm(P(key)[:, 0, 0:IMG], w1b[:, 128 * c:128 * c + 128], simT, start=False, stop=True).then_inc(FULL(key), 1)
                        pe.wait_ge(h1_ready, 1)
                        wait_free(pe, "tok")
                        for t in range(NT):
                            w = TW if t < 4 else IMG_LAST
                            o = P("tok")[0:w, t // 4, 128 * (t % 4):128 * (t % 4) + 128]
                            for c in range(HC):
                                mm(o, h1T[:, c, TW * t:TW * t + w], tw2_s[:, c, :], start=c == 0, stop=False)
                            last = mm(o, ones[0:1, 0:w], tb2_s[:], start=False, stop=True)
                        last.then_inc(FULL("tok"), 1)

                    def norm(i):
                        key = ("xnT", i)
                        wait_free(pe, key)
                        for t in range(NT):
                            pe.wait_ge(xn_ready[i], t + 1)
                            last = tr(P(key)[:, t // 4, TW * (t % 4):TW * (t % 4) + TW], xn[i // 2][:, t, 0:D], ident[0:TW, 0:TW])
                        last.then_inc(FULL(key), 1)

                    def project(key, w, s):
                        wait_free(pe, key)
                        for c in range(2):
                            last = mm(P(key)[:, c, 0:TH], w, xnT[s][:, TH * c:TH * c + TH], start=True, stop=True)
                        last.then_inc(FULL(key), 1)

                    def qk(p):
                        if p == 0:
                            wait_read(pe, ("xnT", 0))
                        project(("q", p), wqkv[:, 128 * p:128 * p + 128], 0)
                        project(("k", p), wqkv[:, 512 + 128 * p:512 + 128 * p + 128], 0)

                    def raw_scores(o, hd, t):
                        for c in range(2):
                            last = mm(o[0:TW, c, 0:HALF], qa[0:DH, hd, TW * t:TW * t + TW],
                                      ka[0:DH, hd, HALF * c:HALF * c + HALF], start=True, stop=True)
                        return last

                    def scores(hp):
                        for hh in range(2):
                            for t in range(NT):
                                key = ("s", 2 * hp + hh, t)
                                wait_free(pe, key)
                                raw_scores(P(key), 2 * hp + hh, t).then_inc(FULL(key), 1)

                    def means():
                        for p in range(PAIRS):
                            wait_read(pe, ("q", p))
                            wait_read(pe, ("k", p))
                        wait_free(pe, "means")
                        for hd in range(HEADS):
                            for t in range(NT):
                                n = hd * NT + t
                                last = mm(P("means")[0:TW, 0, n:n + 1], qa[0:DH, hd, TW * t:TW * t + TW], ksum[:, hd:hd + 1],
                                          start=True, stop=True)
                        last.then_inc(FULL("means"), 1)

                    def check():
                        pe.wait_ge(worst_ready, 1)
                        wait_free(pe, "residue")
                        tr(P("residue")[0:1, 0, 0:TW], worst[:], ident[0:TW, 0:TW]).then_inc(FULL("residue"), 1)

                    def more():
                        pe.wait_ge(flag_ready, 1)
                        go = pe.value_load(unsettled[0:1, 0:1], min_val=0, max_val=1)
                        wait_free(pe, ("av", 0))
                        with pe.If(go > 0):
                            for hd in range(HEADS):
                                for t in range(NT):
                                    n = hd * NT + t
                                    if n > 0:
                                        pe.wait_ge(more_z, n)
                                    raw_scores(ps[AV], hd, t).then_inc(more_full, 1)
                            pe.wait_ge(more_ntau, HEADS * (MORE_STEPS + 1))

                    def rows():
                        pe.wait_ge(ntau_ready, 1)
                        wait_free(pe, "ntT")
                        tr(P("ntT")[0:HEADS * NT, 0, 0:TW], ntau[:].rearrange("p h t -> p (h t)"), ident[0:TW, 0:TW]).then_inc(FULL("ntT"), 1)
                        for t in range(NT):
                            key = ("v", t)
                            wait_free(pe, key)
                            mm(P(key)[0:TW, 0, :], xnT[0][:, TW * t:TW * t + TW], wqkv[:, 1024:1536], start=True, stop=True).then_inc(FULL(key), 1)

                    def weigh(n):
                        if n == 0:
                            pe.wait_ge(thr_in, 16)
                            pe.wait_ge(ones_row, 1)
                            wait_read(pe, ("v", NT - 1))
                        if n < HEADS * NT:
                            p, jt, hh = unit(n)
                            hd, key = 2 * p + hh, ("st", n)
                            wait_free(pe, key)
                            for c in range(2):
                                last = mm(P(key)[0:TW, c, 0:HALF], ka[:, hd, TW * jt:TW * jt + TW],
                                          qa[:, hd, HALF * c:HALF * c + HALF], start=True, stop=True)
                            last.then_inc(FULL(key), 1)
                        if n >= 2:
                            p, jt, hh = unit(n - 2)
                            if jt == 0 and hh == 0:
                                wait_free(pe, ("av", p))
                            pe.wait_ge(pt_ready, n - 1)
                            hd = 2 * p + hh
                            for c in range(2):
                                last = mm(P(("av", p))[64 * hh:64 * hh + 64, c, 0:HALF], v[:, jt, DH * hd:DH * hd + DH],
                                          R[:, (n - 2) % NT, HALF * c:HALF * c + HALF], start=jt == 0, stop=jt == NT - 1,
                                          skip_group_check=True)
                            last.then_inc(pt_used, 1)

                    def o():
                        for p in range(PAIRS):
                            wait_read(pe, ("av", p))
                        wait_free(pe, "o")
                        for t in range(NT):
                            for p in range(PAIRS):
                                last = mm(P("o")[0:TW, t // 4, 128 * (t % 4):128 * (t % 4) + 128], oT[:, p, TW * t:TW * t + TW],
                                          wout[:, p, :], start=p == 0, stop=p == PAIRS - 1)
                        last.then_inc(FULL("o"), 1)

                    def gate(f):
                        key = ("lg", f)
                        wait_read(pe, ("xnT", 2 * f + 1))
                        wait_free(pe, key)
                        for t in range(NT):
                            o_ = P(key)[0:TW, 0, E * t:E * t + E]
                            mm(o_, xnT[f][:, TW * t:TW * t + TW], wr[f][:], start=True, stop=False)
                            last = mm(o_, ones[0:1, 0:TW], br_s[f][:], start=False, stop=True)
                        last.then_inc(FULL(key), 1)
                        if f == 0:
                            pe.wait_ge(cw_ready, 1)
                            wait_free(pe, "cwT")
                            for t in range(NT):
                                last = tr(P("cwT")[0:E, t // 4, TW * (t % 4):TW * (t % 4) + TW], cw[:, t, :], ident[0:TW, 0:TW])
                            last.then_inc(FULL("cwT"), 1)
                            wait_read(pe, "cwT")
                            wait_free(pe, "b2")
                            for t in range(NT):
                                last = mm(P("b2")[0:TW, t // 4, 128 * (t % 4):128 * (t % 4) + 128],
                                          cwT[:, TW * t:TW * t + TW], b2_s[:], start=True, stop=True)
                            last.then_inc(FULL("b2"), 1)

                    def up(e):
                        for c in range(FC):
                            project(("hid", e, c), w1[:, e, 128 * c:128 * c + 128], 0)

                    def y(e):
                        key = ("y", e)
                        wait_free(pe, key)
                        for c in range(FC):
                            wait_read(pe, ("hid", e, c))
                        for t in range(NT):
                            for c in range(FC):
                                last = mm(P(key)[0:TW, t // 4, 128 * (t % 4):128 * (t % 4) + 128],
                                          hid[:, e % 2, T * c + TW * t:T * c + TW * t + TW], w2[:, e, c, :],
                                          start=c == 0, stop=c == FC - 1)
                        last.then_inc(FULL(key), 1)

                    def k2q2():
                        wait_read(pe, ("xnT", 2))
                        project("k2", wxx[:], 1)
                        wait_free(pe, "q2")
                        for c in range(2):
                            last = mm(P("q2")[U * c:U * c + U, 0, 0:TH], wt[:], xnT[1][:, TH * c:TH * c + TH], start=True, stop=True,
                                      skip_group_check=True)
                        last.then_inc(FULL("q2"), 1)

                    def quad(n):
                        G, m = n // M, n % M
                        if m == 0:
                            wait_free(pe, ("logits", G))
                        pe.wait_ge(th_ready, n + 1)
                        for c in range(2):
                            for g in range(4):
                                last = mm(ps[LOGITS][32 * g:32 * g + 32, c, 0:HALF], wasel[:, m, :],
                                          th[:, n % TH_RING, N * g + HALF * c:N * g + HALF * c + HALF],
                                          start=m == 0, stop=m == M - 1, skip_group_check=True)
                        last.then_inc(th_used, 1)

                    def turn(G):
                        key = ("turned", G)
                        wait_read(pe, ("logits", G))
                        wait_free(pe, key)
                        for jt in range(NT):
                            last = tr(P(key)[0:TW, jt // 4, 128 * (jt % 4):128 * (jt % 4) + 128], ex[:, G % 2, TW * jt:TW * jt + TW], ident[:])
                        last.then_inc(FULL(key), 1)

                    def v1():
                        wait_read(pe, ("turned", GROUPS - 1))
                        wait_free(pe, "v1")
                        for t in range(NT):
                            for jt in range(NT):
                                last = mm(P("v1")[0:TW, t // 3, (D + 1) * (t % 3):(D + 1) * (t % 3) + D + 1],
                                          ET[:, jt, TW * t:TW * t + TW], xn[1][:, jt, :], start=jt == 0, stop=jt == NT - 1)
                        last.then_inc(FULL("v1"), 1)

                    run(dict(score=score, pick=pick, sims=sims, mlp=mlp, norm=norm, qk=qk, means=means, scores=scores, check=check,
                             more=more, rows=rows, weigh=weigh, o=o, gate=gate, up=up, y=y, k2q2=k2q2, quad=quad, turn=turn, v1=v1))

                @block.scalar
                def _(act):
                    A = nc.scalar.activation

                    def mlp():
                        wait_full(act, "tok")
                        act.wait_ge(pad_zero, 1)
                        A(h[0][:, 0:4, :].rearrange("p t d -> p (t d)"), P("tok")[0:TW, 0, :], ACT.Tanh)
                        A(h[0][0:IMG_LAST, 4, :], P("tok")[0:IMG_LAST, 1, 0:D], ACT.Tanh).then_inc(READ("tok"), 1)

                    def qk(p):
                        key = ("k", p)
                        wait_full(act, key)
                        for hh in range(2):
                            last = A(halves(ka[0:DH, 2 * p + hh, :]), P(key)[DH * hh:DH * hh + DH, :, 0:TH], ACT.Identity,
                                     accum_out=ksum[:, 2 * p + hh:2 * p + hh + 1])
                        last.then_inc(READ(key), 1)

                    def scores(hp):
                        if hp == 0:
                            wait_read(act, "means")
                        for hh in range(2):
                            hd = 2 * hp + hh
                            for t in range(NT):
                                key = ("s", hd, t)
                                wait_full(act, key)
                                if hp > 0:
                                    act.wait_ge(relu_ready, hp * 2 * NT * (STEPS - 1))
                                A(halves(Z[:, NT * hh + t, :]), P(key)[0:TW, :, 0:HALF], ACT.Relu, bias=ntau[:, hd, t:t + 1],
                                  accum_out=s1[:, hd, t:t + 1]).then_inc(READ(key), 1)

                    def step(hp, k):
                        for hh in range(2):
                            hd = 2 * hp + hh
                            act.wait_ge(rise_ready, (hp * STEPS + k - 1) * 2 + hh + 1)
                            for t in range(NT):
                                n = ((hp * STEPS + k) * 2 + hh) * NT + t
                                act.wait_ge(square_ready, n - NT + 1)
                                A(R[:, t, :], Z[:, NT * hh + t, :], ACT.Relu, bias=rise[:, hd, t:t + 1],
                                  accum_out=s1[:, hd, t:t + 1]).then_inc(relu_ready, 1)

                    def more():
                        act.wait_ge(flag_ready, 1)
                        go = act.value_load(unsettled[0:1, 0:1], min_val=0, max_val=1)
                        with act.If(go > 0):
                            act.wait_ge(relu_ready, HEADS * NT * (STEPS - 1))
                            act.wait_ge(square_ready, HEADS * NT * STEPS)
                            for hd in range(HEADS):
                                for t in range(NT):
                                    act.wait_ge(more_full, hd * NT + t + 1)
                                    if hd > 0:
                                        act.wait_ge(more_relu, hd * NT * MORE_STEPS)
                                    A(halves(Z[:, t, :]), ps[AV][0:TW, :, 0:HALF], ACT.Copy).then_inc(more_z, 1)
                                act.wait_ge(more_z, (hd + 1) * NT)
                                for k in range(MORE_STEPS):
                                    act.wait_ge(more_ntau, hd * (MORE_STEPS + 1) + k + 1)
                                    for t in range(NT):
                                        A(R[:, t, :], Z[:, t, :], ACT.Relu, bias=ntau[:, hd, t:t + 1],
                                          accum_out=s1[:, hd, t:t + 1]).then_inc(more_relu, 1)
                            act.wait_ge(more_ntau, HEADS * (MORE_STEPS + 1))

                    def rows():
                        wait_full(act, "ntT")
                        A(ntT[:], P("ntT")[0:HEADS * NT, 0, 0:TW], ACT.Copy).then_inc(READ("ntT"), 1)

                    def weigh(n):
                        if n < HEADS * NT:
                            key = ("st", n)
                            wait_full(act, key)
                            if n >= NT:
                                act.wait_ge(pt_used, n - NT + 1)
                            A(halves(R[:, n % NT, :]), P(key)[0:TW, :, 0:HALF], ACT.Relu).then_inc(READ(key), 1)
                        p = (n - 2) // (2 * NT)
                        if n > 2 and n - 2 == 2 * NT * (p + 1) - 1:
                            act.wait_ge(pt_used, 2 * NT * (p + 1))
                            A(halves(oT[:, p, 0:N]), P(("av", p))[:, :, 0:HALF], ACT.Copy).then_inc(READ(("av", p)), 1)

                    def gate(f):
                        act.wait_ge(lg_ready[f], 1)
                        A(pr[f][:], lg[f][:], ACT.Exp).then_inc(exp_ready[f], 1)

                    def tanh(n):
                        G, m = n // M, n % M
                        if n == 0:
                            wait_read(act, "k2")
                            wait_read(act, "q2")
                        if n >= TH_RING:
                            act.wait_ge(th_used, n - TH_RING + 1)
                        for g in range(4):
                            i = 4 * M * G + M * g + m
                            last = A(th[:, n % TH_RING, N * g:N * g + N], K2[:, 0:N], ACT.Tanh, bias=Q2[:, i:i + 1])
                        last.then_inc(th_ready, 1)

                    def exp(G):
                        key = ("logits", G)
                        act.wait_ge(th_used, M * (G + 1))
                        if G >= 2:
                            wait_full(act, ("turned", G - 2))
                        A(halves(ex[:, G % 2, 0:N]), ps[LOGITS][:, :, 0:HALF], ACT.Exp, bias=ba_s[:]).then_inc(READ(key), 1)

                    run(dict(mlp=mlp, qk=qk, scores=scores, step=step, more=more, rows=rows, weigh=weigh, gate=gate, tanh=tanh, exp=exp))

                @block.vector
                def _(dve):
                    V = nc.vector
                    links, more_links = [0], [0]

                    def raised(ins):
                        links[0] += 1
                        ins.then_inc(dve_link, 1)

                    def link(ins):
                        raised(ins)
                        dve.wait_ge(dve_link, links[0])

                    def link_more(ins):
                        more_links[0] += 1
                        ins.then_inc(more_link, 1)
                        dve.wait_ge(more_link, more_links[0])

                    def wide(ap):
                        return ap.unsqueeze(2).broadcast_to([TW, NT, E])

                    def score():
                        wait_full(dve, "score")
                        for t in range(4):
                            last = V.max(tmx8[:, t, :], P("score")[0:SW, 0, VC * t:VC * t + VC])
                        link(last)
                        for t in range(4):
                            last = V.max_index(tidx8[:, t, :], tmx8[:, t, :], P("score")[0:SW, 0, VC * t:VC * t + VC])
                        last.then_inc(READ("score"), 1)
                        wait_read(dve, "score")
                        link(V.tensor_copy(tidxf[:], tidx8[:, :, 0]))
                        for t in range(4):
                            last = V.tensor_scalar(oh[:, t, :], iota_v[:], tidxf[:, t:t + 1], None, ALU.is_equal)
                        last.then_inc(oh_ready, 1)

                    def pick():
                        wait_full(dve, "ohT")
                        V.tensor_copy(ohT[:], P("ohT")[0:VC, 0, 0:4 * SW]).then_inc(READ("ohT"), 1)
                        wait_full(dve, "vsel")
                        V.tensor_copy(vT, P("vsel")[:, 0, 0:IMG]).then_inc(READ("vsel"), 1)

                    def sims():
                        wait_read(dve, "vsel")
                        for di in range(K):
                            if di >= 2:
                                dve.wait_ge(prod_used, di - 1)
                            whole = xb[:]
                            patch = bass.AP(whole.tensor, whole.offset + RES * di,
                                            [list(whole.ap[0]), [1, K], [STRIDE * RES, SIDE], [STRIDE, SIDE]])
                            word = bass.AP(vT.tensor, vT.offset, [list(vT.ap[0]), [0, K], [SIDE, SIDE], [1, SIDE]])
                            V.tensor_tensor(prod[:, di % 2, :].rearrange("p (k i j) -> p k i j", k=K, i=SIDE), word, patch,
                                            ALU.mult).then_inc(prod_ready, 1)
                        wait_full(dve, "simmax")
                        V.tensor_copy(simT, P("simmax")[:, 0, 0:IMG]).then_inc(READ("simmax"), 1)

                    def mlp():
                        for c in range(HC):
                            key = ("h1", c)
                            wait_full(dve, key)
                            V.tensor_scalar(h1T[:, c, :], P(key)[:, 0, 0:IMG], tb1_s[:, c:c + 1], None, ALU.add).then_inc(READ(key), 1)
                        for c in range(HC):
                            wait_read(dve, ("h1", c))
                        V.scalar_tensor_tensor(h1T[:], h1T[:], 0.2, h1T[:], ALU.mult, ALU.max).then_inc(h1_ready, 1)

                    def norm(i):
                        s = i // 2
                        if i == 0:
                            wait_read(dve, "tok")
                            dve.wait_ge(txt_in, 16)
                        if i == 2:
                            dve.wait_ge(h_taken, 1)
                        for t in range(NT):
                            last = V.bn_stats(stats[s][:, t, :], h[s][:, t, :])
                        link(last)
                        for t in range(NT):
                            last = V.bn_aggr(mv[s][:, t, :], stats[s][:, t, :])
                        link(last)
                        V.tensor_scalar(vare[s][:], mv[s][:, :, 1], EPS, None, ALU.add).then_inc(var_ready[i], 1)
                        dve.wait_ge(rstd_ready[i], 1)
                        for t in range(NT):
                            V.tensor_scalar(xn[s][:, t, 0:D], h[s][:, t, :], mv[s][:, t, 0:1], rstd[s][:, t:t + 1],
                                            ALU.subtract, ALU.mult).then_inc(xn_ready[i], 1)
                        key = ("xnT", i)
                        wait_full(dve, key)
                        V.tensor_copy(xnT[s][:, 0:4 * TW], P(key)[:, 0, 0:4 * TW])
                        V.tensor_copy(xnT[s][:, 4 * TW:T], P(key)[:, 1, 0:TW]).then_inc(READ(key), 1)

                    def qk(p):
                        key = ("q", p)
                        wait_full(dve, key)
                        for hh in range(2):
                            last = V.tensor_scalar(halves(qa[0:DH, 2 * p + hh, :]), P(key)[DH * hh:DH * hh + DH, :, 0:TH],
                                                   DH ** -0.5 / 2, None, ALU.mult)
                        last.then_inc(READ(key), 1)

                    def means():
                        wait_full(dve, "means")
                        V.tensor_scalar(ntau[:].rearrange("p h t -> p (h t)"), P("means")[0:TW, 0, 0:HEADS * NT], -1.0 / N,
                                        1.0 / sqrt(N), ALU.mult, ALU.add).then_inc(READ("means"), 1)

                    def squares(src, t, hd):
                        return V.scalar_tensor_tensor(R[:, t, :], src, 1.0, src, ALU.mult, ALU.mult, accum_out=s2[:, hd, t:t + 1])

                    def newton(hd, link, dst, first):
                        link(V.tensor_scalar(sa[:], s2[:, hd, :], 3.0, 1.0, ALU.mult, ALU.add))
                        link(V.tensor_tensor(sa[:], sa[:], s1[:, hd, :], ALU.mult))
                        link(V.reciprocal(sa[:], sa[:]))
                        link(V.scalar_tensor_tensor(sc[:], s2[:, hd, :], -1.0, s2[:, hd, :], ALU.add, ALU.mult))
                        if first:
                            return V.scalar_tensor_tensor(dst, sc[:], -2.0, sa[:], ALU.mult, ALU.mult)
                        link(V.scalar_tensor_tensor(sc[:], sc[:], -2.0, sa[:], ALU.mult, ALU.mult))
                        return V.tensor_tensor(dst, dst, sc[:], ALU.add)

                    def scores(hp):
                        step(hp, 0)

                    def step(hp, k):
                        for hh in range(2):
                            hd = 2 * hp + hh
                            for t in range(NT):
                                n = ((hp * STEPS + k) * 2 + hh) * NT + t
                                if k == 0:
                                    wait_read(dve, ("s", hd, t))
                                    if n >= NT:
                                        dve.wait_ge(square_ready, n - NT + 1)
                                else:
                                    dve.wait_ge(relu_ready, ((hp * (STEPS - 1) + k - 1) * 2 + hh) * NT + t + 1)
                                squares(R[:, t, :] if k else Z[:, NT * hh + t, :], t, hd).then_inc(square_ready, 1)
                            dve.wait_ge(square_ready, n + 1)
                            newton(hd, link, rise[:, hd, :], k == 0).then_inc(rise_ready, 1)

                    def check():
                        dve.wait_ge(rise_ready, HEADS * STEPS)
                        V.tensor_tensor(ntau[:], ntau[:], rise[:], ALU.add).then_inc(ntau_ready, 1)
                        link(V.tensor_scalar(res[:], s2[:].rearrange("p h t -> p (h t)"), -1.0, None, ALU.add))
                        link(V.tensor_tensor(res[:], res[:], res[:], ALU.mult))
                        V.tensor_reduce(worst[:], res[:], AX_X, ALU.max).then_inc(worst_ready, 1)
                        wait_full(dve, "residue")
                        V.tensor_reduce(flag_f[:], P("residue")[0:1, 0, 0:TW], AX_X, ALU.max).then_inc(READ("residue"), 1)
                        wait_read(dve, "residue")
                        V.tensor_scalar(unsettled[:], flag_f[:], SETTLED ** 2, None, ALU.is_gt).then_inc(flag_ready, 1)

                    def more():
                        dve.wait_ge(flag_ready, 1)
                        dve.wait_ge(ntau_ready, 1)
                        go = dve.value_load(unsettled[0:1, 0:1], min_val=0, max_val=1)
                        with dve.If(go > 0):
                            for hd in range(HEADS):
                                dve.wait_ge(more_z, (hd + 1) * NT)
                                link_more(V.tensor_reduce(zmax[:], Z[:, 0:NT, :], AX_X, ALU.max))
                                link_more(V.tensor_scalar(zmax[:], zmax[:], -1.0, 1.0, ALU.mult, ALU.add))
                                V.tensor_tensor(ntau[:, hd, :], ntau[:, hd, :], zmax[:], ALU.min).then_inc(more_ntau, 1)
                                dve.wait_ge(more_ntau, hd * (MORE_STEPS + 1) + 1)
                                for k in range(MORE_STEPS):
                                    for t in range(NT):
                                        n = (hd * MORE_STEPS + k) * NT + t
                                        dve.wait_ge(more_relu, n + 1)
                                        squares(R[:, t, :], t, hd).then_inc(more_square, 1)
                                    dve.wait_ge(more_square, n + 1)
                                    newton(hd, link_more, ntau[:, hd, :], False).then_inc(more_ntau, 1)

                    def rows():
                        for t in range(NT):
                            key = ("v", t)
                            wait_full(dve, key)
                            V.tensor_copy(v[:, t, :], P(key)[0:TW, 0, :]).then_inc(READ(key), 1)

                    def weigh(n):
                        if n < HEADS * NT:
                            wait_read(dve, ("st", n))
                            V.tensor_tensor(R[:, n % NT, :], R[:, n % NT, :], R[:, n % NT, :], ALU.mult).then_inc(pt_ready, 1)

                    def add_rows(key):
                        wait_full(dve, key)
                        for c, t0, t1 in ((0, 0, 4), (1, 4, 5)):
                            d = h[0][:, t0:t1, :].rearrange("p t d -> p (t d)")
                            last = V.tensor_tensor(d, d, P(key)[0:TW, c, 0:D * (t1 - t0)], ALU.add)
                        last.then_inc(READ(key), 1)
                        wait_read(dve, key)

                    def o():
                        add_rows("o")

                    def gate(f):
                        key = ("lg", f)
                        L, m8, i8, xf, p_, dn = lg[f], mx8[f], idx8[f], idxf[f], pr[f], den[f]
                        wait_full(dve, key)
                        V.tensor_copy(L[:].rearrange("p t e -> p (t e)"), P(key)[0:TW, 0, 0:NT * E]).then_inc(READ(key), 1)
                        wait_read(dve, key)
                        for t in range(NT):
                            last = V.max(m8[:, t, :], L[:, t, :])
                        link(last)
                        V.tensor_tensor(L[:], L[:], wide(m8[:, :, 0]), ALU.subtract).then_inc(lg_ready[f], 1)
                        dve.wait_ge(exp_ready[f], 1)
                        link(V.tensor_reduce(dn[:], p_[:], AX_X, ALU.add))
                        link(V.reciprocal(dn[:], dn[:]))
                        link(V.tensor_tensor(p_[:], p_[:], wide(dn[:]), ALU.mult))
                        for t in range(NT):
                            last = V.max(m8[:, t, :], p_[:, t, :])
                        link(last)
                        for t in range(NT):
                            last = V.max_index(i8[:, t, :], m8[:, t, :], p_[:, t, :])
                        link(last)
                        link(V.tensor_copy(xf[:], i8[:, :, 0:2]))
                        experts_iota = iota_e[:].unsqueeze(1).broadcast_to([TW, NT, E])
                        if f == 0:
                            link(V.tensor_tensor(cw[:], experts_iota, wide(xf[:, :, 0]), ALU.is_equal))
                            link(V.tensor_tensor(oh2[:], experts_iota, wide(xf[:, :, 1]), ALU.is_equal))
                            link(V.tensor_tensor(cw[:], cw[:], oh2[:], ALU.add))
                            V.tensor_tensor(cw[:], cw[:], p_[:], ALU.mult).then_inc(cw_ready, 1)
                            wait_full(dve, "cwT")
                            V.tensor_copy(cwT[:, 0:4 * TW], P("cwT")[0:E, 0, 0:4 * TW])
                            V.tensor_copy(cwT[:, 4 * TW:T], P("cwT")[0:E, 1, 0:TW]).then_inc(READ("cwT"), 1)
                            dve.wait_ge(cw_ready, 1)
                            add_rows("b2")
                        else:
                            for t in range(NT):
                                V.tensor_scalar(xn[1][:, t, 0:D], xn[1][:, t, 0:D], m8[:, t, 0:1], None, ALU.mult).then_inc(xs_ready, 1)
                            link(V.tensor_tensor(p_[:], experts_iota, wide(xf[:, :, 0]), ALU.is_equal))
                            link(V.tensor_tensor(OH[:, bass.ds(by * NT, NT), :], p_[:], wide(valid[:]), ALU.mult))

                    def up(e):
                        for c in range(FC):
                            key = ("hid", e, c)
                            wait_full(dve, key)
                            V.tensor_scalar(halves(hid[:, e % 2, T * c:T * c + T]), P(key)[:, :, 0:TH], b1_s[:, e, c:c + 1],
                                            0.0, ALU.add, ALU.max).then_inc(READ(key), 1)

                    def y(e):
                        key = ("y", e)
                        wait_full(dve, key)
                        if e > 0:
                            wait_read(dve, ("y", e - 1))
                        for t in range(NT):
                            last = V.scalar_tensor_tensor(h[0][:, t, :], P(key)[0:TW, t // 4, 128 * (t % 4):128 * (t % 4) + 128],
                                                          cw[:, t, e:e + 1], h[0][:, t, :], ALU.mult, ALU.add)
                        last.then_inc(READ(key), 1)

                    def k2q2():
                        wait_full(dve, "k2")
                        V.tensor_copy(halves(K2[:]), P("k2")[:, :, 0:TH]).then_inc(READ("k2"), 1)
                        wait_full(dve, "q2")
                        V.tensor_scalar(Q2[:], P("q2")[:, 0, 0:TH], bt2[:], None, ALU.add).then_inc(READ("q2"), 1)

                    def turn(G):
                        key = ("turned", G)
                        wait_full(dve, key)
                        first = 4 * M * G
                        for s in range(2):
                            V.tensor_copy(ET[:, 0:4, TH * s + first:TH * s + first + 4 * M].rearrange("p j (g m) -> p j g m", g=4),
                                          P(key)[0:TW, 0, :].rearrange("p (j g m) -> p j g m", j=4, g=4)[:, :, :, M * s:M * s + M])
                        for s in range(2):
                            last = V.tensor_copy(ET[:, 4, TH * s + first:TH * s + first + 4 * M].rearrange("p (g m) -> p g m", g=4),
                                                 P(key)[0:TW, 1, 0:128].rearrange("p (g m) -> p g m", g=4)[:, :, M * s:M * s + M])
                        last.then_inc(READ(key), 1)

                    def v1():
                        wait_full(dve, "v1")
                        sums = P("v1")[0:TW, :, 0:3 * (D + 1)].rearrange("p c (t d) -> p c t d", d=D + 1)
                        raised(V.tensor_scalar(den[1][:, 0:3], sums[:, 0, 0:3, D], 1e-7, None, ALU.add))
                        link(V.tensor_scalar(den[1][:, 3:5], sums[:, 1, 0:2, D], 1e-7, None, ALU.add))
                        link(V.reciprocal(den[1][:], den[1][:]))
                        for t in range(NT):
                            last = V.scalar_tensor_tensor(h[1][:, t, :], sums[:, t // 3, t % 3, 0:D], den[1][:, t:t + 1],
                                                          h[1][:, t, :], ALU.mult, ALU.add)
                        last.then_inc(READ("v1"), 1)
                        wait_read(dve, "v1")

                    run(dict(score=score, pick=pick, sims=sims, mlp=mlp, norm=norm, qk=qk, means=means, scores=scores, step=step,
                             check=check, more=more, rows=rows, weigh=weigh, o=o, gate=gate, up=up, y=y, k2q2=k2q2,
                             turn=turn, v1=v1))

            nc.all_engine_barrier(sems_to_clear=batch_sems)

        batch(schedule(True, False), 0, None, 1 % B)
        if B > 1:
            with nc.Fori(0, B - 1) as b:
                batch(schedule(True, True), b + 1, b, (b + 2) % B)
        batch(schedule(False, True), None, B - 1, None)

        rows_out = out.rearrange("b t d -> (b t) d")
        whole = B * N // ROWS
        rest = B * N - whole * ROWS
        with nc.Block() as place:
            @place.sync
            def _(sp):
                sp.dma_start(xall, x_rows.rearrange("b p n -> p b n")).then_inc(xall_in, 16)
                sp.dma_start(y_sum[:, 0:whole, :], rows_out[0:whole * ROWS, :].rearrange("(t p) d -> p t d", p=ROWS)).then_inc(last_loaded, 16)
                sp.dma_start(w1[:], V1.rearrange("e d f -> d e f")).then_inc(last_loaded, 16)
                for e in range(E):
                    sp.dma_start(w2[:, e], V2[e].rearrange("(c p) d -> p c d", p=128)).then_inc(last_loaded, 16)
                sp.dma_start(c1_s.rearrange("p e f -> p (e f)"),
                             c1.rearrange("(o e) f -> o (e f)", o=1).broadcast_to([ROWS, E * FC * 128])).then_inc(last_loaded, 16)
                sp.dma_start(c2_s.rearrange("p e d -> p (e d)"),
                             c2.rearrange("(o e) d -> o (e d)", o=1).broadcast_to([ROWS, E * D])).then_inc(last_loaded, 16)
                n = E + 4
                if rest:
                    sp.wait_ge(pads_zero, 1)
                    sp.dma_start(y_sum[0:rest, whole, :], rows_out[whole * ROWS:B * N, :]).then_inc(last_loaded, 16)
                    sp.dma_start(x_sorted[B * N:SORTED * ROWS, :], ones[0:ROWS - rest, :]).then_inc(last_loaded, 16)
                    n += 2
                sp.wait_ge(last_loaded, 16 * n)

            @place.gpsimd
            def _(pool):
                g = nc.gpsimd
                if rest:
                    g.memset(y_sum[:, whole, :], 0.0).then_inc(pads_zero, 1)
                g.iota(tile_no[:], [[ROWS, SORTED]], base=0, channel_multiplier=0, allow_small_or_imprecise_dtypes=True).then_inc(iotas, 1)
                g.iota(pair_no[:], [[1, PP]], base=0, channel_multiplier=0, allow_small_or_imprecise_dtypes=True).then_inc(iotas, 1)
                g.iota(row_no[:], [[0, 1]], base=0, channel_multiplier=1, allow_small_or_imprecise_dtypes=True).then_inc(iotas, 1)
                pool.wait_ge(xall_in, 16)
                pool.wait_ge(pos_ready, 1)
                for n in range(B * NT):
                    w = TW if n % NT < NT - 1 else LAST
                    g.indirect_dma_start(out=x_sorted, out_offset=bass.IndirectOffsetOnAxis(ap=pos_u[0:w, n:n + 1], axis=0),
                                         in_=xall[0:w, n // NT, D * (n % NT):D * (n % NT) + D], in_offset=None).then_inc(scattered, 16)
                pool.wait_ge(scattered, 16 * B * NT)

            @place.tensor
            def _(pe):
                mm = nc.tensor.matmul
                W = B * NT * E // 2
                for n, w in enumerate((before[:], ones[0:TW, :])):
                    for c in range(2):
                        last = mm(ps[n][0:TW if n == 0 else 128, c, 0:W], w, OH[:].rearrange("p t e -> p (t e)")[:, W * c:W * c + W],
                                  start=True, stop=True)
                last.then_inc(place_full, 1)

            @place.vector
            def _(dve):
                V = nc.vector
                step = [0]

                def then(ins):
                    step[0] += 1
                    ins.then_inc(place_step, 1)
                    dve.wait_ge(place_step, step[0])

                tiles = B * NT
                dve.wait_ge(place_full, 1)
                W = tiles * E // 2

                def run(ap):
                    return ap.rearrange("p (c n) -> p c n", c=2)

                then(V.tensor_copy(run(inc[:, 0, :]), ps[1][:, :, 0:W]))
                cur, d = 0, 1
                while d < tiles:
                    V.tensor_copy(inc[:, 1 - cur, 0:d * E], inc[:, cur, 0:d * E])
                    then(V.tensor_tensor(inc[:, 1 - cur, d * E:], inc[:, cur, d * E:], inc[:, cur, 0:(tiles - d) * E], ALU.add))
                    cur, d = 1 - cur, 2 * d
                then(V.tensor_copy(total[:], inc[:, cur, (tiles - 1) * E:tiles * E]))

                def sums_up_to(dst, src):
                    then(V.tensor_copy(dst[:, 0:1], src[:, 0:1]))
                    for e in range(1, E):
                        then(V.tensor_tensor(dst[:, e:e + 1], dst[:, e - 1:e], src[:, e:e + 1], ALU.add))

                sums_up_to(end_row, total)
                then(V.tensor_tensor(first_row[:], end_row[:], total[:], ALU.subtract))
                s = inc[0:TW, cur, :]
                then(V.tensor_tensor(run(s), run(s), ps[1][0:TW, :, 0:W], ALU.subtract))
                then(V.tensor_tensor(run(s), run(s), ps[0][0:TW, :, 0:W], ALU.add))
                s3 = s.rearrange("p (t e) -> p t e", e=E)
                then(V.tensor_tensor(s3, s3, first_row[0:TW, :].unsqueeze(1).broadcast_to([TW, tiles, E]), ALU.add))
                then(V.tensor_tensor(s3, s3, OH[:], ALU.mult))
                then(V.tensor_reduce(pos[:], s3, AX_X, ALU.add))
                V.tensor_copy(pos_u[:], pos[:]).then_inc(pos_ready, 1)
                dve.wait_ge(iotas, 3)

                def over_tiles(ap):
                    return ap.unsqueeze(2).broadcast_to([128, E, SORTED])

                def over_pairs(ap):
                    return ap.unsqueeze(2).broadcast_to([128, E, PP])

                starts = tile_no[:].unsqueeze(1).broadcast_to([128, E, SORTED])
                then(V.tensor_tensor(over[:], starts, over_tiles(end_row[:]), ALU.is_lt))
                then(V.tensor_reduce(end_tile[:], over[:], AX_X, ALU.add))
                then(V.tensor_tensor(over[:], starts, over_tiles(first_row[:]), ALU.is_le))
                then(V.tensor_reduce(first_tile[:], over[:], AX_X, ALU.add))
                then(V.tensor_scalar(first_tile[:], first_tile[:], -1.0, None, ALU.add))
                then(V.tensor_tensor(end_tile[:], end_tile[:], first_tile[:], ALU.subtract))
                then(V.tensor_scalar(total[:], total[:], 1.0, None, ALU.min))
                then(V.tensor_tensor(total[:], total[:], end_tile[:], ALU.mult))
                sums_up_to(pair_end, total)
                then(V.tensor_tensor(shift[:], total[:], pair_end[:], ALU.subtract))
                then(V.tensor_tensor(shift[:], shift[:], first_tile[:], ALU.add))
                numbers = pair_no[:].unsqueeze(1).broadcast_to([128, E, PP])
                then(V.tensor_tensor(gt[:], numbers, over_pairs(pair_end[:]), ALU.is_ge))
                then(V.tensor_scalar(own[:, 0, :], gt[:, 0, :], -1.0, 1.0, ALU.mult, ALU.add))
                then(V.tensor_tensor(own[:, 1:E, :], gt[:, 0:E - 1, :], gt[:, 1:E, :], ALU.subtract))

                def of_pair(dst, values):
                    then(V.tensor_tensor(part[:], own[:], over_pairs(values[:]), ALU.mult))
                    then(V.tensor_reduce(dst[:], part[:].rearrange("p e n -> p n e"), AX_X, ALU.add))

                of_pair(pair_t, shift)
                of_pair(pair_lo, first_row)
                of_pair(pair_hi, end_row)
                then(V.tensor_reduce(pair_e[:], gt[:].rearrange("p e n -> p n e"), AX_X, ALU.add))
                then(V.tensor_tensor(pair_t[:], pair_t[:], pair_no[:], ALU.add))
                then(V.tensor_scalar(pair_e[:], pair_e[:], E - 1.0, None, ALU.min))
                then(V.tensor_scalar(pair_t[:], pair_t[:], SORTED - 1.0, None, ALU.min))
                then(V.tensor_copy(e_tab[:], pair_e[:]))
                then(V.tensor_copy(t_tab[:], pair_t[:]))
                then(V.tensor_scalar(pair_t[:], pair_t[:], float(ROWS), row_no[:], ALU.mult, ALU.add))
                then(V.tensor_tensor(mask[:], pair_t[:], pair_lo[:], ALU.is_ge))
                then(V.tensor_tensor(pair_hi[:], pair_t[:], pair_hi[:], ALU.is_lt))
                V.tensor_tensor(mask[:], mask[:], pair_hi[:], ALU.mult).then_inc(tables_made, 1)
                dve.wait_ge(tables_made, 1)

        nc.all_engine_barrier()
        with nc.Fori(0, PASSES) as q:
            with nc.Block() as block:
                @block.sync
                def _(sp):
                    sp.wait_ge(now_ready, 3)
                    for i in range(PER_PASS):
                        t = sp.value_load(t_now[0:1, i:i + 1], min_val=0, max_val=SORTED - 1)
                        if i >= XT_RING:
                            sp.wait_ge(xt_full, i - XT_RING + 1)
                        sp.dma_start(xt[:, i % XT_RING, :], x_sorted[bass.ds(t * ROWS, ROWS), :]).then_inc(xt_in[i % XT_RING], 16)

                @block.tensor
                def _(pe):
                    mm, tr = nc.tensor.matmul, nc.tensor.transpose
                    pe.wait_ge(now_ready, 3)
                    w1f, w2f = w1[:].rearrange("d e f -> d (e f)"), w2[:].rearrange("p e c d -> p (e c d)")
                    for i in range(PER_PASS + 1):
                        if i < PER_PASS:
                            pe.wait_ge(xt_in[i % XT_RING], 16 * (i // XT_RING + 1))
                            if i > 1:
                                pe.wait_ge(xtT_ready, i - 1)
                            tr(ps[2][:, i % 2, 0:ROWS], xt[:, i % XT_RING, :], ident[:]).then_inc(xt_full, 1)
                            e = pe.value_load(e_now[0:1, i:i + 1], min_val=0, max_val=E - 1)
                            pe.wait_ge(xtT_ready, i + 1)
                            if i > 1:
                                pe.wait_ge(up_ready, i - 1)
                            mm(ps[0][:, i % 2, :], xtT[:, i % 2, :], w1f[:, bass.ds(e * (FC * 128), FC * 128)],
                               start=True, stop=True).then_inc(up_full, 1)
                        if i > 0:
                            j = i - 1
                            e = pe.value_load(e_now[0:1, j:j + 1], min_val=0, max_val=E - 1)
                            pe.wait_ge(up_ready, j + 1)
                            if j > 1:
                                pe.wait_ge(upT_ready, j - 1)
                            for c in range(FC):
                                last = tr(ps[1][:, j % 2, ROWS * c:ROWS * c + ROWS], up_b[:, j % 2, 128 * c:128 * c + 128], ident[:])
                            last.then_inc(upT_full, 1)
                            pe.wait_ge(upT_ready, j + 1)
                            if j > 1:
                                pe.wait_ge(y_read, j - 1)
                            for c in range(FC):
                                last = mm(ps[3][:, j % 2, 0:D], upT[:, j % 2, ROWS * c:ROWS * c + ROWS],
                                          w2f[:, bass.ds(e * (FC * D) + c * D, D)], start=c == 0, stop=c == FC - 1)
                            last.then_inc(y_full, 1)

                @block.scalar
                def _(act):
                    A = nc.scalar.activation
                    for i in range(PER_PASS + 1):
                        if i < PER_PASS:
                            act.wait_ge(xt_full, i + 1)
                            if i > 1:
                                act.wait_ge(up_full, i - 1)
                            A(xtT[:, i % 2, :], ps[2][:, i % 2, 0:ROWS], ACT.Copy).then_inc(xtT_ready, 1)
                        if i > 0:
                            j = i - 1
                            act.wait_ge(upT_full, j + 1)
                            if j > 1:
                                act.wait_ge(y_full, j - 1)
                            A(upT[:, j % 2, :], ps[1][:, j % 2, :], ACT.Relu).then_inc(upT_ready, 1)

                @block.vector
                def _(dve):
                    V = nc.vector
                    V.tensor_copy(e_now[:], e_tab[0:1, bass.ds(q * PER_PASS, PER_PASS)]).then_inc(now_ready, 1)
                    V.tensor_copy(t_now[:], t_tab[0:1, bass.ds(q * PER_PASS, PER_PASS)]).then_inc(now_ready, 1)
                    V.tensor_copy(mask_now[:], mask[:, bass.ds(q * PER_PASS, PER_PASS)]).then_inc(now_ready, 1)
                    dve.wait_ge(now_ready, 3)
                    c1f, c2f = c1_s.rearrange("p e f -> p (e f)"), c2_s.rearrange("p e d -> p (e d)")
                    yf = y_sum.rearrange("p t d -> p (t d)")
                    for i in range(PER_PASS + 1):
                        if i < PER_PASS:
                            e = dve.value_load(e_now[0:1, i:i + 1], min_val=0, max_val=E - 1)
                            dve.wait_ge(up_full, i + 1)
                            if i > 1:
                                dve.wait_ge(upT_full, i - 1)
                            V.tensor_tensor(up_b[:, i % 2, :], ps[0][:, i % 2, :], c1f[:, bass.ds(e * (FC * 128), FC * 128)],
                                            ALU.add).then_inc(up_ready, 1)
                        if i > 0:
                            j = i - 1
                            e = dve.value_load(e_now[0:1, j:j + 1], min_val=0, max_val=E - 1)
                            t = dve.value_load(t_now[0:1, j:j + 1], min_val=0, max_val=SORTED - 1)
                            dve.wait_ge(y_full, j + 1)
                            if j > 1:
                                dve.wait_ge(y_added, j - 1)
                            V.tensor_tensor(y_row[:, j % 2, :], ps[3][:, j % 2, 0:D], c2f[:, bass.ds(e * D, D)], ALU.add).then_inc(y_read, 1)
                            dve.wait_ge(y_read, j + 1)
                            if j > 0:
                                dve.wait_ge(y_added, j)
                            V.scalar_tensor_tensor(yf[:, bass.ds(t * D, D)], y_row[:, j % 2, :], mask_now[:, j:j + 1],
                                                   yf[:, bass.ds(t * D, D)], ALU.mult, ALU.add).then_inc(y_added, 1)
                    dve.wait_ge(y_added, PER_PASS)

            nc.all_engine_barrier(sems_to_clear=pass_sems)
        with nc.Block() as finish:
            @finish.sync
            def _(sp):
                sp.dma_start(rows_out[0:whole * ROWS, :].rearrange("(t p) d -> p t d", p=ROWS), y_sum[:, 0:whole, :]).then_inc(out_stored, 16)
                if rest:
                    sp.dma_start(rows_out[whole * ROWS:B * N, :], y_sum[0:rest, whole, :]).then_inc(out_stored, 16)
                sp.wait_ge(out_stored, 32 if rest else 16)


_INS = ["x", "txt", "L0_tok_vc_dict", "L0_tok_W1", "L0_tok_b1", "L0_tok_W2", "L0_tok_b2", "L0_attn_w_qkv",
        "L0_attn_w_out", "L0_ffn_Wr", "L0_ffn_br", "L0_ffn_W1", "L0_ffn_b1", "L0_ffn_W2", "L0_ffn_b2", "L1_attn_Wx",
        "L1_attn_Wt", "L1_attn_bt", "L1_attn_Wa", "L1_attn_ba", "L1_ffn_Wg", "L1_ffn_bg", "L1_ffn_W1", "L1_ffn_b1",
        "L1_ffn_W2", "L1_ffn_b2"]


def kernel(**inputs):
    import concourse.bacc as bacc
    from concourse.bass_utils import run_bass_kernel_spmd

    nc = bacc.Bacc("TRN2", target_bir_lowering=False, num_devices=1)
    arrays, args = {}, []
    for name in _INS:
        a = np.ascontiguousarray(inputs[name])
        arrays[f"in_{name}"] = a
        args.append(nc.dram_tensor(f"in_{name}", a.shape, mybir.dt.from_np(a.dtype), kind="ExternalInput").ap())
    batches = inputs["x"].shape[0]
    out = nc.dram_tensor("out", (batches, N, D), F32, kind="ExternalOutput").ap()
    x_rows = nc.dram_tensor("x_rows", (batches, TW, NT * D), F32, kind="Internal").ap()
    tiles = (batches * N + ROWS - 1) // ROWS
    x_sorted = nc.dram_tensor("x_sorted", (tiles * ROWS, D), F32, kind="Internal").ap()
    fusion_kernel(nc, *args, out, x_rows, x_sorted, B=batches)
    r = run_bass_kernel_spmd(nc, [arrays], core_ids=[0])
    return r.results[0]["out"]
```

```python
from contextlib import ExitStack
from math import sqrt

import numpy as np

import concourse.bass as bass
from concourse import mybir

F32 = mybir.dt.float32
U32 = mybir.dt.uint32
I32 = mybir.dt.int32
ALU = mybir.AluOpType
ACT = mybir.ActivationFunctionType
AX_X = mybir.AxisListType.X

D = 128
RES, K, STRIDE = 64, 4, 3
SIDE = (RES - K) // STRIDE + 1
IMG = SIDE * SIDE
TXT = 77
N = IMG + TXT
HALF = N // 2
NT, TW = 5, 104
T = NT * TW
TH = T // 2
IMG_LAST = IMG - 4 * TW
LAST = N - 4 * TW
VC = 100
SW = 111
HEADS, DH = 8, 64
PAIRS = HEADS // 2
STEPS = 3
MORE_STEPS = 12
SETTLED = 1e-3
E, FC = 8, 4
HC = 3
U = 64
GROUPS, M = 5, 13
QUADS = GROUPS * M
SHARE = 2
ROWS = 128
XT_RING = 3
RING, AV, LOGITS = (0, 1), 2, 3
TH_RING = 3
EPS = 1e-5


TANH_AFTER = {"score": 16, "pick": 16, "sims": 16, "mlp": 6, "norm0": 4, "qk": 4, "means": 8, "scores": 1,
              "step": 2, "check": 6, "rows": 14, "weigh": 0.75, "o": 6, "norm1": 8, "gate": 16, "up": 4.75,
              "y": 2.25}


def front_stages():
    out = [("sims",), ("mlp",), ("norm", 0), ("turn_x", 0)] + [("qk", 0), ("means",)] + [("qk", p) for p in range(1, PAIRS)]
    for hp in range(PAIRS):
        out += [("scores", hp, hh, t) for hh in range(2) for t in range(NT)]
        out += [("step", hp, k, hh) for k in range(1, STEPS) for hh in range(2)]
    out += [("check",), ("more",), ("rows",)] + [("weigh", n) for n in range(HEADS * NT + 2)]
    out += [("o",), ("norm", 1), ("box",), ("turn_x", 1), ("gate", 0), ("up", 0), ("route", 0)]
    for e in range(E):
        out += ([("up", e + 1)] if e + 1 < E else []) + [("y", e)]
        out += {E // 2 - 1: [("score",)], E // 2: [("pick",)]}.get(e, [])
    return out


def back_stages():
    out = [("take",), ("norm", 2), ("turn_x", 2), ("k2q2",)]
    for n in range(QUADS + 1):
        out += [("tanh", n, g) for g in range(4)] if n < QUADS else []
        out += [("quad", n - 1)] if n > 0 else []
        if n > 0 and n % M == 0:
            out += [("exp", n // M - 1)]
        if n % M == 2 and n > M:
            out += [("turn", n // M - 1)]
    return out + [("turn", GROUPS - 1), ("v1",), ("norm", 3), ("turn_x", 3), ("gate", 1), ("route", 1)]


def schedule(front, back):
    if not back:
        return front_stages()
    if not front:
        return back_stages()
    rest = back_stages()
    out = [rest.pop(0) for _ in range(4)]
    steps = 0
    for stage in front_stages():
        out.append(stage)
        kind = f"norm{stage[1]}" if stage[0] == "norm" else stage[0]
        steps += TANH_AFTER.get(kind, 0)
        while rest and (rest[0][0] != "tanh" or steps >= 1):
            out.append(rest.pop(0))
            steps -= out[-1][0] == "tanh"
            if out[-1][0] in ("v1", "norm", "turn_x", "gate"):
                break
    return out + rest


def psum_plan(stages):
    pair, nth, count, signalled, turn, wide_turn = {}, {}, [0] * 4, [0] * 4, 0, 0
    for stage in stages:
        kind, arg = stage[0], stage[1:]
        keys = {
            "score": ["score"], "pick": ["ohT", "vsel"], "sims": ["simmax"],
            "mlp": [("h1", c) for c in range(HC)] + ["tok"], "turn_x": [("xnT",) + arg], "qk": [("q",) + arg, ("k",) + arg],
            "scores": [("s", 2 * arg[0] + arg[1], arg[2])] if kind == "scores" else [],
            "means": ["uq", "means"], "check": ["residue"], "rows": ["ntT"] + [("v", t) for t in range(NT)],
            "weigh": ([("av", arg[0] // (2 * NT))] if arg and arg[0] % (2 * NT) == 0 and arg[0] < HEADS * NT else [])
            + ([("st",) + arg] if arg and arg[0] < HEADS * NT else []),
            "o": ["o"], "gate": [("lg",) + arg], "route": ["cwT", "b2"] if arg == (0,) else [],
            "up": [("hid",) + arg + (c,) for c in range(FC)], "y": [("y",) + arg],
            "k2q2": ["k2", "q2"], "quad": [("logits", arg[0] // M)] if arg and arg[0] % M == 0 else [],
            "turn": [("turned",) + arg], "v1": ["v1"],
        }.get(kind, [])
        for key in keys:
            name = key[0] if isinstance(key, tuple) else key
            if name in ("av", "y", "tok", "simmax"):
                p = AV
            elif name == "logits":
                p = LOGITS
            elif name in ("s", "q", "k"):
                p, wide_turn = (*RING, AV)[wide_turn], (wide_turn + 1) % 3
            else:
                p, turn = RING[turn], (turn + 1) % len(RING)
            pair[key], nth[key] = p, (count[p], signalled[p])
            count[p] += 1
            signalled[p] += name not in ("av", "logits")
    return pair, nth



def fusion_kernel(nc, x, txt, vc, tW1, tb1, tW2, tb2, w_qkv, w_out, Wr, br, W1, b1, W2, b2,
                  Wx, Wt, bt, Wa, ba, Wg, bg, V1, c1, V2, c2, out, x_rows, x_sorted, B=16):
    ctx = ExitStack()
    SORTED = (B * N + ROWS - 1) // ROWS
    PAIRED = SORTED + E - 1
    PER_PASS = -(-PAIRED // 4)
    PASSES = -(-PAIRED // PER_PASS)
    PP = PASSES * PER_PASS

    def sb(name, shape, dt=F32):
        return ctx.enter_context(nc.sbuf_tensor(name, shape, dt))

    def sem(name):
        return ctx.enter_context(nc.semaphore(name))

    with ctx:
        vc_v = sb("vc_v", [VC, D])
        vcT = sb("vcT", [D, VC])
        w1a = sb("w1a", [D, HC * 128])
        w1b = sb("w1b", [128, HC * 128])
        tb1_s = sb("tb1_s", [128, HC])
        tw2_s = sb("tw2_s", [128, HC, D])
        tb2_s = sb("tb2_s", [1, D])
        wqkv = sb("wqkv", [D, 3 * HEADS * DH])
        wout = sb("wout", [128, PAIRS, D])
        wr = [sb(f"wr{f}", [D, E]) for f in range(2)]
        br_s = [sb(f"br{f}", [1, E]) for f in range(2)]
        w1 = sb("w1", [D, E, FC * 128])
        b1_s = sb("b1_s", [128, E, FC])
        w2 = sb("w2", [128, E, FC, D])
        b2_s = sb("b2_s", [E, D])
        wxx = sb("wxx", [D, 2 * U])
        wt = sb("wt", [D, U])
        bt2 = sb("bt2", [128, 1])
        wa2 = sb("wa2", [128, 1])
        ba_s = sb("ba_s", [128, 1])
        ident = sb("ident", [128, 128])
        ones = sb("ones", [128, 128])
        before = sb("before", [TW, TW])
        valid = sb("valid", [TW, NT])
        sel = sb("sel", [128, K, 32])
        wasel = sb("wasel", [128, M, 32])
        iota_v = sb("iota_v", [SW, VC])
        iota_e = sb("iota_e", [TW, E])
        neg_half = sb("neg_half", [TW, NT])
        xb = sb("xb", [D, RES * RES])
        h = [sb(f"h{i}", [TW, NT, D]) for i in range(2)]
        xn = [sb(f"xn{i}", [TW, NT, D + 1]) for i in range(2)]
        xnT = [sb(f"xnT{i}", [D, T]) for i in range(2)]
        stats = [sb(f"stats{i}", [TW, NT, 6]) for i in range(2)]
        mv = [sb(f"mv{i}", [TW, NT, 2]) for i in range(2)]
        vare = [sb(f"vare{i}", [TW, NT]) for i in range(2)]
        rstd = [sb(f"rstd{i}", [TW, NT]) for i in range(2)]
        lg = [sb(f"lg{i}", [TW, NT, E]) for i in range(2)]
        mx8 = [sb(f"mx8{i}", [TW, NT, 8]) for i in range(2)]
        idx8 = [sb(f"idx8{i}", [TW, NT, 8], U32) for i in range(2)]
        idxf = [sb(f"idxf{i}", [TW, NT, 2]) for i in range(2)]
        pr = [sb(f"pr{i}", [TW, NT, E]) for i in range(2)]
        den = [sb(f"den{i}", [TW, NT]) for i in range(2)]
        ntau = sb("ntau", [TW, HEADS, NT])
        ntT = sb("ntT", [HEADS * NT, TW])
        rise = sb("rise", [TW, HEADS, NT])
        wkq = sb("wkq", [D, HEADS, D])
        xsum = sb("xsum", [D, 1])
        uq = sb("uq", [D, HEADS])
        zmax = sb("zmax", [TW, NT])
        s1 = sb("s1", [TW, HEADS, NT])
        s2 = sb("s2", [TW, HEADS, NT])
        sa = sb("sa", [TW, NT])
        sc = sb("sc", [TW, NT])
        res = sb("res", [TW, HEADS * NT])
        worst = sb("worst", [TW, 1])
        flag_f = sb("flag_f", [1, 1])
        unsettled = sb("unsettled", [1, 1], I32)
        oh2 = sb("oh2", [TW, NT, E])
        cw = sb("cw", [TW, NT, E])
        cwT = sb("cwT", [E, T])
        K2 = sb("K2", [128, T])
        Q2 = sb("Q2", [128, TH])
        ex = sb("ex", [128, 2, T])
        OH = sb("OH", [TW, B * NT, E])
        tidx8 = sb("tidx8", [SW, 4, 8], U32)
        tidxf = sb("tidxf", [SW, 4])
        tmx8 = sb("tmx8", [SW, 4, 8])
        QK = 7770
        BACK = QK + 2 * HEADS * T
        WORDS = BACK + 4 * N * TH_RING + NT * T
        arena = sb("arena", [128, WORDS])

        def cut(at, parts, *dims):
            n = int(np.prod(dims))
            assert at + n <= WORDS
            ap = arena[0:parts, at:at + n]
            if len(dims) == 2:
                return ap.rearrange("p (a c) -> p a c", a=dims[0])
            if len(dims) == 3:
                return ap.rearrange("p (a c d) -> p a c d", a=dims[0], c=dims[1])
            return ap

        rs_a, rs_b = cut(QK, 128, RES, SIDE), cut(QK + 1344, 128, RES, SIDE)
        box = cut(QK + 2688, 128, 4 * SW)
        prod = cut(0, 128, 2, K * IMG)
        vT, simT = cut(QK + 3132, 128, IMG), cut(3528, 128, IMG)
        ohT, oh = cut(QK + 3573, VC, 4 * SW), cut(QK, SW, 4, VC)
        h1T = cut(5254, 128, HC, IMG)
        qa = cut(QK, DH + 1, HEADS, T)
        ka = cut(QK + HEADS * T, DH + 1, HEADS, T)
        Z, R = cut(0, TW, 2 * NT, N), cut(5180, TW, NT, N)
        oT, v = cut(0, 128, PAIRS, T), cut(2100, TW, NT, HEADS * DH)
        wT = cut(0, 128, 2, 4 * D)
        hid = cut(0, 128, 2, FC * T)
        th, ET = cut(BACK, 128, TH_RING, 4 * N), cut(BACK + 4 * N * TH_RING, TW, NT, T)
        c1_s, c2_s = cut(0, ROWS, E, FC * 128), cut(E * FC * 128, ROWS, E, D)
        at = E * (FC + 1) * 128
        y_sum = cut(at, ROWS, SORTED, D)
        xall = cut(at + SORTED * D, TW, B, NT * D)
        inc = xb[:, 0:2 * B * NT * E].rearrange("p (a c) -> p a c", a=2)
        xt = xb[:, 0:XT_RING * D].rearrange("p (a c) -> p a c", a=XT_RING)
        xtT, y_row = [xb[:, (XT_RING + i) * D:(XT_RING + i + 2) * D].rearrange("p (a c) -> p a c", a=2) for i in (0, 2)]
        up_b, upT = [xb[:, (XT_RING + 4 + i) * D:(XT_RING + 4 + i + 2 * FC) * D].rearrange("p (a c) -> p a c", a=2)
                     for i in (0, 2 * FC)]
        pos = sb("pos", [TW, B * NT])
        pos_u = sb("pos_u", [TW, B * NT], U32)
        total = sb("total", [128, E])
        first_row = sb("first_row", [128, E])
        end_row = sb("end_row", [128, E])
        first_tile = sb("first_tile", [128, E])
        end_tile = sb("end_tile", [128, E])
        pair_end = sb("pair_end", [128, E])
        shift = sb("shift", [128, E])
        tile_no = sb("tile_no", [128, SORTED])
        over = cut(at + SORTED * D + B * NT * D, 128, E, SORTED)
        pair_no = sb("pair_no", [128, PP])
        row_no = sb("row_no", [128, 1])
        gt = sb("gt", [128, E, PP])
        own = sb("own", [128, E, PP])
        part = cut(at + SORTED * D + B * NT * D + E * SORTED, 128, E, PP)
        pair_e = sb("pair_e", [128, PP])
        pair_t = sb("pair_t", [128, PP])
        pair_lo = sb("pair_lo", [128, PP])
        pair_hi = sb("pair_hi", [128, PP])
        mask = sb("mask", [128, PP])
        e_tab = sb("e_tab", [128, PP], I32)
        t_tab = sb("t_tab", [128, PP], I32)
        e_now = sb("e_now", [1, PER_PASS], I32)
        t_now = sb("t_now", [1, PER_PASS], I32)
        mask_now = sb("mask_now", [128, PER_PASS])

        ps = [ctx.enter_context(nc.psum_tensor(f"ps{i}", [128, 2, 512], F32)) for i in range(4)]
        full = [sem(f"psum_full{s}") for s in range(4)]
        read = [sem(f"psum_read{s}") for s in range(4)]
        x_in, txt_in, thr_in, out_written = sem("x_in"), sem("txt_in"), sem("thr_in"), sem("out_written")
        pad_zero, box_step, ones_row = sem("pad_zero"), sem("box_step"), sem("ones_row")
        oh_ready, h1_ready = sem("oh_ready"), sem("h1_ready")
        prod_ready, prod_used = sem("prod_ready"), sem("prod_used")
        var_ready = [sem(f"var_ready{i}") for i in range(4)]
        rstd_ready = [sem(f"rstd_ready{i}") for i in range(4)]
        xn_ready = [sem(f"xn_ready{i}") for i in range(4)]
        rise_ready, relu_ready, square_ready = sem("rise_ready"), sem("relu_ready"), sem("square_ready")
        ntau_ready, xsum_ready = sem("ntau_ready"), sem("xsum_ready")
        worst_ready, flag_ready = sem("worst_ready"), sem("flag_ready")
        more_full, more_z, more_ntau = sem("more_full"), sem("more_z"), sem("more_ntau")
        more_relu, more_square, more_link = sem("more_relu"), sem("more_square"), sem("more_link")
        pt_ready, pt_used = sem("pt_ready"), sem("pt_used")
        lg_ready = [sem(f"lg_ready{f}") for f in range(2)]
        exp_ready = [sem(f"exp_ready{f}") for f in range(2)]
        cw_ready, h_taken, xs_ready = sem("cw_ready"), sem("h_taken"), sem("xs_ready")
        th_ready, th_used = sem("th_ready"), sem("th_used")
        dve_link = sem("dve_link")
        batch_sems = range(full[0].num, dve_link.num + 1)
        now_ready = sem("now_ready")
        xt_in = [sem(f"xt_in{i}") for i in range(XT_RING)]
        xt_full, xtT_ready = sem("xt_full"), sem("xtT_ready")
        up_full, up_ready, upT_full, upT_ready = sem("up_full"), sem("up_ready"), sem("upT_full"), sem("upT_ready")
        y_full, y_read, y_added = sem("y_full"), sem("y_read"), sem("y_added")
        pass_sems = range(now_ready.num, y_added.num + 1)
        loaded, setup_done, zeroed, x0_in = sem("loaded"), sem("setup_done"), sem("zeroed"), sem("x0_in")
        vcT_full, tables_ready, box0_step = sem("vcT_full"), sem("tables_ready"), sem("box0_step")
        wT_full, wT_read, wkq_full = sem("wT_full"), sem("wT_read"), sem("wkq_full")
        place_full, place_step, pos_ready = sem("place_full"), sem("place_step"), sem("pos_ready")
        xall_in, last_loaded, pads_zero, iotas = sem("xall_in"), sem("last_loaded"), sem("pads_zero"), sem("iotas")
        scattered, tables_made, out_stored = sem("scattered"), sem("tables_made"), sem("out_stored")

        def box_sums(pool, step):
            g = nc.gpsimd
            xv = xb[:].rearrange("p (i j) -> p i j", i=RES)
            c = [xv[:, :, dj:dj + STRIDE * (SIDE - 1) + 1:STRIDE] for dj in range(K)]
            g.tensor_tensor(rs_a, c[0], c[1], ALU.add).then_inc(step, 1)
            g.tensor_tensor(rs_b, c[2], c[3], ALU.add).then_inc(step, 1)
            pool.wait_ge(step, 2)
            g.tensor_tensor(rs_a, rs_a, rs_b, ALU.add).then_inc(step, 1)
            pool.wait_ge(step, 3)
            r = [rs_a[:, di:di + STRIDE * (SIDE - 1) + 1:STRIDE, :] for di in range(K)]
            sums, rb = box[:, 0:IMG].rearrange("p (i j) -> p i j", i=SIDE), rs_b[:, 0:SIDE, :]
            g.memset(box[:, IMG:4 * SW], 0.0).then_inc(step, 1)
            g.tensor_tensor(sums, r[0], r[1], ALU.add).then_inc(step, 1)
            g.tensor_tensor(rb, r[2], r[3], ALU.add).then_inc(step, 1)
            pool.wait_ge(step, 6)
            g.tensor_tensor(sums, sums, rb, ALU.add).then_inc(step, 1)
            pool.wait_ge(step, 7)

        N_LOADS, SETUP = [0], [0]
        with nc.Block() as setup:
            @setup.sync
            def _(sp):
                loads = [
                    (vc_v[:], vc), (w1a[:], tW1[0:D, :]),
                    (tb1_s[:], tb1.rearrange("(c p) -> p c", p=128)),
                    (tw2_s[:], tW2.rearrange("(c p) d -> p c d", p=128)),
                    (tb2_s[:], tb2.rearrange("(o d) -> o d", o=1)),
                    (wqkv[:], w_qkv), (wout[:], w_out.rearrange("(c p) d -> p c d", p=128)),
                    (wxx[:, 0:U], Wx), (wxx[:, U:2 * U], Wx), (wt[:], Wt),
                    (bt2[0:U, :], bt.rearrange("(u o) -> u o", o=1)), (bt2[U:2 * U, :], bt.rearrange("(u o) -> u o", o=1)),
                    (wa2[0:U, :], Wa), (wa2[U:2 * U, :], Wa),
                    (ba_s[:], ba.rearrange("(o p) -> o p", o=1).broadcast_to([128, 1])),
                    (wr[0][:], Wr), (br_s[0][:], br.rearrange("(o e) -> o e", o=1)),
                    (wr[1][:], Wg), (br_s[1][:], bg.rearrange("(o e) -> o e", o=1)),
                    (w1[:], W1.rearrange("e d f -> d e f")),
                    (b1_s[:].rearrange("p e c -> p (e c)"), b1.rearrange("e (c p) -> p (e c)", p=128)),
                    (b2_s[:], b2),
                ]
                loads += [(w2[:, e], W2[e].rearrange("(c p) d -> p c d", p=128)) for e in range(E)]
                sp.dma_start(xb[:], x[0].rearrange("c i j -> c (i j)")).then_inc(x0_in, 16)
                for dst, src in loads:
                    sp.dma_start(dst, src, allow_slow_non_contiguous=True).then_inc(loaded, 16)
                sp.wait_ge(zeroed, 1)
                for dj in range(K):
                    sp.dma_start(w1b[32 * dj:32 * dj + K, :], tW1[D + dj:D + K * K:K, :]).then_inc(loaded, 16)
                N_LOADS[0] = 16 * (len(loads) + K)
                sp.wait_ge(loaded, N_LOADS[0])
                sp.wait_ge(x0_in, 16)

            @setup.gpsimd
            def _(pool):
                g = nc.gpsimd
                n = [0]

                def done(ins):
                    ins.then_inc(setup_done, 1)
                    n[0] += 1
                    return n[0]

                g.memset(w1b[:], 0.0).then_inc(zeroed, 1)
                done(g.memset(ident[:], 0.0))
                done(g.memset(sel[:], 0.0))
                done(g.memset(before[:], 1.0))
                done(g.memset(valid[:], 1.0))
                done(g.memset(ones[:], 1.0))
                done(g.memset(neg_half[:], -0.5))
                for i in range(2):
                    done(g.memset(xn[i][:, :, D:D + 1], 1.0))
                done(g.memset(ex[:], 0.0))
                done(g.memset(wasel[:], 0.0))
                done(g.iota(iota_v[:], [[1, VC]], base=0, channel_multiplier=0, allow_small_or_imprecise_dtypes=True))
                k = done(g.iota(iota_e[:], [[1, E]], base=0, channel_multiplier=0, allow_small_or_imprecise_dtypes=True))
                pool.wait_ge(setup_done, k)
                done(g.affine_select(out=ident[:], in_=ident[:], compare_op=ALU.not_equal, fill=1.0, base=0,
                                     pattern=[[-1, 128]], channel_multiplier=1))
                done(g.affine_select(out=sel[:], in_=sel[:], compare_op=ALU.not_equal, fill=1.0, base=0,
                                     pattern=[[1, K], [-1, 32]], channel_multiplier=0))
                done(g.affine_select(out=before[:], in_=before[:], compare_op=ALU.is_gt, fill=0.0, base=0,
                                     pattern=[[1, TW]], channel_multiplier=-1))
                done(g.affine_select(out=valid[:], in_=valid[:], compare_op=ALU.is_gt, fill=0.0, base=N,
                                     pattern=[[-TW, NT]], channel_multiplier=-1))
                SETUP[0] = n[0]
                pool.wait_ge(setup_done, SETUP[0])
                pool.wait_ge(x0_in, 16)
                box_sums(pool, box0_step)

            @setup.tensor
            def _(pe):
                pe.wait_ge(loaded, N_LOADS[0])
                pe.wait_ge(setup_done, SETUP[0])
                nc.tensor.transpose(ps[0][0:D, 0, 0:VC], vc_v[:], ident[0:VC, 0:VC]).then_inc(vcT_full, 1)
                for i in range(2):
                    for p in range(PAIRS):
                        last = nc.tensor.transpose(ps[1][:, i, 128 * p:128 * p + 128], wqkv[:, 512 * i + 128 * p:512 * i + 128 * p + 128], ident[:])
                last.then_inc(wT_full, 1)
                pe.wait_ge(wT_read, 1)
                for hd in range(HEADS):
                    at = DH * (hd % 2)
                    last = nc.tensor.matmul(ps[2 + hd % 2][:, 0, D * (hd // 2):D * (hd // 2) + D],
                                            wT[at:at + DH, 1, D * (hd // 2):D * (hd // 2) + D],
                                            wT[at:at + DH, 0, D * (hd // 2):D * (hd // 2) + D], start=True, stop=True,
                                            skip_group_check=True)
                last.then_inc(wkq_full, 1)

            @setup.vector
            def _(dve):
                V = nc.vector
                dve.wait_ge(loaded, N_LOADS[0])
                dve.wait_ge(setup_done, SETUP[0])
                for s in range(2):
                    flat = wasel[U * s:U * s + U].rearrange("p m j -> p (m j)")
                    V.tensor_copy(flat[:, M * s:M * s + 33 * (M - 1) + 1:33],
                                  wa2[U * s:U * s + U, :].broadcast_to([U, M])).then_inc(tables_ready, 1)
                dve.wait_ge(vcT_full, 1)
                V.tensor_copy(vcT[:], ps[0][0:D, 0, 0:VC]).then_inc(tables_ready, 1)
                dve.wait_ge(wT_full, 1)
                V.tensor_copy(wT, ps[1][:]).then_inc(wT_read, 1)
                dve.wait_ge(wkq_full, 1)
                for i in range(2):
                    V.tensor_copy(wkq[:, i:HEADS:2, :], ps[2 + i][:, 0, :].rearrange("p (h d) -> p h d", d=D)).then_inc(tables_ready, 1)
                dve.wait_ge(tables_ready, 5)

        def batch(stages, bx, by, x_next):
            pair, nth = psum_plan(stages)
            front, back = ("sims",) in stages, ("take",) in stages

            def P(key):
                return ps[pair[key]]

            def FULL(key):
                return full[pair[key]]

            def READ(key):
                return read[pair[key]]

            def wait_full(eng, key):
                eng.wait_ge(full[pair[key]], nth[key][1] + 1)

            def wait_free(eng, key):
                if nth[key][0] > 0:
                    eng.wait_ge(read[pair[key]], nth[key][0])

            def wait_read(eng, key):
                eng.wait_ge(read[pair[key]], nth[key][0] + 1)

            def run(per_stage):
                for stage in stages:
                    if stage[0] in per_stage:
                        per_stage[stage[0]](*stage[1:])

            def unit(n):
                return n // (2 * NT), n // 2 % NT, n % 2

            def halves(dst):
                return dst.rearrange("p (c n) -> p c n", c=2)

            with nc.Block() as block:
                @block.sync
                def _(sp):
                    if front:
                        sp.wait_ge(pad_zero, 1)
                        sp.dma_start(h[0][IMG_LAST:LAST, NT - 1, :],
                                     txt[bass.ds(bx, 1)].rearrange("o t d -> (o t) d")).then_inc(txt_in, 16)
                        sp.wait_ge(prod_ready, K)
                        sp.dma_start(xb[:], x[bass.ds(x_next, 1)].rearrange("o c i j -> (o c) (i j)")).then_inc(x_in, 16)
                        wait_read(sp, "ntT")
                        sp.dma_start(qa[DH:DH + 1, :, :].rearrange("o h (t i) -> o (h t) i", t=NT), ntT[:]).then_inc(thr_in, 16)
                    if back and not front:
                        sp.dma_start(w1[:], V1.rearrange("e d f -> d e f")).then_inc(last_loaded, 16)
                        for e in range(E):
                            sp.dma_start(w2[:, e], V2[e].rearrange("(c p) d -> p c d", p=128)).then_inc(last_loaded, 16)
                    if back:
                        wait_read(sp, "v1")
                        ob = out[bass.ds(by, 1)].rearrange("o t d -> (o t) d")
                        sp.dma_start(ob[0:4 * TW, :].rearrange("(t p) d -> p t d", p=TW), h[1][:, 0:4, :]).then_inc(out_written, 16)
                        sp.dma_start(ob[4 * TW:N, :], h[1][0:LAST, 4, :]).then_inc(out_written, 16)
                        sp.wait_ge(xs_ready, NT)
                        sp.dma_start(x_rows[bass.ds(by, 1)].rearrange("o p (t d) -> (o p) t d", t=NT), xn[1][:, :, 0:D]).then_inc(out_written, 16)
                        sp.wait_ge(out_written, 48)
                    if front:
                        sp.wait_ge(x_in, 16)
                    if back and not front:
                        sp.wait_ge(last_loaded, 16 * (E + 1))

                @block.gpsimd
                def _(pool):
                    g = nc.gpsimd

                    def box_next():
                        pool.wait_ge(x_in, 16)
                        wait_full(pool, ("st", HEADS * NT - 1))
                        box_sums(pool, box_step)

                    def sims():
                        g.memset(ka[DH:DH + 1, :, :], 1.0).then_inc(ones_row, 1)
                        pool.wait_ge(ones_row, 1)
                        if back:
                            pool.wait_ge(h_taken, 1)
                        g.memset(h[0][96:TW, NT - 1, :], 0.0).then_inc(pad_zero, 1)
                        pool.wait_ge(pad_zero, 1)

                    def norm(i):
                        s = i // 2
                        pool.wait_ge(var_ready[i], 1)
                        g.tensor_tensor(rstd[s][:], vare[s][:], neg_half[:], ALU.pow).then_inc(rstd_ready[i], 1)
                        pool.wait_ge(rstd_ready[i], 1)

                    run(dict(sims=sims, norm=norm, box=box_next))

                @block.tensor
                def _(pe):
                    mm, tr = nc.tensor.matmul, nc.tensor.transpose

                    def score():
                        if front:
                            pe.wait_ge(box_step, 7)
                        wait_free(pe, "score")
                        for t in range(4):
                            last = mm(P("score")[0:SW, 0, VC * t:VC * t + VC], box[:, SW * t:SW * t + SW], vcT[:], start=True, stop=True)
                        last.then_inc(FULL("score"), 1)

                    def pick():
                        pe.wait_ge(oh_ready, 1)
                        wait_free(pe, "ohT")
                        for t in range(4):
                            last = tr(P("ohT")[0:VC, 0, SW * t:SW * t + SW], oh[:, t, :], ident[0:SW, 0:SW])
                        last.then_inc(FULL("ohT"), 1)
                        wait_read(pe, "ohT")
                        wait_free(pe, "vsel")
                        mm(P("vsel")[:, 0, 0:IMG], vc_v[:], ohT[:, 0:IMG], start=True, stop=True).then_inc(FULL("vsel"), 1)

                    def sims():
                        wait_free(pe, "simmax")
                        for di in range(K):
                            pe.wait_ge(prod_ready, di + 1)
                            for dj in range(K):
                                last = mm(P("simmax")[32 * dj:32 * dj + 32, 0, 0:IMG], sel[:, di, :],
                                          prod[:, di % 2, dj * IMG:(dj + 1) * IMG], start=di == 0, stop=di == K - 1,
                                          skip_group_check=True)
                            last.then_inc(prod_used if di < K - 1 else FULL("simmax"), 1)

                    def mlp():
                        wait_read(pe, "simmax")
                        for c in range(HC):
                            key = ("h1", c)
                            wait_free(pe, key)
                            mm(P(key)[:, 0, 0:IMG], w1a[:, 128 * c:128 * c + 128], vT, start=True, stop=False)
                            mm(P(key)[:, 0, 0:IMG], w1b[:, 128 * c:128 * c + 128], simT, start=False, stop=True).then_inc(FULL(key), 1)
                        pe.wait_ge(h1_ready, 1)
                        wait_free(pe, "tok")
                        for t in range(NT):
                            w = TW if t < 4 else IMG_LAST
                            o = P("tok")[0:w, t // 4, 128 * (t % 4):128 * (t % 4) + 128]
                            for c in range(HC):
                                mm(o, h1T[:, c, TW * t:TW * t + w], tw2_s[:, c, :], start=c == 0, stop=False)
                            last = mm(o, ones[0:1, 0:w], tb2_s[:], start=False, stop=True)
                        last.then_inc(FULL("tok"), 1)

                    def turn_x(i):
                        key = ("xnT", i)
                        wait_free(pe, key)
                        for t in range(NT):
                            pe.wait_ge(xn_ready[i], t + 1)
                            last = tr(P(key)[:, t // 4, TW * (t % 4):TW * (t % 4) + TW], xn[i // 2][:, t, 0:D], ident[0:TW, 0:TW])
                        last.then_inc(FULL(key), 1)

                    def project(key, w, s):
                        wait_free(pe, key)
                        for c in range(2):
                            last = mm(P(key)[:, c, 0:TH], w, xnT[s][:, TH * c:TH * c + TH], start=True, stop=True)
                        last.then_inc(FULL(key), 1)

                    def qk(p):
                        if p == 0:
                            wait_read(pe, ("xnT", 0))
                        project(("q", p), wqkv[:, 128 * p:128 * p + 128], 0)
                        project(("k", p), wqkv[:, 512 + 128 * p:512 + 128 * p + 128], 0)

                    def raw_scores(o, hd, t):
                        for c in range(2):
                            last = mm(o[0:TW, c, 0:HALF], qa[0:DH, hd, TW * t:TW * t + TW],
                                      ka[0:DH, hd, HALF * c:HALF * c + HALF], start=True, stop=True)
                        return last

                    def scores(hp, hh, t):
                        key = ("s", 2 * hp + hh, t)
                        if hh + t == 0:
                            wait_read(pe, ("q", hp))
                            wait_read(pe, ("k", hp))
                        wait_free(pe, key)
                        raw_scores(P(key), 2 * hp + hh, t).then_inc(FULL(key), 1)

                    def means():
                        pe.wait_ge(xsum_ready, 1)
                        wait_free(pe, "uq")
                        for hd in range(HEADS):
                            last = mm(P("uq")[:, 0, hd:hd + 1], wkq[:, hd, :], xsum[:], start=True, stop=True)
                        last.then_inc(FULL("uq"), 1)
                        wait_read(pe, "uq")
                        wait_free(pe, "means")
                        for t in range(NT):
                            last = mm(P("means")[0:TW, 0, HEADS * t:HEADS * t + HEADS], xnT[0][:, TW * t:TW * t + TW], uq[:],
                                      start=True, stop=True)
                        last.then_inc(FULL("means"), 1)

                    def check():
                        pe.wait_ge(worst_ready, 1)
                        wait_free(pe, "residue")
                        tr(P("residue")[0:1, 0, 0:TW], worst[:], ident[0:TW, 0:TW]).then_inc(FULL("residue"), 1)

                    def more():
                        pe.wait_ge(flag_ready, 1)
                        go = pe.value_load(unsettled[0:1, 0:1], min_val=0, max_val=1)
                        wait_free(pe, ("av", 0))
                        with pe.If(go > 0):
                            for hd in range(HEADS):
                                for t in range(NT):
                                    n = hd * NT + t
                                    if n > 0:
                                        pe.wait_ge(more_z, n)
                                    raw_scores(ps[AV], hd, t).then_inc(more_full, 1)
                            pe.wait_ge(more_ntau, HEADS * (MORE_STEPS + 1))

                    def rows():
                        pe.wait_ge(ntau_ready, 1)
                        wait_free(pe, "ntT")
                        tr(P("ntT")[0:HEADS * NT, 0, 0:TW], ntau[:].rearrange("p h t -> p (h t)"), ident[0:TW, 0:TW]).then_inc(FULL("ntT"), 1)
                        for t in range(NT):
                            key = ("v", t)
                            wait_free(pe, key)
                            mm(P(key)[0:TW, 0, :], xnT[0][:, TW * t:TW * t + TW], wqkv[:, 1024:1536], start=True, stop=True).then_inc(FULL(key), 1)

                    def weigh(n):
                        if n == 0:
                            pe.wait_ge(thr_in, 16)
                            pe.wait_ge(ones_row, 1)
                            wait_read(pe, ("v", NT - 1))
                        if n < HEADS * NT:
                            p, jt, hh = unit(n)
                            hd, key = 2 * p + hh, ("st", n)
                            wait_free(pe, key)
                            for c in range(2):
                                last = mm(P(key)[0:TW, c, 0:HALF], ka[:, hd, TW * jt:TW * jt + TW],
                                          qa[:, hd, HALF * c:HALF * c + HALF], start=True, stop=True)
                            last.then_inc(FULL(key), 1)
                        if n >= 2:
                            p, jt, hh = unit(n - 2)
                            if jt == 0 and hh == 0:
                                wait_free(pe, ("av", p))
                            pe.wait_ge(pt_ready, n - 1)
                            hd = 2 * p + hh
                            for c in range(2):
                                last = mm(P(("av", p))[64 * hh:64 * hh + 64, c, 0:HALF], v[:, jt, DH * hd:DH * hd + DH],
                                          R[:, (n - 2) % NT, HALF * c:HALF * c + HALF], start=jt == 0, stop=jt == NT - 1,
                                          skip_group_check=True)
                            last.then_inc(pt_used, 1)

                    def o():
                        for p in range(PAIRS):
                            wait_read(pe, ("av", p))
                        wait_free(pe, "o")
                        for t in range(NT):
                            for p in range(PAIRS):
                                last = mm(P("o")[0:TW, t // 4, 128 * (t % 4):128 * (t % 4) + 128], oT[:, p, TW * t:TW * t + TW],
                                          wout[:, p, :], start=p == 0, stop=p == PAIRS - 1)
                        last.then_inc(FULL("o"), 1)

                    def gate(f):
                        key = ("lg", f)
                        wait_read(pe, ("xnT", 2 * f + 1))
                        wait_free(pe, key)
                        for t in range(NT):
                            o_ = P(key)[0:TW, 0, E * t:E * t + E]
                            mm(o_, xnT[f][:, TW * t:TW * t + TW], wr[f][:], start=True, stop=False)
                            last = mm(o_, ones[0:1, 0:TW], br_s[f][:], start=False, stop=True)
                        last.then_inc(FULL(key), 1)

                    def route(f):
                        if f == 0:
                            pe.wait_ge(cw_ready, 1)
                            wait_free(pe, "cwT")
                            for t in range(NT):
                                last = tr(P("cwT")[0:E, t // 4, TW * (t % 4):TW * (t % 4) + TW], cw[:, t, :], ident[0:TW, 0:TW])
                            last.then_inc(FULL("cwT"), 1)
                            wait_read(pe, "cwT")
                            wait_free(pe, "b2")
                            for t in range(NT):
                                last = mm(P("b2")[0:TW, t // 4, 128 * (t % 4):128 * (t % 4) + 128],
                                          cwT[:, TW * t:TW * t + TW], b2_s[:], start=True, stop=True)
                            last.then_inc(FULL("b2"), 1)

                    def up(e):
                        for c in range(FC):
                            project(("hid", e, c), w1[:, e, 128 * c:128 * c + 128], 0)

                    def y(e):
                        key = ("y", e)
                        wait_free(pe, key)
                        for c in range(FC):
                            wait_read(pe, ("hid", e, c))
                        for t in range(NT):
                            for c in range(FC):
                                last = mm(P(key)[0:TW, t // 4, 128 * (t % 4):128 * (t % 4) + 128],
                                          hid[:, e % 2, T * c + TW * t:T * c + TW * t + TW], w2[:, e, c, :],
                                          start=c == 0, stop=c == FC - 1)
                        last.then_inc(FULL(key), 1)

                    def k2q2():
                        wait_read(pe, ("xnT", 2))
                        project("k2", wxx[:], 1)
                        wait_free(pe, "q2")
                        for c in range(2):
                            last = mm(P("q2")[U * c:U * c + U, 0, 0:TH], wt[:], xnT[1][:, TH * c:TH * c + TH], start=True, stop=True,
                                      skip_group_check=True)
                        last.then_inc(FULL("q2"), 1)

                    def quad(n):
                        G, m = n // M, n % M
                        if m == 0:
                            wait_free(pe, ("logits", G))
                        pe.wait_ge(th_ready, n + 1)
                        for c in range(2):
                            for g in range(4):
                                last = mm(ps[LOGITS][32 * g:32 * g + 32, c, 0:HALF], wasel[:, m, :],
                                          th[:, n % TH_RING, N * g + HALF * c:N * g + HALF * c + HALF],
                                          start=m == 0, stop=m == M - 1, skip_group_check=True)
                        last.then_inc(th_used, 1)

                    def turn(G):
                        key = ("turned", G)
                        wait_read(pe, ("logits", G))
                        wait_free(pe, key)
                        for jt in range(NT):
                            last = tr(P(key)[0:TW, jt // 4, 128 * (jt % 4):128 * (jt % 4) + 128], ex[:, G % 2, TW * jt:TW * jt + TW], ident[:])
                        last.then_inc(FULL(key), 1)

                    def v1():
                        wait_read(pe, ("turned", GROUPS - 1))
                        wait_free(pe, "v1")
                        for t in range(NT):
                            for jt in range(NT):
                                last = mm(P("v1")[0:TW, t // 3, (D + 1) * (t % 3):(D + 1) * (t % 3) + D + 1],
                                          ET[:, jt, TW * t:TW * t + TW], xn[1][:, jt, :], start=jt == 0, stop=jt == NT - 1)
                        last.then_inc(FULL("v1"), 1)

                    run(dict(score=score, pick=pick, sims=sims, mlp=mlp, turn_x=turn_x, qk=qk, means=means, scores=scores,
                             check=check, more=more, rows=rows, weigh=weigh, o=o, gate=gate, route=route, up=up, y=y, k2q2=k2q2, quad=quad, turn=turn, v1=v1))

                @block.scalar
                def _(act):
                    A = nc.scalar.activation

                    def take():
                        A(h[1][:].rearrange("p t d -> p (t d)"), h[0][:].rearrange("p t d -> p (t d)"), ACT.Copy).then_inc(h_taken, 1)

                    def mlp():
                        wait_full(act, "tok")
                        act.wait_ge(pad_zero, 1)
                        A(h[0][:, 0:4, :].rearrange("p t d -> p (t d)"), P("tok")[0:TW, 0, :], ACT.Tanh)
                        A(h[0][0:IMG_LAST, 4, :], P("tok")[0:IMG_LAST, 1, 0:D], ACT.Tanh).then_inc(READ("tok"), 1)

                    def qk(p):
                        key = ("k", p)
                        wait_full(act, key)
                        for hh in range(2):
                            last = A(halves(ka[0:DH, 2 * p + hh, :]), P(key)[DH * hh:DH * hh + DH, :, 0:TH], ACT.Copy)
                        last.then_inc(READ(key), 1)

                    def scores(hp, hh, t):
                        hd, key = 2 * hp + hh, ("s", 2 * hp + hh, t)
                        if hd + t == 0:
                            wait_read(act, "means")
                        wait_full(act, key)
                        if hp > 0:
                            act.wait_ge(relu_ready, hp * 2 * NT * (STEPS - 1))
                        A(halves(Z[:, NT * hh + t, :]), P(key)[0:TW, :, 0:HALF], ACT.Relu, bias=ntau[:, hd, t:t + 1],
                          accum_out=s1[:, hd, t:t + 1]).then_inc(READ(key), 1)

                    def step(hp, k, hh):
                        hd = 2 * hp + hh
                        act.wait_ge(rise_ready, (hp * STEPS + k - 1) * 2 + hh + 1)
                        for t in range(NT):
                            n = ((hp * STEPS + k) * 2 + hh) * NT + t
                            act.wait_ge(square_ready, n - NT + 1)
                            A(R[:, t, :], Z[:, NT * hh + t, :], ACT.Relu, bias=rise[:, hd, t:t + 1],
                              accum_out=s1[:, hd, t:t + 1]).then_inc(relu_ready, 1)

                    def more():
                        act.wait_ge(flag_ready, 1)
                        go = act.value_load(unsettled[0:1, 0:1], min_val=0, max_val=1)
                        with act.If(go > 0):
                            act.wait_ge(relu_ready, HEADS * NT * (STEPS - 1))
                            act.wait_ge(square_ready, HEADS * NT * STEPS)
                            for hd in range(HEADS):
                                for t in range(NT):
                                    act.wait_ge(more_full, hd * NT + t + 1)
                                    if hd > 0:
                                        act.wait_ge(more_relu, hd * NT * MORE_STEPS)
                                    A(halves(Z[:, t, :]), ps[AV][0:TW, :, 0:HALF], ACT.Copy).then_inc(more_z, 1)
                                act.wait_ge(more_z, (hd + 1) * NT)
                                for k in range(MORE_STEPS):
                                    act.wait_ge(more_ntau, hd * (MORE_STEPS + 1) + k + 1)
                                    for t in range(NT):
                                        A(R[:, t, :], Z[:, t, :], ACT.Relu, bias=ntau[:, hd, t:t + 1],
                                          accum_out=s1[:, hd, t:t + 1]).then_inc(more_relu, 1)
                            act.wait_ge(more_ntau, HEADS * (MORE_STEPS + 1))

                    def rows():
                        wait_full(act, "ntT")
                        A(ntT[:], P("ntT")[0:HEADS * NT, 0, 0:TW], ACT.Copy).then_inc(READ("ntT"), 1)

                    def weigh(n):
                        if n < HEADS * NT and n % SHARE:
                            key = ("st", n)
                            wait_full(act, key)
                            if n >= NT:
                                act.wait_ge(pt_used, n - NT + 1)
                            A(halves(R[:, n % NT, :]), P(key)[0:TW, :, 0:HALF], ACT.Relu).then_inc(READ(key), 1)
                        p = (n - 2) // (2 * NT)
                        if n > 2 and n - 2 == 2 * NT * (p + 1) - 1:
                            act.wait_ge(pt_used, 2 * NT * (p + 1))
                            A(halves(oT[:, p, 0:N]), P(("av", p))[:, :, 0:HALF], ACT.Copy).then_inc(READ(("av", p)), 1)

                    def up(e):
                        for c in range(0, FC, 2):
                            key = ("hid", e, c)
                            wait_full(act, key)
                            A(halves(hid[:, e % 2, T * c:T * c + T]), P(key)[:, :, 0:TH], ACT.Relu,
                              bias=b1_s[:, e, c:c + 1]).then_inc(READ(key), 1)

                    def gate(f):
                        act.wait_ge(lg_ready[f], 1)
                        A(pr[f][:], lg[f][:], ACT.Exp).then_inc(exp_ready[f], 1)

                    def tanh(n, g):
                        G, m = n // M, n % M
                        if n + g == 0:
                            wait_read(act, "k2")
                            wait_read(act, "q2")
                        if n >= TH_RING:
                            act.wait_ge(th_used, n - TH_RING + 1)
                        i = 4 * M * G + M * g + m
                        made = A(th[:, n % TH_RING, N * g:N * g + N], K2[:, 0:N], ACT.Tanh, bias=Q2[:, i:i + 1])
                        if g == 3:
                            made.then_inc(th_ready, 1)

                    def exp(G):
                        key = ("logits", G)
                        act.wait_ge(th_used, M * (G + 1))
                        if G >= 2:
                            wait_full(act, ("turned", G - 2))
                        A(halves(ex[:, G % 2, 0:N]), ps[LOGITS][:, :, 0:HALF], ACT.Exp, bias=ba_s[:]).then_inc(READ(key), 1)

                    run(dict(take=take, mlp=mlp, qk=qk, scores=scores, step=step, more=more, rows=rows, weigh=weigh, up=up, gate=gate,
                             tanh=tanh, exp=exp))

                @block.vector
                def _(dve):
                    V = nc.vector
                    links, more_links = [0], [0]

                    def raised(ins):
                        links[0] += 1
                        ins.then_inc(dve_link, 1)

                    def link(ins):
                        raised(ins)
                        dve.wait_ge(dve_link, links[0])

                    def link_more(ins):
                        more_links[0] += 1
                        ins.then_inc(more_link, 1)
                        dve.wait_ge(more_link, more_links[0])

                    def wide(ap):
                        return ap.unsqueeze(2).broadcast_to([TW, NT, E])

                    def score():
                        wait_full(dve, "score")
                        for t in range(4):
                            last = V.max(tmx8[:, t, :], P("score")[0:SW, 0, VC * t:VC * t + VC])
                        link(last)
                        for t in range(4):
                            last = V.max_index(tidx8[:, t, :], tmx8[:, t, :], P("score")[0:SW, 0, VC * t:VC * t + VC])
                        last.then_inc(READ("score"), 1)
                        wait_read(dve, "score")
                        link(V.tensor_copy(tidxf[:], tidx8[:, :, 0]))
                        for t in range(4):
                            last = V.tensor_scalar(oh[:, t, :], iota_v[:], tidxf[:, t:t + 1], None, ALU.is_equal)
                        last.then_inc(oh_ready, 1)

                    def pick():
                        wait_full(dve, "ohT")
                        V.tensor_copy(ohT[:], P("ohT")[0:VC, 0, 0:4 * SW]).then_inc(READ("ohT"), 1)
                        wait_full(dve, "vsel")
                        V.tensor_copy(vT, P("vsel")[:, 0, 0:IMG]).then_inc(READ("vsel"), 1)

                    def sims():
                        for di in range(K):
                            if di >= 2:
                                dve.wait_ge(prod_used, di - 1)
                            whole = xb[:]
                            patch = bass.AP(whole.tensor, whole.offset + RES * di,
                                            [list(whole.ap[0]), [1, K], [STRIDE * RES, SIDE], [STRIDE, SIDE]])
                            word = bass.AP(vT.tensor, vT.offset, [list(vT.ap[0]), [0, K], [SIDE, SIDE], [1, SIDE]])
                            V.tensor_tensor(prod[:, di % 2, :].rearrange("p (k i j) -> p k i j", k=K, i=SIDE), word, patch,
                                            ALU.mult).then_inc(prod_ready, 1)
                        wait_full(dve, "simmax")
                        V.tensor_copy(simT, P("simmax")[:, 0, 0:IMG]).then_inc(READ("simmax"), 1)

                    def mlp():
                        for c in range(HC):
                            key = ("h1", c)
                            wait_full(dve, key)
                            V.tensor_scalar(h1T[:, c, :], P(key)[:, 0, 0:IMG], tb1_s[:, c:c + 1], None, ALU.add).then_inc(READ(key), 1)
                        for c in range(HC):
                            wait_read(dve, ("h1", c))
                        V.scalar_tensor_tensor(h1T[:], h1T[:], 0.2, h1T[:], ALU.mult, ALU.max).then_inc(h1_ready, 1)

                    def norm(i):
                        s = i // 2
                        if i == 0:
                            wait_read(dve, "tok")
                            dve.wait_ge(txt_in, 16)
                        if i == 2:
                            dve.wait_ge(h_taken, 1)
                        for t in range(NT):
                            last = V.bn_stats(stats[s][:, t, :], h[s][:, t, :])
                        link(last)
                        for t in range(NT):
                            last = V.bn_aggr(mv[s][:, t, :], stats[s][:, t, :])
                        link(last)
                        V.tensor_scalar(vare[s][:], mv[s][:, :, 1], EPS, None, ALU.add).then_inc(var_ready[i], 1)
                        dve.wait_ge(rstd_ready[i], 1)
                        for t in range(NT):
                            V.tensor_scalar(xn[s][:, t, 0:D], h[s][:, t, :], mv[s][:, t, 0:1], rstd[s][:, t:t + 1],
                                            ALU.subtract, ALU.mult).then_inc(xn_ready[i], 1)

                    def turn_x(i):
                        s, key = i // 2, ("xnT", i)
                        wait_full(dve, key)
                        V.tensor_copy(xnT[s][:, 0:4 * TW], P(key)[:, 0, 0:4 * TW])
                        V.tensor_copy(xnT[s][:, 4 * TW:T], P(key)[:, 1, 0:TW]).then_inc(READ(key), 1)
                        if i == 0:
                            wait_read(dve, key)
                            V.tensor_reduce(xsum[:], xnT[0][:], AX_X, ALU.add).then_inc(xsum_ready, 1)

                    def qk(p):
                        key = ("q", p)
                        wait_full(dve, key)
                        for hh in range(2):
                            last = V.tensor_scalar(halves(qa[0:DH, 2 * p + hh, :]), P(key)[DH * hh:DH * hh + DH, :, 0:TH],
                                                   DH ** -0.5 / 2, None, ALU.mult)
                        last.then_inc(READ(key), 1)

                    def means():
                        wait_full(dve, "uq")
                        V.tensor_copy(uq[:], P("uq")[:, 0, 0:HEADS]).then_inc(READ("uq"), 1)
                        wait_full(dve, "means")
                        V.tensor_scalar(ntau[:].rearrange("p h t -> p t h"),
                                        P("means")[0:TW, 0, 0:HEADS * NT].rearrange("p (t h) -> p t h", h=HEADS),
                                        -DH ** -0.5 / 2 / N, 1.0 / sqrt(N), ALU.mult, ALU.add).then_inc(READ("means"), 1)

                    def squares(src, t, hd):
                        return V.scalar_tensor_tensor(R[:, t, :], src, 1.0, src, ALU.mult, ALU.mult, accum_out=s2[:, hd, t:t + 1])

                    def newton(hd, link, dst, first):
                        link(V.tensor_scalar(sa[:], s2[:, hd, :], 3.0, 1.0, ALU.mult, ALU.add))
                        link(V.tensor_tensor(sa[:], sa[:], s1[:, hd, :], ALU.mult))
                        link(V.reciprocal(sa[:], sa[:]))
                        link(V.scalar_tensor_tensor(sc[:], s2[:, hd, :], -1.0, s2[:, hd, :], ALU.add, ALU.mult))
                        if first:
                            return V.scalar_tensor_tensor(dst, sc[:], -2.0, sa[:], ALU.mult, ALU.mult)
                        link(V.scalar_tensor_tensor(sc[:], sc[:], -2.0, sa[:], ALU.mult, ALU.mult))
                        return V.tensor_tensor(dst, dst, sc[:], ALU.add)

                    def scores(hp, hh, t):
                        hd, n = 2 * hp + hh, (hp * STEPS * 2 + hh) * NT + t
                        wait_read(dve, ("s", hd, t))
                        if n >= NT:
                            dve.wait_ge(square_ready, n - NT + 1)
                        squares(Z[:, NT * hh + t, :], t, hd).then_inc(square_ready, 1)
                        if t == NT - 1:
                            dve.wait_ge(square_ready, n + 1)
                            newton(hd, link, rise[:, hd, :], True).then_inc(rise_ready, 1)

                    def step(hp, k, hh):
                        hd = 2 * hp + hh
                        for t in range(NT):
                            n = ((hp * STEPS + k) * 2 + hh) * NT + t
                            dve.wait_ge(relu_ready, ((hp * (STEPS - 1) + k - 1) * 2 + hh) * NT + t + 1)
                            squares(R[:, t, :], t, hd).then_inc(square_ready, 1)
                        dve.wait_ge(square_ready, n + 1)
                        newton(hd, link, rise[:, hd, :], False).then_inc(rise_ready, 1)

                    def check():
                        dve.wait_ge(rise_ready, HEADS * STEPS)
                        V.tensor_tensor(ntau[:], ntau[:], rise[:], ALU.add).then_inc(ntau_ready, 1)
                        link(V.tensor_scalar(res[:], s2[:].rearrange("p h t -> p (h t)"), -1.0, None, ALU.add))
                        link(V.tensor_tensor(res[:], res[:], res[:], ALU.mult))
                        V.tensor_reduce(worst[:], res[:], AX_X, ALU.max).then_inc(worst_ready, 1)
                        wait_full(dve, "residue")
                        V.tensor_reduce(flag_f[:], P("residue")[0:1, 0, 0:TW], AX_X, ALU.max).then_inc(READ("residue"), 1)
                        wait_read(dve, "residue")
                        V.tensor_scalar(unsettled[:], flag_f[:], SETTLED ** 2, None, ALU.is_gt).then_inc(flag_ready, 1)

                    def more():
                        dve.wait_ge(flag_ready, 1)
                        dve.wait_ge(ntau_ready, 1)
                        go = dve.value_load(unsettled[0:1, 0:1], min_val=0, max_val=1)
                        with dve.If(go > 0):
                            for hd in range(HEADS):
                                dve.wait_ge(more_z, (hd + 1) * NT)
                                link_more(V.tensor_reduce(zmax[:], Z[:, 0:NT, :], AX_X, ALU.max))
                                link_more(V.tensor_scalar(zmax[:], zmax[:], -1.0, 1.0, ALU.mult, ALU.add))
                                V.tensor_tensor(ntau[:, hd, :], ntau[:, hd, :], zmax[:], ALU.min).then_inc(more_ntau, 1)
                                dve.wait_ge(more_ntau, hd * (MORE_STEPS + 1) + 1)
                                for k in range(MORE_STEPS):
                                    for t in range(NT):
                                        n = (hd * MORE_STEPS + k) * NT + t
                                        dve.wait_ge(more_relu, n + 1)
                                        squares(R[:, t, :], t, hd).then_inc(more_square, 1)
                                    dve.wait_ge(more_square, n + 1)
                                    newton(hd, link_more, ntau[:, hd, :], False).then_inc(more_ntau, 1)

                    def rows():
                        for t in range(NT):
                            key = ("v", t)
                            wait_full(dve, key)
                            V.tensor_copy(v[:, t, :], P(key)[0:TW, 0, :]).then_inc(READ(key), 1)

                    def weigh(n):
                        if n < HEADS * NT:
                            key = ("st", n)
                            if n % SHARE:
                                wait_read(dve, key)
                            else:
                                wait_full(dve, key)
                                if n >= NT:
                                    dve.wait_ge(pt_used, n - NT + 1)
                                V.tensor_scalar(halves(R[:, n % NT, :]), P(key)[0:TW, :, 0:HALF], 0.0, None, ALU.max).then_inc(READ(key), 1)
                                wait_read(dve, key)
                            V.tensor_tensor(R[:, n % NT, :], R[:, n % NT, :], R[:, n % NT, :], ALU.mult).then_inc(pt_ready, 1)

                    def add_rows(key):
                        wait_full(dve, key)
                        for c, t0, t1 in ((0, 0, 4), (1, 4, 5)):
                            d = h[0][:, t0:t1, :].rearrange("p t d -> p (t d)")
                            last = V.tensor_tensor(d, d, P(key)[0:TW, c, 0:D * (t1 - t0)], ALU.add)
                        last.then_inc(READ(key), 1)
                        wait_read(dve, key)

                    def o():
                        add_rows("o")

                    def gate(f):
                        key, L, m8 = ("lg", f), lg[f], mx8[f]
                        wait_full(dve, key)
                        V.tensor_copy(L[:].rearrange("p t e -> p (t e)"), P(key)[0:TW, 0, 0:NT * E]).then_inc(READ(key), 1)
                        wait_read(dve, key)
                        for t in range(NT):
                            last = V.max(m8[:, t, :], L[:, t, :])
                        link(last)
                        V.tensor_tensor(L[:], L[:], wide(m8[:, :, 0]), ALU.subtract).then_inc(lg_ready[f], 1)

                    def route(f):
                        m8, i8, xf, p_, dn = mx8[f], idx8[f], idxf[f], pr[f], den[f]
                        dve.wait_ge(exp_ready[f], 1)
                        link(V.tensor_reduce(dn[:], p_[:], AX_X, ALU.add))
                        link(V.reciprocal(dn[:], dn[:]))
                        link(V.tensor_tensor(p_[:], p_[:], wide(dn[:]), ALU.mult))
                        for t in range(NT):
                            last = V.max(m8[:, t, :], p_[:, t, :])
                        link(last)
                        for t in range(NT):
                            last = V.max_index(i8[:, t, :], m8[:, t, :], p_[:, t, :])
                        link(last)
                        link(V.tensor_copy(xf[:], i8[:, :, 0:2]))
                        experts_iota = iota_e[:].unsqueeze(1).broadcast_to([TW, NT, E])
                        if f == 0:
                            link(V.tensor_tensor(cw[:], experts_iota, wide(xf[:, :, 0]), ALU.is_equal))
                            link(V.tensor_tensor(oh2[:], experts_iota, wide(xf[:, :, 1]), ALU.is_equal))
                            link(V.tensor_tensor(cw[:], cw[:], oh2[:], ALU.add))
                            V.tensor_tensor(cw[:], cw[:], p_[:], ALU.mult).then_inc(cw_ready, 1)
                            wait_full(dve, "cwT")
                            V.tensor_copy(cwT[:, 0:4 * TW], P("cwT")[0:E, 0, 0:4 * TW])
                            V.tensor_copy(cwT[:, 4 * TW:T], P("cwT")[0:E, 1, 0:TW]).then_inc(READ("cwT"), 1)
                            dve.wait_ge(cw_ready, 1)
                            add_rows("b2")
                        else:
                            for t in range(NT):
                                V.tensor_scalar(xn[1][:, t, 0:D], xn[1][:, t, 0:D], m8[:, t, 0:1], None, ALU.mult).then_inc(xs_ready, 1)
                            link(V.tensor_tensor(p_[:], experts_iota, wide(xf[:, :, 0]), ALU.is_equal))
                            link(V.tensor_tensor(OH[:, bass.ds(by * NT, NT), :], p_[:], wide(valid[:]), ALU.mult))

                    def up(e):
                        for c in range(1, FC, 2):
                            key = ("hid", e, c)
                            wait_full(dve, key)
                            V.tensor_scalar(halves(hid[:, e % 2, T * c:T * c + T]), P(key)[:, :, 0:TH], b1_s[:, e, c:c + 1],
                                            0.0, ALU.add, ALU.max).then_inc(READ(key), 1)

                    def y(e):
                        key = ("y", e)
                        wait_full(dve, key)
                        if e > 0:
                            wait_read(dve, ("y", e - 1))
                        for t in range(NT):
                            last = V.scalar_tensor_tensor(h[0][:, t, :], P(key)[0:TW, t // 4, 128 * (t % 4):128 * (t % 4) + 128],
                                                          cw[:, t, e:e + 1], h[0][:, t, :], ALU.mult, ALU.add)
                        last.then_inc(READ(key), 1)

                    def k2q2():
                        wait_full(dve, "k2")
                        V.tensor_copy(halves(K2[:]), P("k2")[:, :, 0:TH]).then_inc(READ("k2"), 1)
                        wait_full(dve, "q2")
                        V.tensor_scalar(Q2[:], P("q2")[:, 0, 0:TH], bt2[:], None, ALU.add).then_inc(READ("q2"), 1)

                    def turn(G):
                        key = ("turned", G)
                        wait_full(dve, key)
                        first = 4 * M * G
                        for s in range(2):
                            V.tensor_copy(ET[:, 0:4, TH * s + first:TH * s + first + 4 * M].rearrange("p j (g m) -> p j g m", g=4),
                                          P(key)[0:TW, 0, :].rearrange("p (j g m) -> p j g m", j=4, g=4)[:, :, :, M * s:M * s + M])
                        for s in range(2):
                            last = V.tensor_copy(ET[:, 4, TH * s + first:TH * s + first + 4 * M].rearrange("p (g m) -> p g m", g=4),
                                                 P(key)[0:TW, 1, 0:128].rearrange("p (g m) -> p g m", g=4)[:, :, M * s:M * s + M])
                        last.then_inc(READ(key), 1)

                    def v1():
                        wait_full(dve, "v1")
                        sums = P("v1")[0:TW, :, 0:3 * (D + 1)].rearrange("p c (t d) -> p c t d", d=D + 1)
                        raised(V.tensor_scalar(den[1][:, 0:3], sums[:, 0, 0:3, D], 1e-7, None, ALU.add))
                        link(V.tensor_scalar(den[1][:, 3:5], sums[:, 1, 0:2, D], 1e-7, None, ALU.add))
                        link(V.reciprocal(den[1][:], den[1][:]))
                        for t in range(NT):
                            last = V.scalar_tensor_tensor(h[1][:, t, :], sums[:, t // 3, t % 3, 0:D], den[1][:, t:t + 1],
                                                          h[1][:, t, :], ALU.mult, ALU.add)
                        last.then_inc(READ("v1"), 1)
                        wait_read(dve, "v1")

                    run(dict(score=score, pick=pick, sims=sims, mlp=mlp, norm=norm, turn_x=turn_x, qk=qk, means=means, scores=scores,
                             step=step, check=check, more=more, rows=rows, weigh=weigh, o=o, gate=gate, route=route, up=up, y=y, k2q2=k2q2,
                             turn=turn, v1=v1))

            nc.all_engine_barrier(sems_to_clear=batch_sems)

        batch([("score",), ("pick",)], None, None, None)
        batch(schedule(True, False), 0, None, 1 % B)
        if B > 1:
            with nc.Fori(0, B - 1) as b:
                batch(schedule(True, True), b + 1, b, (b + 2) % B)
        batch(schedule(False, True), None, B - 1, None)

        rows_out = out.rearrange("b t d -> (b t) d")
        whole = B * N // ROWS
        rest = B * N - whole * ROWS
        with nc.Block() as place:
            @place.sync
            def _(sp):
                sp.dma_start(xall, x_rows.rearrange("b p n -> p b n")).then_inc(xall_in, 16)
                sp.dma_start(y_sum[:, 0:whole, :], rows_out[0:whole * ROWS, :].rearrange("(t p) d -> p t d", p=ROWS)).then_inc(last_loaded, 16)
                sp.dma_start(c1_s.rearrange("p e f -> p (e f)"),
                             c1.rearrange("(o e) f -> o (e f)", o=1).broadcast_to([ROWS, E * FC * 128])).then_inc(last_loaded, 16)
                sp.dma_start(c2_s.rearrange("p e d -> p (e d)"),
                             c2.rearrange("(o e) d -> o (e d)", o=1).broadcast_to([ROWS, E * D])).then_inc(last_loaded, 16)
                n = E + 4
                if rest:
                    sp.wait_ge(pads_zero, 1)
                    sp.dma_start(y_sum[0:rest, whole, :], rows_out[whole * ROWS:B * N, :]).then_inc(last_loaded, 16)
                    sp.dma_start(x_sorted[B * N:SORTED * ROWS, :], ones[0:ROWS - rest, :]).then_inc(last_loaded, 16)
                    n += 2
                sp.wait_ge(last_loaded, 16 * n)

            @place.gpsimd
            def _(pool):
                g = nc.gpsimd
                if rest:
                    g.memset(y_sum[:, whole, :], 0.0).then_inc(pads_zero, 1)
                g.iota(tile_no[:], [[ROWS, SORTED]], base=0, channel_multiplier=0, allow_small_or_imprecise_dtypes=True).then_inc(iotas, 1)
                g.iota(pair_no[:], [[1, PP]], base=0, channel_multiplier=0, allow_small_or_imprecise_dtypes=True).then_inc(iotas, 1)
                g.iota(row_no[:], [[0, 1]], base=0, channel_multiplier=1, allow_small_or_imprecise_dtypes=True).then_inc(iotas, 1)
                pool.wait_ge(xall_in, 16)
                pool.wait_ge(pos_ready, 1)
                for n in range(B * NT):
                    w = TW if n % NT < NT - 1 else LAST
                    g.indirect_dma_start(out=x_sorted, out_offset=bass.IndirectOffsetOnAxis(ap=pos_u[0:w, n:n + 1], axis=0),
                                         in_=xall[0:w, n // NT, D * (n % NT):D * (n % NT) + D], in_offset=None).then_inc(scattered, 16)
                pool.wait_ge(scattered, 16 * B * NT)

            @place.tensor
            def _(pe):
                mm = nc.tensor.matmul
                W = B * NT * E // 2
                for n, w in enumerate((before[:], ones[0:TW, :])):
                    for c in range(2):
                        last = mm(ps[n][0:TW if n == 0 else 128, c, 0:W], w, OH[:].rearrange("p t e -> p (t e)")[:, W * c:W * c + W],
                                  start=True, stop=True)
                last.then_inc(place_full, 1)

            @place.vector
            def _(dve):
                V = nc.vector
                step = [0]

                def then(ins):
                    step[0] += 1
                    ins.then_inc(place_step, 1)
                    dve.wait_ge(place_step, step[0])

                tiles = B * NT
                dve.wait_ge(place_full, 1)
                W = tiles * E // 2

                def run(ap):
                    return ap.rearrange("p (c n) -> p c n", c=2)

                then(V.tensor_copy(run(inc[:, 0, :]), ps[1][:, :, 0:W]))
                cur, d = 0, 1
                while d < tiles:
                    V.tensor_copy(inc[:, 1 - cur, 0:d * E], inc[:, cur, 0:d * E])
                    then(V.tensor_tensor(inc[:, 1 - cur, d * E:], inc[:, cur, d * E:], inc[:, cur, 0:(tiles - d) * E], ALU.add))
                    cur, d = 1 - cur, 2 * d
                then(V.tensor_copy(total[:], inc[:, cur, (tiles - 1) * E:tiles * E]))

                def sums_up_to(dst, src):
                    then(V.tensor_copy(dst[:, 0:1], src[:, 0:1]))
                    for e in range(1, E):
                        then(V.tensor_tensor(dst[:, e:e + 1], dst[:, e - 1:e], src[:, e:e + 1], ALU.add))

                sums_up_to(end_row, total)
                then(V.tensor_tensor(first_row[:], end_row[:], total[:], ALU.subtract))
                s = inc[0:TW, cur, :]
                then(V.tensor_tensor(run(s), run(s), ps[1][0:TW, :, 0:W], ALU.subtract))
                then(V.tensor_tensor(run(s), run(s), ps[0][0:TW, :, 0:W], ALU.add))
                s3 = s.rearrange("p (t e) -> p t e", e=E)
                then(V.tensor_tensor(s3, s3, first_row[0:TW, :].unsqueeze(1).broadcast_to([TW, tiles, E]), ALU.add))
                then(V.tensor_tensor(s3, s3, OH[:], ALU.mult))
                then(V.tensor_reduce(pos[:], s3, AX_X, ALU.add))
                V.tensor_copy(pos_u[:], pos[:]).then_inc(pos_ready, 1)
                dve.wait_ge(iotas, 3)

                def over_tiles(ap):
                    return ap.unsqueeze(2).broadcast_to([128, E, SORTED])

                def over_pairs(ap):
                    return ap.unsqueeze(2).broadcast_to([128, E, PP])

                starts = tile_no[:].unsqueeze(1).broadcast_to([128, E, SORTED])
                then(V.tensor_tensor(over, starts, over_tiles(end_row[:]), ALU.is_lt))
                then(V.tensor_reduce(end_tile[:], over, AX_X, ALU.add))
                then(V.tensor_tensor(over, starts, over_tiles(first_row[:]), ALU.is_le))
                then(V.tensor_reduce(first_tile[:], over, AX_X, ALU.add))
                then(V.tensor_scalar(first_tile[:], first_tile[:], -1.0, None, ALU.add))
                then(V.tensor_tensor(end_tile[:], end_tile[:], first_tile[:], ALU.subtract))
                then(V.tensor_scalar(total[:], total[:], 1.0, None, ALU.min))
                then(V.tensor_tensor(total[:], total[:], end_tile[:], ALU.mult))
                sums_up_to(pair_end, total)
                then(V.tensor_tensor(shift[:], total[:], pair_end[:], ALU.subtract))
                then(V.tensor_tensor(shift[:], shift[:], first_tile[:], ALU.add))
                numbers = pair_no[:].unsqueeze(1).broadcast_to([128, E, PP])
                then(V.tensor_tensor(gt[:], numbers, over_pairs(pair_end[:]), ALU.is_ge))
                then(V.tensor_scalar(own[:, 0, :], gt[:, 0, :], -1.0, 1.0, ALU.mult, ALU.add))
                then(V.tensor_tensor(own[:, 1:E, :], gt[:, 0:E - 1, :], gt[:, 1:E, :], ALU.subtract))

                def of_pair(dst, values):
                    then(V.tensor_tensor(part, own[:], over_pairs(values[:]), ALU.mult))
                    then(V.tensor_reduce(dst[:], part.rearrange("p e n -> p n e"), AX_X, ALU.add))

                of_pair(pair_t, shift)
                of_pair(pair_lo, first_row)
                of_pair(pair_hi, end_row)
                then(V.tensor_reduce(pair_e[:], gt[:].rearrange("p e n -> p n e"), AX_X, ALU.add))
                then(V.tensor_tensor(pair_t[:], pair_t[:], pair_no[:], ALU.add))
                then(V.tensor_scalar(pair_e[:], pair_e[:], E - 1.0, None, ALU.min))
                then(V.tensor_scalar(pair_t[:], pair_t[:], SORTED - 1.0, None, ALU.min))
                then(V.tensor_copy(e_tab[:], pair_e[:]))
                then(V.tensor_copy(t_tab[:], pair_t[:]))
                then(V.tensor_scalar(pair_t[:], pair_t[:], float(ROWS), row_no[:], ALU.mult, ALU.add))
                then(V.tensor_tensor(mask[:], pair_t[:], pair_lo[:], ALU.is_ge))
                then(V.tensor_tensor(pair_hi[:], pair_t[:], pair_hi[:], ALU.is_lt))
                V.tensor_tensor(mask[:], mask[:], pair_hi[:], ALU.mult).then_inc(tables_made, 1)
                dve.wait_ge(tables_made, 1)

        nc.all_engine_barrier()
        with nc.Fori(0, PASSES) as q:
            with nc.Block() as block:
                @block.sync
                def _(sp):
                    sp.wait_ge(now_ready, 3)
                    for i in range(PER_PASS):
                        t = sp.value_load(t_now[0:1, i:i + 1], min_val=0, max_val=SORTED - 1)
                        if i >= XT_RING:
                            sp.wait_ge(xt_full, i - XT_RING + 1)
                        sp.dma_start(xt[:, i % XT_RING, :], x_sorted[bass.ds(t * ROWS, ROWS), :]).then_inc(xt_in[i % XT_RING], 16)

                @block.tensor
                def _(pe):
                    mm, tr = nc.tensor.matmul, nc.tensor.transpose
                    pe.wait_ge(now_ready, 3)
                    w1f, w2f = w1[:].rearrange("d e f -> d (e f)"), w2[:].rearrange("p e c d -> p (e c d)")

                    def turn_rows(i):
                        pe.wait_ge(xt_in[i % XT_RING], 16 * (i // XT_RING + 1))
                        if i > 1:
                            pe.wait_ge(xtT_ready, i - 1)
                        tr(ps[2][:, i % 2, 0:ROWS], xt[:, i % XT_RING, :], ident[:]).then_inc(xt_full, 1)

                    def up(i):
                        e = pe.value_load(e_now[0:1, i:i + 1], min_val=0, max_val=E - 1)
                        pe.wait_ge(xtT_ready, i + 1)
                        if i > 1:
                            pe.wait_ge(up_ready, i - 1)
                        mm(ps[0][:, i % 2, :], xtT[:, i % 2, :], w1f[:, bass.ds(e * (FC * 128), FC * 128)],
                           start=True, stop=True).then_inc(up_full, 1)

                    def turn_up(i):
                        pe.wait_ge(up_ready, i + 1)
                        if i > 1:
                            pe.wait_ge(upT_ready, i - 1)
                        for c in range(FC):
                            last = tr(ps[1][:, i % 2, ROWS * c:ROWS * c + ROWS], up_b[:, i % 2, 128 * c:128 * c + 128], ident[:])
                        last.then_inc(upT_full, 1)

                    def down(i):
                        e = pe.value_load(e_now[0:1, i:i + 1], min_val=0, max_val=E - 1)
                        pe.wait_ge(upT_ready, i + 1)
                        if i > 1:
                            pe.wait_ge(y_read, i - 1)
                        for c in range(FC):
                            last = mm(ps[3][:, i % 2, 0:D], upT[:, i % 2, ROWS * c:ROWS * c + ROWS],
                                      w2f[:, bass.ds(e * (FC * D) + c * D, D)], start=c == 0, stop=c == FC - 1)
                        last.then_inc(y_full, 1)

                    for i in range(PER_PASS + 3):
                        for lag, stage in enumerate((turn_rows, up, turn_up, down)):
                            if 0 <= i - lag < PER_PASS:
                                stage(i - lag)

                @block.scalar
                def _(act):
                    A = nc.scalar.activation
                    for i in range(PER_PASS + 2):
                        if i < PER_PASS:
                            act.wait_ge(xt_full, i + 1)
                            if i > 1:
                                act.wait_ge(up_full, i - 1)
                            A(xtT[:, i % 2, :], ps[2][:, i % 2, 0:ROWS], ACT.Copy).then_inc(xtT_ready, 1)
                        if i > 1:
                            j = i - 2
                            act.wait_ge(upT_full, j + 1)
                            if j > 1:
                                act.wait_ge(y_full, j - 1)
                            A(upT[:, j % 2, :], ps[1][:, j % 2, :], ACT.Relu).then_inc(upT_ready, 1)

                @block.vector
                def _(dve):
                    V = nc.vector
                    V.tensor_copy(e_now[:], e_tab[0:1, bass.ds(q * PER_PASS, PER_PASS)]).then_inc(now_ready, 1)
                    V.tensor_copy(t_now[:], t_tab[0:1, bass.ds(q * PER_PASS, PER_PASS)]).then_inc(now_ready, 1)
                    V.tensor_copy(mask_now[:], mask[:, bass.ds(q * PER_PASS, PER_PASS)]).then_inc(now_ready, 1)
                    dve.wait_ge(now_ready, 3)
                    c1f, c2f = c1_s.rearrange("p e f -> p (e f)"), c2_s.rearrange("p e d -> p (e d)")
                    yf = y_sum.rearrange("p t d -> p (t d)")
                    for i in range(PER_PASS + 2):
                        if i < PER_PASS:
                            e = dve.value_load(e_now[0:1, i:i + 1], min_val=0, max_val=E - 1)
                            dve.wait_ge(up_full, i + 1)
                            if i > 1:
                                dve.wait_ge(upT_full, i - 1)
                            V.tensor_tensor(up_b[:, i % 2, :], ps[0][:, i % 2, :], c1f[:, bass.ds(e * (FC * 128), FC * 128)],
                                            ALU.add).then_inc(up_ready, 1)
                        if i > 1:
                            j = i - 2
                            e = dve.value_load(e_now[0:1, j:j + 1], min_val=0, max_val=E - 1)
                            t = dve.value_load(t_now[0:1, j:j + 1], min_val=0, max_val=SORTED - 1)
                            dve.wait_ge(y_full, j + 1)
                            if j > 1:
                                dve.wait_ge(y_added, j - 1)
                            V.tensor_tensor(y_row[:, j % 2, :], ps[3][:, j % 2, 0:D], c2f[:, bass.ds(e * D, D)], ALU.add).then_inc(y_read, 1)
                            dve.wait_ge(y_read, j + 1)
                            if j > 0:
                                dve.wait_ge(y_added, j)
                            V.scalar_tensor_tensor(yf[:, bass.ds(t * D, D)], y_row[:, j % 2, :], mask_now[:, j:j + 1],
                                                   yf[:, bass.ds(t * D, D)], ALU.mult, ALU.add).then_inc(y_added, 1)
                    dve.wait_ge(y_added, PER_PASS)

            nc.all_engine_barrier(sems_to_clear=pass_sems)
        with nc.Block() as finish:
            @finish.sync
            def _(sp):
                sp.dma_start(rows_out[0:whole * ROWS, :].rearrange("(t p) d -> p t d", p=ROWS), y_sum[:, 0:whole, :]).then_inc(out_stored, 16)
                if rest:
                    sp.dma_start(rows_out[whole * ROWS:B * N, :], y_sum[0:rest, whole, :]).then_inc(out_stored, 16)
                sp.wait_ge(out_stored, 32 if rest else 16)


_INS = ["x", "txt", "L0_tok_vc_dict", "L0_tok_W1", "L0_tok_b1", "L0_tok_W2", "L0_tok_b2", "L0_attn_w_qkv",
        "L0_attn_w_out", "L0_ffn_Wr", "L0_ffn_br", "L0_ffn_W1", "L0_ffn_b1", "L0_ffn_W2", "L0_ffn_b2", "L1_attn_Wx",
        "L1_attn_Wt", "L1_attn_bt", "L1_attn_Wa", "L1_attn_ba", "L1_ffn_Wg", "L1_ffn_bg", "L1_ffn_W1", "L1_ffn_b1",
        "L1_ffn_W2", "L1_ffn_b2"]


def kernel(**inputs):
    import concourse.bacc as bacc
    from concourse.bass_utils import run_bass_kernel_spmd

    nc = bacc.Bacc("TRN2", target_bir_lowering=False, num_devices=1)
    arrays, args = {}, []
    for name in _INS:
        a = np.ascontiguousarray(inputs[name])
        arrays[f"in_{name}"] = a
        args.append(nc.dram_tensor(f"in_{name}", a.shape, mybir.dt.from_np(a.dtype), kind="ExternalInput").ap())
    batches = inputs["x"].shape[0]
    out = nc.dram_tensor("out", (batches, N, D), F32, kind="ExternalOutput").ap()
    x_rows = nc.dram_tensor("x_rows", (batches, TW, NT * D), F32, kind="Internal").ap()
    tiles = (batches * N + ROWS - 1) // ROWS
    x_sorted = nc.dram_tensor("x_sorted", (tiles * ROWS, D), F32, kind="Internal").ap()
    fusion_kernel(nc, *args, out, x_rows, x_sorted, B=batches)
    r = run_bass_kernel_spmd(nc, [arrays], core_ids=[0])
    return r.results[0]["out"]
```
